# Optimizing a Trainium2 kernel written in Bass

```python
import numpy as np
import jax
import jax.numpy as jnp

def _softmax(x, axis=-1):
    return jax.nn.softmax(x, axis=axis)

def _gelu(x):
    return jax.nn.gelu(x, approximate=True)

def _silu(x):
    return jax.nn.silu(x)

def _sigmoid(x):
    return jax.nn.sigmoid(x)

def _layernorm(x, axis=-1, eps=1e-05):
    m = jnp.mean(x, axis=axis, keepdims=True)
    v = jnp.var(x, axis=axis, keepdims=True)
    return (x - m) / jnp.sqrt(v + eps)

def _scatter_add(tgt, idx, src, axis=0):
    return tgt.at[idx].add(src)

def _segment_sum(src, seg, n):
    return jax.ops.segment_sum(src, seg, n)
kernel_name = 'mk_adaln_d1_jaxref_r4_0fc955'

def setup_inputs(seed: int=0):
    np.random.seed(seed)
    _w = jnp.asarray

    def _L0_attn_setup():
        import jax, jax.numpy as jnp
        import numpy as np
        D_MODEL = 256
        D_STATE = 16
        D_CONV = 4
        EXPAND = 2
        D_INNER = EXPAND * D_MODEL
        DT_RANK = D_MODEL // 16
        BATCH = 4
        SEQLEN = 512

        def _mamba_params(key):
            ks = jax.random.split(key, 6)
            s = 0.02
            return dict(W_in=jax.random.normal(ks[0], (2 * D_INNER, D_MODEL)) * s, W_conv=jax.random.normal(ks[1], (D_INNER, D_CONV)) * s, b_conv=jnp.zeros((D_INNER,), jnp.float32), W_x=jax.random.normal(ks[2], (DT_RANK + 2 * D_STATE, D_INNER)) * s, W_dt=jax.random.normal(ks[3], (D_INNER, DT_RANK)) * s, b_dt=jax.random.normal(ks[4], (D_INNER,)) * 0.1, A_log=jnp.log(jnp.tile(jnp.arange(1, D_STATE + 1, dtype=jnp.float32), (D_INNER, 1))), D=jnp.ones((D_INNER,), jnp.float32), W_out=jax.random.normal(ks[5], (D_MODEL, D_INNER)) * s)

        def _layernorm(x, w, b, eps=1e-05):
            mu = jnp.mean(x, axis=-1, keepdims=True)
            var = jnp.mean(jnp.square(x - mu), axis=-1, keepdims=True)
            return (x - mu) * jax.lax.rsqrt(var + eps) * w + b

        def _mamba(x, W_in, W_conv, b_conv, W_x, W_dt, b_dt, A_log, Dp, W_out):
            Bb = x.shape[0]
            xz = x @ W_in.T
            xp, z = jnp.split(xz, 2, axis=-1)
            xc = jax.lax.conv_general_dilated(xp.transpose(0, 2, 1), W_conv[:, None, :], window_strides=(1,), padding=[(D_CONV - 1, 0)], dimension_numbers=('NCH', 'OIH', 'NCH'), feature_group_count=D_INNER)
            xc = jax.nn.silu(xc.transpose(0, 2, 1) + b_conv)
            x_dbl = xc @ W_x.T
            dt, Bm, Cm = jnp.split(x_dbl, [DT_RANK, DT_RANK + D_STATE], axis=-1)
            dt = jax.nn.softplus(dt @ W_dt.T + b_dt)
            A = -jnp.exp(A_log)

            def step(h, inp):
                dt_t, u_t, B_t, C_t = inp
                h = h * jnp.exp(dt_t[:, :, None] * A) + (dt_t * u_t)[:, :, None] * B_t[:, None, :]
                y = jnp.einsum('bdn,bn->bd', h, C_t)
                return (h, y)
            xs = (dt.transpose(1, 0, 2), xc.transpose(1, 0, 2), Bm.transpose(1, 0, 2), Cm.transpose(1, 0, 2))
            h0 = jnp.zeros((Bb, D_INNER, D_STATE), x.dtype)
            _, ys = jax.lax.scan(step, h0, xs)
            y = ys.transpose(1, 0, 2) + xc * Dp
            y = y * jax.nn.silu(z)
            return y @ W_out.T
        key = jax.random.key(seed)
        kx, kf, kb = jax.random.split(key, 3)
        inp = {'x': jax.random.normal(kx, (BATCH, SEQLEN, D_MODEL), jnp.float32), 'ln_w': jnp.ones((D_MODEL,), jnp.float32), 'ln_b': jnp.zeros((D_MODEL,), jnp.float32)}
        for pref, k in (('f_', kf), ('b_', kb)):
            p = _mamba_params(k)
            for name, v in p.items():
                inp[pref + name] = v
        return inp
    _L0_attn_in = _L0_attn_setup()

    def _L0_ffn_setup():
        import jax, jax.numpy as jnp
        import numpy as np
        D = 256
        H = 256
        E = 8
        K = 2
        I = 2 * 256
        ROUTE_SCALE = 1.0
        key = jax.random.key(seed)
        ks = jax.random.split(key, 12)
        s = lambda *sh: 1.0 / np.sqrt(sh[-1])
        return {'x': jax.random.normal(ks[0], (1, 512, D), jnp.float32), 'gate_w': jax.random.normal(ks[1], (E, D), jnp.float32) * s(E, D), 'w1': jax.random.normal(ks[2], (E, H, D), jnp.float32) * s(H, D), 'b1': jax.random.normal(ks[3], (E, H), jnp.float32) * 0.01, 'w2': jax.random.normal(ks[4], (E, D, H), jnp.float32) * s(D, H), 'b2': jax.random.normal(ks[5], (E, D), jnp.float32) * 0.01, 'w3': jax.random.normal(ks[6], (E, H, D), jnp.float32) * s(H, D), 'b3': jax.random.normal(ks[7], (E, H), jnp.float32) * 0.01, 'sw1': jax.random.normal(ks[8], (I, D), jnp.float32) * s(I, D), 'sw2': jax.random.normal(ks[9], (I, D), jnp.float32) * s(I, D), 'sw3': jax.random.normal(ks[10], (D, I), jnp.float32) * s(D, I)}
    _L0_ffn_in = _L0_ffn_setup()
    _L0_c = _w((lambda *s: np.random.randn(*s).astype(np.float32) * 0.05)(2, 256))
    _L0_wmod = _w((lambda *s: np.random.randn(*s).astype(np.float32) * 0.05)(256, 6 * 256) * 256 ** (-0.5))
    _d = {'L0_attn_x': _L0_attn_in['x'], 'L0_attn_ln_w': _L0_attn_in['ln_w'], 'L0_attn_ln_b': _L0_attn_in['ln_b'], 'L0_attn_f_W_in': _L0_attn_in['f_W_in'], 'L0_attn_f_W_conv': _L0_attn_in['f_W_conv'], 'L0_attn_f_b_conv': _L0_attn_in['f_b_conv'], 'L0_attn_f_W_x': _L0_attn_in['f_W_x'], 'L0_attn_f_W_dt': _L0_attn_in['f_W_dt'], 'L0_attn_f_b_dt': _L0_attn_in['f_b_dt'], 'L0_attn_f_A_log': _L0_attn_in['f_A_log'], 'L0_attn_f_D': _L0_attn_in['f_D'], 'L0_attn_f_W_out': _L0_attn_in['f_W_out'], 'L0_attn_b_W_in': _L0_attn_in['b_W_in'], 'L0_attn_b_W_conv': _L0_attn_in['b_W_conv'], 'L0_attn_b_b_conv': _L0_attn_in['b_b_conv'], 'L0_attn_b_W_x': _L0_attn_in['b_W_x'], 'L0_attn_b_W_dt': _L0_attn_in['b_W_dt'], 'L0_attn_b_b_dt': _L0_attn_in['b_b_dt'], 'L0_attn_b_A_log': _L0_attn_in['b_A_log'], 'L0_attn_b_D': _L0_attn_in['b_D'], 'L0_attn_b_W_out': _L0_attn_in['b_W_out'], 'L0_ffn_gate_w': _L0_ffn_in['gate_w'], 'L0_ffn_w1': _L0_ffn_in['w1'], 'L0_ffn_b1': _L0_ffn_in['b1'], 'L0_ffn_w2': _L0_ffn_in['w2'], 'L0_ffn_b2': _L0_ffn_in['b2'], 'L0_ffn_w3': _L0_ffn_in['w3'], 'L0_ffn_b3': _L0_ffn_in['b3'], 'L0_ffn_sw1': _L0_ffn_in['sw1'], 'L0_ffn_sw2': _L0_ffn_in['sw2'], 'L0_ffn_sw3': _L0_ffn_in['sw3'], 'L0_c': _L0_c, 'L0_wmod': _L0_wmod}
    _x0 = _d['L0_attn_x']
    _d['L0_attn_x'] = jax.random.normal(jax.random.fold_in(jax.random.key(seed), 1), (2, 2048, 256), dtype=_x0.dtype)
    del _x0
    return _d

def reference(L0_attn_x, L0_attn_ln_w, L0_attn_ln_b, L0_attn_f_W_in, L0_attn_f_W_conv, L0_attn_f_b_conv, L0_attn_f_W_x, L0_attn_f_W_dt, L0_attn_f_b_dt, L0_attn_f_A_log, L0_attn_f_D, L0_attn_f_W_out, L0_attn_b_W_in, L0_attn_b_W_conv, L0_attn_b_b_conv, L0_attn_b_W_x, L0_attn_b_W_dt, L0_attn_b_b_dt, L0_attn_b_A_log, L0_attn_b_D, L0_attn_b_W_out, L0_ffn_gate_w, L0_ffn_w1, L0_ffn_b1, L0_ffn_w2, L0_ffn_b2, L0_ffn_w3, L0_ffn_b3, L0_ffn_sw1, L0_ffn_sw2, L0_ffn_sw3, L0_c, L0_wmod):

    def _L0_attn_ref(x, ln_w, ln_b, f_W_in, f_W_conv, f_b_conv, f_W_x, f_W_dt, f_b_dt, f_A_log, f_D, f_W_out, b_W_in, b_W_conv, b_b_conv, b_W_x, b_W_dt, b_b_dt, b_A_log, b_D, b_W_out):
        import jax, jax.numpy as jnp
        import numpy as np
        D_MODEL = 256
        D_STATE = 16
        D_CONV = 4
        EXPAND = 2
        D_INNER = EXPAND * D_MODEL
        DT_RANK = D_MODEL // 16
        BATCH = 4
        SEQLEN = 512

        def _mamba_params(key):
            ks = jax.random.split(key, 6)
            s = 0.02
            return dict(W_in=jax.random.normal(ks[0], (2 * D_INNER, D_MODEL)) * s, W_conv=jax.random.normal(ks[1], (D_INNER, D_CONV)) * s, b_conv=jnp.zeros((D_INNER,), jnp.float32), W_x=jax.random.normal(ks[2], (DT_RANK + 2 * D_STATE, D_INNER)) * s, W_dt=jax.random.normal(ks[3], (D_INNER, DT_RANK)) * s, b_dt=jax.random.normal(ks[4], (D_INNER,)) * 0.1, A_log=jnp.log(jnp.tile(jnp.arange(1, D_STATE + 1, dtype=jnp.float32), (D_INNER, 1))), D=jnp.ones((D_INNER,), jnp.float32), W_out=jax.random.normal(ks[5], (D_MODEL, D_INNER)) * s)

        def _layernorm(x, w, b, eps=1e-05):
            mu = jnp.mean(x, axis=-1, keepdims=True)
            var = jnp.mean(jnp.square(x - mu), axis=-1, keepdims=True)
            return (x - mu) * jax.lax.rsqrt(var + eps) * w + b

        def _mamba(x, W_in, W_conv, b_conv, W_x, W_dt, b_dt, A_log, Dp, W_out):
            Bb = x.shape[0]
            xz = x @ W_in.T
            xp, z = jnp.split(xz, 2, axis=-1)
            xc = jax.lax.conv_general_dilated(xp.transpose(0, 2, 1), W_conv[:, None, :], window_strides=(1,), padding=[(D_CONV - 1, 0)], dimension_numbers=('NCH', 'OIH', 'NCH'), feature_group_count=D_INNER)
            xc = jax.nn.silu(xc.transpose(0, 2, 1) + b_conv)
            x_dbl = xc @ W_x.T
            dt, Bm, Cm = jnp.split(x_dbl, [DT_RANK, DT_RANK + D_STATE], axis=-1)
            dt = jax.nn.softplus(dt @ W_dt.T + b_dt)
            A = -jnp.exp(A_log)

            def step(h, inp):
                dt_t, u_t, B_t, C_t = inp
                h = h * jnp.exp(dt_t[:, :, None] * A) + (dt_t * u_t)[:, :, None] * B_t[:, None, :]
                y = jnp.einsum('bdn,bn->bd', h, C_t)
                return (h, y)
            xs = (dt.transpose(1, 0, 2), xc.transpose(1, 0, 2), Bm.transpose(1, 0, 2), Cm.transpose(1, 0, 2))
            h0 = jnp.zeros((Bb, D_INNER, D_STATE), x.dtype)
            _, ys = jax.lax.scan(step, h0, xs)
            y = ys.transpose(1, 0, 2) + xc * Dp
            y = y * jax.nn.silu(z)
            return y @ W_out.T
        xn = _layernorm(x, ln_w, ln_b)
        y_fwd = _mamba(xn, f_W_in, f_W_conv, f_b_conv, f_W_x, f_W_dt, f_b_dt, f_A_log, f_D, f_W_out)
        xr = jnp.flip(xn, axis=1)
        y_bwd = jnp.flip(_mamba(xr, b_W_in, b_W_conv, b_b_conv, b_W_x, b_W_dt, b_b_dt, b_A_log, b_D, b_W_out), axis=1)
        return x + 0.5 * (y_fwd + y_bwd)

    def _L0_ffn_ref(x, gate_w, w1, b1, w2, b2, w3, b3, sw1, sw2, sw3):
        import jax, jax.numpy as jnp
        import numpy as np
        D = 256
        H = 256
        E = 8
        K = 2
        I = 2 * 256
        ROUTE_SCALE = 1.0
        B, S, _ = x.shape
        xt = x.reshape(-1, D)
        logits = xt @ gate_w.T
        scores = jax.nn.softmax(logits.astype(jnp.float32), axis=-1)
        top_vals, idx = jax.lax.top_k(scores, K)
        weights = jnp.take_along_axis(scores, idx, axis=1).astype(x.dtype) * ROUTE_SCALE
        xs = xt[:, None, :] * weights[:, :, None]
        y = jnp.zeros_like(xt)
        for e in range(E):
            mask = (idx == e).astype(x.dtype)
            h = jax.nn.silu(jnp.einsum('tkd,hd->tkh', xs, w1[e]) + b1[e])
            x2 = jnp.einsum('tkh,dh->tkd', h, w2[e]) + b2[e]
            x3 = jnp.einsum('tkd,hd->tkh', xs, w3[e]) + b3[e]
            y = y + jnp.sum(x2 * x3 * mask[:, :, None], axis=1)
        z = jax.nn.silu(xt @ sw1.T) * (xt @ sw2.T) @ sw3.T
        return (y + z).reshape(B, S, D)
    x = L0_attn_x
    mod = (_silu(L0_c) @ L0_wmod).reshape(L0_c.shape[0], 6, 1, -1)
    sa, ca, ga, sb, cb, gb = (mod[:, 0], mod[:, 1], mod[:, 2], mod[:, 3], mod[:, 4], mod[:, 5])
    ga = (2 * (ga >= 0) - 1) * jnp.maximum(jnp.abs(ga), 0.25)
    gb = (2 * (gb >= 0) - 1) * jnp.maximum(jnp.abs(gb), 0.25)
    h = _layernorm(x, axis=-1) * (1 + ca) + sa
    x = x + ga * _L0_attn_ref(h, L0_attn_ln_w, L0_attn_ln_b, L0_attn_f_W_in, L0_attn_f_W_conv, L0_attn_f_b_conv, L0_attn_f_W_x, L0_attn_f_W_dt, L0_attn_f_b_dt, L0_attn_f_A_log, L0_attn_f_D, L0_attn_f_W_out, L0_attn_b_W_in, L0_attn_b_W_conv, L0_attn_b_b_conv, L0_attn_b_W_x, L0_attn_b_W_dt, L0_attn_b_b_dt, L0_attn_b_A_log, L0_attn_b_D, L0_attn_b_W_out)
    h = _layernorm(x, axis=-1) * (1 + cb) + sb
    x = x + gb * _L0_ffn_ref(h, L0_ffn_gate_w, L0_ffn_w1, L0_ffn_b1, L0_ffn_w2, L0_ffn_b2, L0_ffn_w3, L0_ffn_b3, L0_ffn_sw1, L0_ffn_sw2, L0_ffn_sw3)
    return x

_drawn_inputs = setup_inputs


def setup_inputs(seed=0):
    import zlib

    import numpy as np

    out = dict(_drawn_inputs(seed))
    spreads = {'L0_attn_ln_w': (1.0, 0.6),
     'L0_attn_ln_b': (0.0, 0.8),
     'L0_attn_f_b_conv': (0.0, 0.8),
     'L0_attn_f_D': (1.0, 0.6),
     'L0_attn_b_b_conv': (0.0, 0.8),
     'L0_attn_b_D': (1.0, 0.6)}
    factors = {'L0_attn_f_W_in': 8.0,
     'L0_attn_f_W_conv': 8.0,
     'L0_attn_f_W_x': 8.0,
     'L0_attn_f_W_dt': 8.0,
     'L0_attn_f_b_dt': 8.0,
     'L0_attn_f_A_log': 8.0,
     'L0_attn_f_W_out': 8.0,
     'L0_attn_b_W_in': 8.0,
     'L0_attn_b_W_conv': 8.0,
     'L0_attn_b_W_x': 8.0,
     'L0_attn_b_W_dt': 8.0,
     'L0_attn_b_b_dt': 8.0,
     'L0_attn_b_A_log': 8.0,
     'L0_attn_b_W_out': 8.0,
     'L0_ffn_b1': 64.0,
     'L0_ffn_b2': 64.0,
     'L0_ffn_b3': 64.0,
     'L0_ffn_gate_w': 8.0,
     'L0_ffn_w1': 8.0,
     'L0_ffn_w2': 8.0,
     'L0_ffn_w3': 8.0,
     'L0_ffn_sw1': 8.0,
     'L0_ffn_sw2': 8.0,
     'L0_ffn_sw3': 8.0}
    for name, (base, spread) in spreads.items():
        noise = np.random.default_rng([zlib.crc32(name.encode()), seed]).standard_normal(out[name].shape)
        drawn = base * np.exp(spread * noise) if base else spread * noise
        out[name] = jnp.asarray(drawn.astype(out[name].dtype))
    for name, factor in factors.items():
        out[name] = (out[name] * factor).astype(out[name].dtype)
    return out
```

```python
from contextlib import ExitStack

import concourse.bass as bass
from concourse import mybir

ALU = mybir.AluOpType
ACT = mybir.ActivationFunctionType
AX_X = mybir.AxisListType.X
F32 = mybir.dt.float32
BF16 = mybir.dt.bfloat16

P = 128
BATCH, SEQ, DM = 2, 2048, 256
DI = 2 * DM
DS = 16
DR = DM // 16
TAPS = 4
HALO = TAPS - 1
TB = 512
NBLK = BATCH * SEQ // TB
SEG = SEQ // TB
NT = TB // P
KD = DM // P
NC = DI // P
GN = 4
NG = DS // GN
UNITS = NC * NG
STEPS = 2 * NBLK
NE = 8
BIG = 3.4e38
EPS = 1e-5
ROWS = 2 * DS

ROW_GROUPS = [(0, 0), (0, 1), (1, 0), (0, 2), (1, 1), (0, 3), (1, 2), (1, 3)]
HEAD_ROWS = 20


def rows_until(is_c, g):
    return GN * (ROW_GROUPS.index((is_c, g)) + 1)


def row_of(r):
    is_c, g = ROW_GROUPS[r // GN]
    return is_c, g * GN + r % GN


G_USES = (
    [("weight", e) for e in range(4)] + [("T", 0), ("weight", 4), ("weight", 5), ("gate", 0), ("weight", 6), ("weight", 7)],
    [("mask", e) for e in range(4)] + [("T", 1)] + [("mask", e) for e in (4, 5, 6, 7)] + [("wmT", 1)])
G_FIRST = ([("T", 0), ("gate", 0)], [("T", 1), ("wmT", 1)])
H_USES = 2 * NE + NC
Y_USES = 2 * NE
ROUTE = 10

STEP_USES = (
    [("row", r, (r + 1) % 2) for r in range(HEAD_ROWS, ROWS)]
    + [("xp", 0, 0), ("xp", 1, 1), ("out", 0, 0), ("out", 1, 1), ("xp", 2, 0), ("xp", 3, 1)]
    + [("z", c, c % 2) for c in range(NC)]
    + [("xdbl", 0, 0), ("dt", 0, 1), ("dt", 1, 0), ("dt", 2, 1), ("dt", 3, 0)]
    + [("row", r, (r + 1) % 2) for r in range(HEAD_ROWS)])
FIRST_USES = [u for u in STEP_USES if u[0] in ("xp", "xdbl", "dt") or u[0] == "row" and u[1] < HEAD_ROWS]


def uses_of_step(step):
    if step == -1:
        return FIRST_USES
    if step == STEPS:
        return [u for u in STEP_USES if u[0] == "out"]
    own = [u for u in STEP_USES if u[0] in ("out", "z") or u[0] == "row" and u[1] >= HEAD_ROWS]
    uses = own if step == STEPS - 1 else STEP_USES
    return [u for u in uses if u[0] != "out"] if step == 0 else uses


def bank_use(step, kind, index):
    bank = [u[2] for u in STEP_USES if u[:2] == (kind, index)][0]
    of_bank = lambda uses: [u[:2] for u in uses if u[2] == bank]
    if isinstance(step, int):
        return bank, (sum(len(of_bank(uses_of_step(k))) for k in range(-1, step))
                      + of_bank(uses_of_step(step)).index((kind, index)))
    mine = of_bank(STEP_USES)
    return bank, len(of_bank(FIRST_USES)) - 1 + len(mine) * step + mine.index((kind, index))


def mixer_and_experts(nc, A, out):
    with ExitStack() as top:
        sem = lambda name: top.enter_context(nc.semaphore(name))
        dram = lambda name, shape: nc.dram_tensor(name, shape, F32, kind="Internal").ap()

        xnT_dram = dram("xnT_scratch", (NBLK, P, KD * TB))
        t_dram = dram("t_scratch", (NBLK, P, NT * DM))
        mod_dram = dram("mod_scratch", (P, BATCH * 4 * DM))

        psum = top.enter_context(nc.psum_tensor("psum", [P, 8, TB], F32))
        keep = lambda name, shape, dt=F32: top.enter_context(nc.sbuf_tensor(name, shape, dt))
        ident = keep("ident", [P, P])
        row_pick = keep("row_pick", [96, 32], BF16)
        row_pick32 = keep("row_pick32", [96, 32])

        mix = ExitStack()
        sb2 = lambda name, shape, dt=F32: mix.enter_context(nc.sbuf_tensor(name, shape, dt))
        w_in = sb2("w_in", [P, 2, KD, 2 * DI])
        w_x = sb2("w_x", [P, 2, NC, 48])
        w_dt = sb2("w_dt", [48, 2, DI])
        w_out = sb2("w_out", [P, 2, NC, DM])
        neg_a = sb2("neg_a", [P, 2, NC, DS])
        w_conv = sb2("w_conv", [P, 2, NC, TAPS])
        b_conv = sb2("b_conv", [P, 2, NC])
        b_dt = sb2("b_dt", [P, 2, NC])
        d_skip = sb2("d_skip", [P, 2, NC])
        limits = sb2("limits", [P, NBLK, 2])

        pre = ExitStack()
        sb1 = lambda name, shape, dt=F32: pre.enter_context(nc.sbuf_tensor(name, shape, dt))
        cT = sb1("cT", [P, KD, BATCH])
        c_wide = sb1("c_wide", [P, KD, BATCH, P])
        w_mod = sb1("w_mod", [P, KD, 6 * DM])
        mod = sb1("mod", [P, BATCH, 6, DM])
        mod_abs = sb1("mod_abs", [P, BATCH, DM])
        mod_sign = sb1("mod_sign", [P, BATCH, DM])
        ln_w = sb1("ln_w", [P, KD])
        ln_b = sb1("ln_b", [P, KD])
        X = sb1("X", [P, NBLK * NT, DM])
        H = sb1("H", [P, NBLK * NT, DM])
        stats = sb1("stats", [P, NBLK * NT, 6])
        mv = sb1("mv", [P, 2, NBLK * NT, 2])
        var_eps = sb1("var_eps", [P, 2, NBLK * NT])
        rstd = sb1("rstd", [P, 2, NBLK * NT])
        minus_half = sb1("minus_half", [P, SEG * NT])
        xnT_out = sb1("xnT_out", [P, 2, KD, TB])
        pre.close()

        xnT = sb2("xnT", [P, 2, KD, TB])
        xc = sb2("xc", [P, 2, NC, TB])
        dt = sb2("dt", [P, 2, NC, TB])
        sp_tmp = sb2("sp_tmp", [P, 2, TB])
        t_blk = sp_tmp[:, :, :].rearrange("p a b -> p (a b)")
        xp = sb2("xp", [P, 2, TB + HALO])
        halo = sb2("halo", [P, 2, NC, HALO])
        limit_now = sb2("limit_now", [P, 2, 2])
        sz = sb2("sz", [P, NC, TB])
        b_wide = sb2("b_wide", [P, 2, DS, TB])
        dbu = sb2("dbu", [P, 2, GN, TB])
        hst = sb2("hst", [P, 4, GN, TB])
        state = sb2("state", [P, 2, UNITS * GN])
        dtx = sb2("dtx", [48, TB])
        bc_r = sb2("bc_r", [32, TB])
        bc_mid = sb2("bc_mid", [32, TB], BF16)
        bc3 = sb2("bc3", [96, TB], BF16)
        mix.close()
        PS_A, PS_U, PS_Y, PS_P = 0, 4, 5, 6

        ffn = ExitStack()
        sb3 = lambda name, shape, dt_=F32: ffn.enter_context(nc.sbuf_tensor(name, shape, dt_))
        w1 = sb3("w1", [P, NE, KD, DM])
        w2 = sb3("w2", [P, NE, KD, DM])
        w3 = sb3("w3", [P, NE, KD, DM])
        b1 = sb3("b1", [P, NE, KD])
        b2 = sb3("b2", [P, NE, KD])
        b3 = sb3("b3", [P, NE, KD])
        sw1 = sb3("sw1", [P, KD, 2 * DM])
        sw2 = sb3("sw2", [P, KD, 2 * DM])
        sw3 = sb3("sw3", [P, NC, DM])
        gate = sb3("gate", [P, KD, NE])
        fmod = sb3("fmod", [P, BATCH, 4, DM])
        lower = sb3("lower", [P, NE, NE])
        minus_half3 = sb3("minus_half3", [P, NT])
        xin = sb3("xin", [P, NT, DM])
        tin = sb3("tin", [P, NT, DM])
        x1 = sb3("x1", [P, 2, NT, DM])
        h2 = sb3("h2", [P, NT, DM])
        h2T = sb3("h2T", [P, 2, KD, TB])
        fstats = sb3("fstats", [P, NT, 6])
        fmv = sb3("fmv", [P, NT, 2])
        fvar = sb3("fvar", [P, NT])
        frstd = sb3("frstd", [P, NT])
        fmax = sb3("fmax", [P, NT])
        fsum = sb3("fsum", [P, NT])
        score = sb3("score", [P, NT, NE])
        cmp_gt = sb3("cmp_gt", [P, NT, NE, NE])
        cmp_eq = sb3("cmp_eq", [P, NT, NE, NE])
        rank = sb3("rank", [P, NT, NE])
        wm = sb3("wm", [P, NT, 2 * NE])
        wm_r = sb3("wm_r", [16, TB])
        wm_mid = sb3("wm_mid", [16, TB], BF16)
        wm3 = sb3("wm3", [96, 2, TB], BF16)
        mask_wide = sb3("mask_wide", [P, 2, TB])
        xs = sb3("xs", [P, 2, KD, TB])
        h1 = sb3("h1", [P, 2, KD, TB])
        m3 = sb3("m3", [P, 2, KD, TB])
        prod = sb3("prod", [P, 2, KD, TB])
        y = sb3("y", [P, 2, KD, TB])
        g_silu = sb3("g_silu", [P, 2, TB])
        u_sh = sb3("u_sh", [P, NC, TB])
        o_blk = sb3("o_blk", [P, 2, NT, DM])
        ffn.close()

        phase = sem("phase")
        waited = sem("waited")
        w_loaded = sem("w_loaded")
        x_loaded = [sem("x_loaded0"), sem("x_loaded1")]
        w_mod_loaded = sem("w_mod_loaded")
        consts = sem("consts")
        neg_a_done = sem("neg_a_done")
        w_out_done = sem("w_out_done")
        c_ready = sem("c_ready")
        mod_full = sem("mod_full")
        mod_copied = sem("mod_copied")
        mod_step = sem("mod_step")
        mod_stored = sem("mod_stored")
        p1_stat = sem("p1_stat")
        p1_aggr = sem("p1_aggr")
        p1_var = sem("p1_var")
        p1_rstd = sem("p1_rstd")
        p1_norm = sem("p1_norm")
        p1_scaled = sem("p1_scaled")
        h_done = sem("h_done")
        h_stored = sem("h_stored")
        xn_done = sem("xn_done")
        xnT_full = sem("xnT_full")
        xnT_copied = sem("xnT_copied")
        xnT_stored = [sem("xnT_stored0"), sem("xnT_stored1")]
        xnT_loaded = [sem("xnT_loaded0"), sem("xnT_loaded1")]
        bank_full = [sem("bank_full0"), sem("bank_full1")]
        bank_free = [sem("bank_free0"), sem("bank_free1")]
        xp_head = sem("xp_head")
        halo_saved = sem("halo_saved")
        conv_step = sem("conv_step")
        conv_done = sem("conv_done")
        xc_done = sem("xc_done")
        dtx_done = sem("dtx_done")
        bc_hi = sem("bc_hi")
        bc_mid_done = sem("bc_mid_done")
        bc_lo = sem("bc_lo")
        sp_step = sem("sp_step")
        sp_done = sem("sp_done")
        dt_done = sem("dt_done")
        dtu_done = sem("dtu_done")
        exp_done = sem("exp_done")
        mult_done = sem("mult_done")
        scan_done = sem("scan_done")
        limit_set = sem("limit_set")
        prod_done = sem("prod_done")
        state_saved = sem("state_saved")
        unit_summed = sem("unit_summed")
        y_skip = sem("y_skip")
        yg_done = sem("yg_done")
        t_loaded = sem("t_loaded")
        t_stored = sem("t_stored")
        zeroed = sem("zeroed")
        f_gate_loaded = sem("f_gate_loaded")
        f_w_loaded = sem("f_w_loaded")
        f_const = sem("f_const")
        wm3_zeroed = sem("wm3_zeroed")
        f_in = sem("f_in")
        f_x1 = sem("f_x1")
        f_stat = sem("f_stat")
        f_aggr = sem("f_aggr")
        f_var = sem("f_var")
        f_rstd = sem("f_rstd")
        f_norm = sem("f_norm")
        f_scaled = sem("f_scaled")
        f_h2 = sem("f_h2")
        f_route = sem("f_route")
        f_exp = sem("f_exp")
        f_wm = sem("f_wm")
        f_whi = sem("f_whi")
        f_wmid = sem("f_wmid")
        f_wlo = sem("f_wlo")
        f_h2T = sem("f_h2T")
        g_full = [sem("g_full0"), sem("g_full1")]
        g_free = [sem("g_free0"), sem("g_free1")]
        f_mask = sem("f_mask")
        f_xs = sem("f_xs")
        f_h1_full = sem("f_h1_full")
        f_h1 = sem("f_h1")
        f_x3_full = sem("f_x3_full")
        f_m3 = sem("f_m3")
        f_x2_full = sem("f_x2_full")
        f_prod = sem("f_prod")
        f_y = sem("f_y")
        f_sh_u = sem("f_sh_u")
        f_o_full = sem("f_o_full")
        f_o_mul = sem("f_o_mul")
        f_o = sem("f_o")
        f_out = [sem("f_out0"), sem("f_out1")]

        block = top.enter_context(nc.Block())

        def meet(eng, n):
            eng.drain().then_inc(phase, 1)
            eng.wait_ge(phase, 5 * n)

        def time_order(ap, backward):
            return ap[:, ::-1] if backward else ap

        def wait_apart(eng):
            eng.sem_inc(waited, 1)

        def filled(eng, S, kind, index):
            bank, before = bank_use(S, kind, index)
            eng.wait_ge(bank_full[bank], before + 1)
            return PS_P + bank

        def drained(eng, S, kind, index):
            bank, before = bank_use(S, kind, index)
            eng.wait_ge(bank_free[bank], before + 1)

        def rows_ready(eng, is_c, g, q):
            r = rows_until(is_c, g) - 1
            drained(eng, q if r >= HEAD_ROWS else q - 1, "row", r)

        def take_bank(pe, S, kind, index):
            bank, before = bank_use(S, kind, index)
            if not (isinstance(before, int) and before == 0):
                pe.wait_ge(bank_free[bank], before)
            return bank

        def run_steps(eng, step):
            step(0, 0, 0)
            step(0, 1, 1)
            with eng.Fori(1, NBLK - 1) as i:
                step(i, 0, 2 * i)
                step(i, 1, 2 * i + 1)
            step(NBLK - 1, 0, STEPS - 2)
            step(NBLK - 1, 1, STEPS - 1)

        def is_first(q):
            return isinstance(q, int) and q == 0

        def is_last(q):
            return isinstance(q, int) and q == STEPS - 1

        def run_blocks(eng, body):
            body(0, 0)
            body(1, 1)
            with eng.Fori(1, NBLK // 2 - 1) as k:
                for half in range(2):
                    body(half, 2 * k + half)
            body(0, NBLK - 2)
            body(1, NBLK - 1)

        def g_count(i, kind, index, bank):
            if isinstance(i, int) and i == -1:
                return G_FIRST[bank].index((kind, index))
            uses = G_USES[bank]
            if isinstance(i, int) and i == NBLK - 1:
                uses = [u for u in uses if u not in G_FIRST[bank]]
            return len(G_FIRST[bank]) + len(G_USES[bank]) * i + uses.index((kind, index))

        def g_bank(kind, index):
            return {"T": index, "gate": 0, "weight": 0, "mask": 1, "wmT": 1}[kind]

        def g_filled(eng, i, kind, index):
            bank = g_bank(kind, index)
            eng.wait_ge(g_full[bank], g_count(i, kind, index, bank) + 1)

        def g_drained(eng, i, kind, index):
            bank = g_bank(kind, index)
            eng.wait_ge(g_free[bank], g_count(i, kind, index, bank) + 1)

        def g_take(pe, i, kind, index):
            bank = g_bank(kind, index)
            before = g_count(i, kind, index, bank)
            if not (isinstance(before, int) and before == 0):
                pe.wait_ge(g_free[bank], before)

        @block.sync
        def _(sp):
            for b in range(BATCH):
                sp.dma_start(X[:, b * SEG * NT:(b + 1) * SEG * NT, :].rearrange("p (k t) d -> p k (t d)", t=NT),
                             A["x"][b * SEG:(b + 1) * SEG].rearrange("k p n -> p k n")).then_inc(x_loaded[b], 16)
                if b == 0:
                    sp.dma_start(w_mod[:], A["w_mod"]).then_inc(w_mod_loaded, 16)
                    sp.dma_start(cT[:], A["cT"]).then_inc(w_mod_loaded, 16)
                    sp.dma_start(ln_w[:], A["ln_w"]).then_inc(w_mod_loaded, 16)
                    sp.dma_start(ln_b[:], A["ln_b"]).then_inc(w_mod_loaded, 16)
            for dst, name in ((neg_a, "a_log"), (w_in, "w_in"), (w_x, "w_x"), (w_out, "w_out"),
                              (w_conv, "w_conv"), (b_conv, "b_conv"), (b_dt, "b_dt"), (d_skip, "d_skip")):
                sp.dma_start(dst[:], A[name]).then_inc(w_loaded, 16)
            sp.dma_start(w_dt[32:48], A["w_dt"]).then_inc(w_loaded, 16)
            sp.wait_ge(mod_step, 10)
            sp.dma_start(mod_dram, mod[:, :, 2:6, :]).then_inc(mod_stored, 16)
            with sp.Fori(0, NBLK) as k:
                sp.wait_ge(h_done, k + 1)
                sp.dma_start(t_dram[bass.ds(k, 1)].rearrange("k p n -> (k p) n"),
                             H[:, bass.ds(k * NT, NT), :].rearrange("p t d -> p (t d)")).then_inc(h_stored, 16)
            with sp.Fori(0, NBLK // 2) as k:
                for half in range(2):
                    sp.wait_ge(xnT_copied, k * 4 + 2 * half + 2)
                    sp.dma_start(xnT_dram[bass.ds(2 * k + half, 1)].rearrange("k p n -> (k p) n"),
                                 xnT_out[:, half].rearrange("p k t -> p (k t)")).then_inc(xnT_stored[half], 16)
            sp.wait_ge(h_stored, 16 * NBLK)
            sp.wait_ge(mod_stored, 16)
            sp.wait_ge(w_loaded, 16 * 9)
            for half in range(2):
                sp.wait_ge(xnT_stored[half], 16 * NBLK // 2)
            meet(sp, 1)

            def block_of(i, D):
                if D == 0:
                    return i
                return (i // SEG) * SEG + (SEG - 1 - i % SEG)

            def load_xnT(i, D):
                wait_apart(sp)
                sp.dma_start(xnT[:, D].rearrange("p k t -> p (k t)"),
                             xnT_dram[bass.ds(block_of(i, D), 1)].rearrange("k p n -> (k p) n")
                             ).then_inc(xnT_loaded[D], 16)

            def accumulate(i, D, q):
                if not is_first(q):
                    sp.wait_ge(t_stored, 16 * q)
                sp.wait_ge(dt_done, NC * (q + (1 if is_last(q) else 2)))
                wait_apart(sp)
                sp.dma_start(t_blk, t_dram[bass.ds(block_of(i, D), 1)].rearrange("k p n -> (k p) n")
                             ).then_inc(t_loaded, 16)
                drained(sp, q + 1, "out", 1)
                wait_apart(sp)
                sp.dma_start(t_dram[bass.ds(block_of(i, D), 1)].rearrange("k p n -> (k p) n"), t_blk
                             ).then_inc(t_stored, 16)

            load_xnT(0, 0)
            load_xnT(0, 1)

            def step(i, D, q):
                if not is_first(q):
                    accumulate(i if D else i - 1, 1 - D, q - 1)
                if not (isinstance(q, int) and q + 2 >= STEPS):
                    filled(sp, q, "z", 3)
                    load_xnT(i + 1, D)

            run_steps(sp, step)
            accumulate(NBLK - 1, 1, STEPS - 1)
            sp.wait_ge(t_stored, 16 * STEPS)
            meet(sp, 2)

            for dst, name in ((gate, "gate"), (fmod, None)):
                sp.dma_start(dst[:], mod_dram if name is None else A[name]).then_inc(f_gate_loaded, 16)

            def load_block(i):
                wait_apart(sp)
                sp.dma_start(xin[:].rearrange("p t d -> p (t d)"),
                             A["x"][bass.ds(i, 1)].rearrange("k p n -> (k p) n")).then_inc(f_in, 16)
                sp.dma_start(tin[:].rearrange("p t d -> p (t d)"),
                             t_dram[bass.ds(i, 1)].rearrange("k p n -> (k p) n")).then_inc(f_in, 16)

            load_block(0)
            for dst, name in ((w1, "w1"), (w3, "w3"), (w2, "w2"), (b1, "b1"), (b2, "b2"), (b3, "b3"),
                              (sw1, "sw1"), (sw2, "sw2"), (sw3, "sw3")):
                sp.dma_start(dst[:], A[name]).then_inc(f_w_loaded, 16)

            def store_block(i, half):
                sp.wait_ge(f_o, i + 1)
                wait_apart(sp)
                sp.dma_start(out[bass.ds(i, 1)].rearrange("k p n -> (k p) n"),
                             o_blk[:, half].rearrange("p t d -> p (t d)")).then_inc(f_out[half], 16)

            sp.wait_ge(f_x1, 2)
            load_block(1)
            with sp.Fori(0, NBLK // 2 - 1) as k:
                for half in range(2):
                    sp.wait_ge(f_x1, k * 4 + 2 * half + 4)
                    load_block(2 * k + half + 2)
                    store_block(2 * k + half, half)
            store_block(NBLK - 2, 0)
            store_block(NBLK - 1, 1)
            for half in range(2):
                sp.wait_ge(f_out[half], 16 * NBLK // 2)

        @block.gpsimd
        def _(pool):
            nc.gpsimd.memset(ident[:], 0.0).then_inc(consts, 1)
            nc.gpsimd.memset(row_pick32[:], 0.0).then_inc(consts, 1)
            nc.gpsimd.memset(minus_half[:], -0.5).then_inc(consts, 1)
            pool.wait_ge(consts, 3)
            nc.gpsimd.affine_select(out=ident[:], in_=ident[:], compare_op=ALU.not_equal, fill=1.0,
                                    base=0, pattern=[[-1, P]], channel_multiplier=1).then_inc(consts, 1)
            for part in range(3):
                nc.gpsimd.affine_select(out=row_pick32[:], in_=row_pick32[:], compare_op=ALU.not_equal,
                                        fill=1.0, base=-32 * part, pattern=[[-1, 32]],
                                        channel_multiplier=1).then_inc(consts, 1)
                pool.wait_ge(consts, 5 + part)
            nc.gpsimd.tensor_copy(row_pick[:], row_pick32[:]).then_inc(consts, 1)
            for k in range(NBLK):
                bound = 0.0 if k % SEG == SEG - 1 else BIG
                nc.gpsimd.memset(limits[:, k, 0:1], bound).then_inc(consts, 1)
                nc.gpsimd.memset(limits[:, k, 1:2], -bound).then_inc(consts, 1)
            pool.wait_ge(consts, 8 + 2 * NBLK)

            span = SEG * NT
            for ln in range(2):
                for b in range(BATCH):
                    n = ln * BATCH + b
                    pool.wait_ge(p1_var, n + 1)
                    nc.gpsimd.tensor_tensor(rstd[:, ln, b * span:(b + 1) * span],
                                            var_eps[:, ln, b * span:(b + 1) * span], minus_half[:],
                                            ALU.pow).then_inc(p1_rstd, 1)
                if ln == 0:
                    for b in range(BATCH):
                        with pool.Fori(0, SEG) as s:
                            pool.wait_ge(p1_scaled, s + (b * SEG + 1))
                            Hb = H[:, bass.ds(s * NT + b * span, NT), :]
                            nc.gpsimd.tensor_tensor(Hb, Hb, mod[:, b, 0:1, :].broadcast_to((P, NT, DM)),
                                                    ALU.add).then_inc(h_done, 1)
            meet(pool, 1)

            nc.gpsimd.memset(state[:], 0.0).then_inc(zeroed, 1)
            nc.gpsimd.memset(halo[:], 0.0).then_inc(zeroed, 1)

            def set_limit(i, D):
                nc.gpsimd.tensor_copy(limit_now[:, D:D + 1, :], limits[:, bass.ds(i, 1), :]).then_inc(limit_set, 1)

            def clamp(dst, src, D, signal):
                nc.gpsimd.tensor_scalar(dst, src, limit_now[:, D, 0:1], limit_now[:, D, 1:2],
                                        ALU.min, ALU.max).then_inc(signal, 1)

            def save_halo(c, D, q):
                pool.wait_ge(limit_set, q + 1)
                drained(pool, q - 1, "xp", c)
                wait_apart(pool)
                edge = slice(TB, TB + HALO) if D == 0 else slice(0, HALO)
                clamp(halo[:, D, c, :], xp[:, c % 2, edge], D, halo_saved)

            def add_dt(c, D, q):
                pool.wait_ge(sp_done, NC * q + c + 1)
                nc.gpsimd.tensor_tensor(dt[:, D, c, :], dt[:, D, c, :], sp_tmp[:, c % 2, :],
                                        ALU.add).then_inc(dt_done, 1)

            def unit(u, D, q):
                g = u % NG
                U = UNITS * q + u
                last = TB - 1 if D == 0 else 0
                h = hst[:, u % 4, :, :]
                pool.wait_ge(scan_done, GN * U + GN)
                wait_apart(pool)
                clamp(state[:, D, u * GN:(u + 1) * GN].rearrange("p (a b) -> p a b", b=1),
                      h[:, :, last:last + 1], D, state_saved)
                rows_ready(pool, 1, g, q)
                pool.wait_ge(state_saved, U + 1)
                nc.gpsimd.tensor_tensor(h, h, b_wide[:, 1, g * GN:(g + 1) * GN, :],
                                        ALU.mult).then_inc(prod_done, 1)

            set_limit(0, 0)
            pool.wait_ge(zeroed, 2)
            for c in range(NC):
                save_halo(c, 0, 0)
            for c in range(NC):
                add_dt(c, 0, 0)

            def step(i, D, q):
                for t in range(UNITS):
                    ahead = not is_last(q)
                    if ahead and t == 2:
                        set_limit(i + D, 1 - D)
                    if ahead and t == 4:
                        save_halo(0, 1 - D, q + 1)
                        save_halo(1, 1 - D, q + 1)
                    if ahead and t in (6, 7):
                        save_halo(t - 4, 1 - D, q + 1)
                    if ahead and t == 12:
                        add_dt(0, 1 - D, q + 1)
                    if ahead and t == 13:
                        add_dt(2, 1 - D, q + 1)
                    if ahead and t == 14:
                        add_dt(3, 1 - D, q + 1)
                    if t > 0:
                        unit(t - 1, D, q)
                    elif not is_first(q):
                        unit(UNITS - 1, 1 - D, q - 1)
                    if ahead and t == 12:
                        add_dt(1, 1 - D, q + 1)

            run_steps(pool, step)
            unit(UNITS - 1, 1, STEPS - 1)
            meet(pool, 2)

            nc.gpsimd.memset(minus_half3[:], -0.5).then_inc(f_const, 1)
            nc.gpsimd.memset(lower[:], 1.0).then_inc(f_const, 1)
            pool.wait_ge(f_const, 2)
            nc.gpsimd.affine_select(out=lower[:], in_=lower[:], compare_op=ALU.is_gt, fill=0.0, base=0,
                                    pattern=[[1, NE], [-1, NE]], channel_multiplier=0).then_inc(f_const, 1)
            pool.wait_ge(f_gate_loaded, 32)

            def mod_row(n, j):
                return fmod[:, bass.ds(n // SEG, 1), j:j + 1, :].rearrange(
                    "p a b d -> p (a b) d").broadcast_to((P, NT, DM))

            def norm_power(n):
                pool.wait_ge(f_var, n + 1)
                nc.gpsimd.tensor_tensor(frstd[:], fvar[:], minus_half3[:], ALU.pow).then_inc(f_rstd, 1)

            def norm_shift(n):
                pool.wait_ge(f_scaled, n + 1)
                nc.gpsimd.tensor_tensor(h2[:], h2[:], mod_row(n, 1), ALU.add).then_inc(f_h2, 1)

            def add_expert(e, half, i):
                pool.wait_ge(f_prod, 2 * NE * i + 2 * e + 2)
                if e > 1:
                    pool.wait_ge(f_y, (NE - 1) * i + e - 1)
                nc.gpsimd.tensor_tensor(y[:, half], y[:, half], prod[:, e % 2], ALU.add).then_inc(f_y, 1)

            def add_residual(half, i):
                pool.wait_ge(f_o_mul, 2 * i + 2)
                nc.gpsimd.tensor_tensor(o_blk[:, half], o_blk[:, half], x1[:, half], ALU.add).then_inc(f_o, 1)

            def body(half, i):
                ahead = not (isinstance(i, int) and i == NBLK - 1)
                for e in range(1, NE):
                    if ahead and e == 1:
                        norm_power(i + 1)
                    add_expert(e, half, i)
                    if ahead and e == 2:
                        norm_shift(i + 1)
                add_residual(half, i)

            norm_power(0)
            norm_shift(0)
            run_blocks(pool, body)

        @block.scalar
        def _(act):
            act.wait_ge(w_mod_loaded, 16 * 4)
            for k in range(KD):
                for b in range(BATCH):
                    nc.scalar.activation(c_wide[:, k, b, :], cT[:, k, b:b + 1].broadcast_to((P, P)),
                                         ACT.Silu).then_inc(c_ready, 1)
            for b in range(BATCH):
                for j in range(3):
                    act.wait_ge(mod_full, 3 * b + j + 1)
                    nc.scalar.activation(mod[:, b, 2 * j:2 * j + 2, :].rearrange("p a d -> p (a d)"),
                                         psum[:, 3 * b + j, :], ACT.Copy).then_inc(mod_copied, 1)
            act.wait_ge(w_loaded, 16 * 9)
            nc.scalar.activation(neg_a[:], neg_a[:], ACT.Exp).then_inc(neg_a_done, 1)

            def copy_xnT(k):
                for half in range(2):
                    for kd in range(KD):
                        act.wait_ge(xnT_full, k * 4 + 2 * half + kd + 1)
                        if not isinstance(k, int):
                            act.wait_ge(xnT_stored[half], 16 * k)
                        nc.scalar.activation(xnT_out[:, half, kd, :], psum[:, 2 * half + kd, :], ACT.Identity,
                                             scale=ln_w[:, kd:kd + 1], bias=ln_b[:, kd:kd + 1]
                                             ).then_inc(xnT_copied, 1)

            copy_xnT(0)
            with act.Fori(1, NBLK // 2) as k:
                copy_xnT(k)
            meet(act, 1)

            def copy_xp(c, D, q):
                if not (isinstance(q, int) and q == 0 and c < 2):
                    act.wait_ge(conv_done, NC * q + c - 1)
                    act.wait_ge(halo_saved, NC * q + c - 1)
                edge = slice(0, HALO) if D == 0 else slice(TB, TB + HALO)
                body_ = slice(HALO, HALO + TB) if D == 0 else slice(0, TB)
                nc.scalar.activation(xp[:, c % 2, edge], halo[:, D, c, :], ACT.Copy).then_inc(xp_head, 1)
                bank = filled(act, q - 1, "xp", c)
                nc.scalar.activation(xp[:, c % 2, body_], psum[:, bank, :], ACT.Copy
                                     ).then_inc(bank_free[bank - PS_P], 1)

            def silu_z(c, q):
                if not is_first(q):
                    act.wait_ge(yg_done, NC * q)
                bank = filled(act, q, "z", c)
                nc.scalar.activation(sz[:, c, :], psum[:, bank, :], ACT.Silu).then_inc(bank_free[bank - PS_P], 1)

            def silu_xc(c, D, q):
                act.wait_ge(conv_done, NC * q + c + 1)
                nc.scalar.activation(xc[:, D, c, :], xc[:, D, c, :], ACT.Silu,
                                     bias=b_conv[:, D, c:c + 1]).then_inc(xc_done, 1)

            def split_hi(q):
                bank = filled(act, q - 1, "xdbl", 0)
                nc.scalar.activation(dtx[32:48, :], psum[32:48, bank, :], ACT.Copy).then_inc(dtx_done, 1)
                nc.scalar.activation(bc3[0:32, :], psum[0:32, bank, :], ACT.Copy).then_inc(bc_hi, 1)

            def split_mid(q):
                drained(act, q - 1, "xdbl", 0)
                nc.scalar.activation(bc_mid[:], bc_r[:], ACT.Copy).then_inc(bc_mid_done, 1)
                nc.scalar.activation(bc3[32:64, :], bc_r[:], ACT.Copy).then_inc(bc_mid_done, 1)

            def softplus(c, D, q):
                if not (isinstance(q, int) and q == 0 and c < 2):
                    act.wait_ge(dt_done, NC * q + c - 1)
                if isinstance(q, int) and q < 2:
                    pass
                else:
                    act.wait_ge(t_stored, 16 * (q - 1))
                bank = filled(act, q - 1, "dt", c)
                tmp = sp_tmp[:, c % 2, :]
                nc.scalar.activation(dt[:, D, c, :], psum[:, bank, :], ACT.Relu,
                                     bias=b_dt[:, D, c:c + 1]).then_inc(sp_step, 1)
                nc.scalar.activation(tmp, psum[:, bank, :], ACT.Abs,
                                     bias=b_dt[:, D, c:c + 1]).then_inc(bank_free[bank - PS_P], 1)
                drained(act, q - 1, "dt", c)
                nc.scalar.activation(tmp, tmp, ACT.Exp, scale=-1.0).then_inc(sp_step, 1)
                act.wait_ge(sp_step, 2 * (NC * q + c) + 2)
                nc.scalar.activation(tmp, tmp, ACT.Ln, bias=1.0).then_inc(sp_done, 1)

            def copy_row(r, S, q):
                is_c, n = row_of(r)
                if not is_first(q) and n % GN == 0:
                    reader = prod_done if is_c else mult_done
                    act.wait_ge(reader, UNITS * (q - 1) + UNITS - NG + n // GN + 1)
                bank = filled(act, S, "row", r)
                nc.scalar.activation(b_wide[:, is_c, n, :], psum[:, bank, :], ACT.Copy
                                     ).then_inc(bank_free[bank - PS_P], 1)

            def decay(u, n, D, q):
                c, g = divmod(u, NG)
                K = GN * (UNITS * q + u) + n
                if g == 0 and n == 0:
                    act.wait_ge(dt_done, NC * q + c + 1)
                if not (isinstance(K, int) and K < GN):
                    act.wait_ge(scan_done, K - GN + 1)
                nc.scalar.activation(psum[:, PS_A + n, :], dt[:, D, c, :], ACT.Exp,
                                     scale=neg_a[:, D, c, g * GN + n:g * GN + n + 1]).then_inc(exp_done, 1)

            act.wait_ge(zeroed, 2)
            for c in range(NC):
                copy_xp(c, 0, 0)
            for c in range(NC):
                silu_xc(c, 0, 0)
            split_hi(0)
            split_mid(0)
            for c in range(NC):
                softplus(c, 0, 0)
            for r in range(HEAD_ROWS):
                copy_row(r, -1, 0)

            def step(i, D, q):
                for t in range(UNITS):
                    for n in range(GN):
                        decay(t, n, D, q)
                        if t == 0:
                            copy_row(HEAD_ROWS + 2 * n, q, q)
                            copy_row(HEAD_ROWS + 2 * n + 1, q, q)
                        if t == 1:
                            copy_row(HEAD_ROWS + 8 + n, q, q)
                        if t == 8 and n == 3:
                            silu_z(0, q)
                            silu_z(1, q)
                            if not is_last(q):
                                for c in range(NC):
                                    silu_xc(c, 1 - D, q + 1)
                            silu_z(2, q)
                            silu_z(3, q)
                        if is_last(q):
                            continue
                        if (t, n) in ((3, 0), (3, 1), (5, 2), (6, 1)):
                            copy_xp({(3, 0): 0, (3, 1): 1, (5, 2): 2, (6, 1): 3}[t, n], 1 - D, q + 1)
                        if (t, n) == (10, 0):
                            split_hi(q + 1)
                        if (t, n) == (11, 0):
                            split_mid(q + 1)
                        if (t, n) in ((11, 2), (12, 0), (12, 2), (13, 0)):
                            softplus({(11, 2): 0, (12, 0): 1, (12, 2): 2, (13, 0): 3}[t, n], 1 - D, q + 1)
                        if t == 13:
                            copy_row(n, q, q + 1)
                        if t in (14, 15):
                            copy_row(GN + 8 * (t - 14) + 2 * n, q, q + 1)
                            copy_row(GN + 8 * (t - 14) + 2 * n + 1, q, q + 1)

            run_steps(act, step)
            meet(act, 2)

            def h2_transposed(n, half):
                for kd in range(KD):
                    g_filled(act, n - 1, "T", kd)
                    nc.scalar.activation(h2T[:, half, kd, :], psum[:, kd, :], ACT.Copy).then_inc(g_free[kd], 1)

            def exp_scores(n):
                g_drained(act, n - 1, "gate", 0)
                nc.scalar.activation(score[:], score[:], ACT.Exp).then_inc(f_exp, 1)

            def route_hi(n, half):
                g_filled(act, n - 1, "wmT", 1)
                nc.scalar.activation(wm3[0:16, half, :], psum[0:16, 1, :], ACT.Copy).then_inc(f_whi, 1)

            def route_mid(n, half):
                g_drained(act, n - 1, "wmT", 1)
                nc.scalar.activation(wm_mid[:], wm_r[:], ACT.Copy).then_inc(f_wmid, 1)
                nc.scalar.activation(wm3[32:48, half, :], wm_r[:], ACT.Copy).then_inc(f_wmid, 1)

            def mask_row(e, i):
                if not (isinstance(i, int) and i == 0 and e < 2):
                    act.wait_ge(f_m3, 2 * (NE * i + e - 2) + 2)
                g_filled(act, i, "mask", e)
                nc.scalar.activation(mask_wide[:, e % 2, :], psum[:, 1, :], ACT.Copy).then_inc(g_free[1], 1)

            def silu_h1(e, i):
                for hc in range(2):
                    act.wait_ge(f_h1_full, H_USES * i + 2 * e + hc + 1)
                    if not (isinstance(i, int) and i == 0 and e < 2):
                        act.wait_ge(f_x2_full, Y_USES * i + 2 * e - 2)
                    nc.scalar.activation(h1[:, e % 2, hc, :], psum[:, 2 + hc, :], ACT.Silu,
                                         bias=b1[:, e, hc:hc + 1]).then_inc(f_h1, 1)

            def silu_shared(c, i):
                act.wait_ge(f_h1_full, H_USES * i + 2 * NE + c + 1)
                if not (isinstance(i, int) and i == 0 and c < 2):
                    act.wait_ge(f_sh_u, NC * i + c - 1)
                nc.scalar.activation(g_silu[:, c % 2, :], psum[:, 2 + c % 2, :], ACT.Silu).then_inc(f_h1, 1)

            def body(half, i):
                ahead = not (isinstance(i, int) and i == NBLK - 1)
                mask_row(0, i)
                for e in range(NE):
                    if e + 1 < NE:
                        mask_row(e + 1, i)
                    silu_h1(e, i)
                    if ahead and e == 2:
                        h2_transposed(i + 1, 1 - half)
                    if ahead and e == 5:
                        exp_scores(i + 1)
                    if ahead and e == 6:
                        route_hi(i + 1, 1 - half)
                    if ahead and e == 7:
                        route_mid(i + 1, 1 - half)
                for c in range(NC):
                    silu_shared(c, i)

            act.wait_ge(wm3_zeroed, 1)
            h2_transposed(0, 0)
            exp_scores(0)
            route_hi(0, 0)
            route_mid(0, 0)
            act.wait_ge(f_w_loaded, 16 * 9)
            run_blocks(act, body)

        @block.vector
        def _(dve):
            span = SEG * NT

            def statistics(src, ln, b, ready):
                with dve.Fori(0, SEG) as s:
                    for tt in range(NT):
                        tile = s * NT + (b * span + tt)
                        if ready is not None and tt == 0:
                            dve.wait_ge(ready, s + (b * SEG + 1))
                        nc.vector.bn_stats(stats[:, bass.ds(tile, 1), :].rearrange("p a n -> p (a n)"),
                                           src[:, bass.ds(tile, 1), :].rearrange("p a n -> p (a n)")
                                           ).then_inc(p1_stat, 1)
                dve.wait_ge(p1_stat, span * (ln * BATCH + b + 1))
                for tile in range(b * span, (b + 1) * span):
                    nc.vector.bn_aggr(mv[:, ln, tile, :], stats[:, tile, :]).then_inc(p1_aggr, 1)
                dve.wait_ge(p1_aggr, span * (ln * BATCH + b + 1))
                nc.vector.tensor_scalar(var_eps[:, ln, b * span:(b + 1) * span],
                                        mv[:, ln, b * span:(b + 1) * span, 1], EPS, None, ALU.add
                                        ).then_inc(p1_var, 1)

            def normalise(dst, src, ln, tile):
                nc.vector.tensor_scalar(dst[:, bass.ds(tile, 1), :].rearrange("p a n -> p (a n)"),
                                        src[:, bass.ds(tile, 1), :].rearrange("p a n -> p (a n)"),
                                        mv[:, ln, bass.ds(tile, 1), 0:1].rearrange("p a n -> p (a n)"),
                                        rstd[:, ln, bass.ds(tile, 1)],
                                        ALU.subtract, ALU.mult).then_inc(p1_norm, 1)

            dve.wait_ge(x_loaded[0], 16)
            statistics(X, 0, 0, None)
            dve.wait_ge(mod_copied, 6)
            for j in (1, 4):
                nc.vector.tensor_scalar(mod[:, :, j, :], mod[:, :, j, :], 1.0, None, ALU.add).then_inc(mod_step, 1)
            for n, j in enumerate((2, 5)):
                nc.vector.tensor_scalar(mod_abs[:], mod[:, :, j, :], -1.0, 0.25, ALU.mult, ALU.max
                                        ).then_inc(mod_step, 1)
                nc.vector.tensor_scalar(mod_sign[:], mod[:, :, j, :], 0.0, 2.0, ALU.is_ge, ALU.mult
                                        ).then_inc(mod_step, 1)
                dve.wait_ge(mod_step, 2 + 4 * n + 2)
                nc.vector.tensor_tensor(mod_abs[:], mod_abs[:], mod[:, :, j, :], ALU.max).then_inc(mod_step, 1)
                dve.wait_ge(mod_step, 2 + 4 * n + 3)
                nc.vector.scalar_tensor_tensor(mod[:, :, j, :], mod_sign[:], -1.0, mod_abs[:], ALU.add, ALU.mult
                                               ).then_inc(mod_step, 1)
                dve.wait_ge(mod_step, 2 + 4 * n + 4)
            dve.wait_ge(x_loaded[1], 16)
            statistics(X, 0, 1, None)
            for b in range(BATCH):
                dve.wait_ge(p1_rstd, b + 1)
                with dve.Fori(0, SEG) as s:
                    for tt in range(NT):
                        normalise(H, X, 0, s * NT + (b * span + tt))
                    dve.wait_ge(p1_norm, s * NT + (b * span + NT))
                    Hb = H[:, bass.ds(s * NT + b * span, NT), :]
                    nc.vector.tensor_tensor(Hb, Hb, mod[:, b, 1:2, :].broadcast_to((P, NT, DM)),
                                            ALU.mult).then_inc(p1_scaled, 1)
            dve.wait_ge(w_loaded, 16 * 9)
            dve.wait_ge(neg_a_done, 1)
            nc.vector.tensor_scalar(neg_a[:], neg_a[:], -1.0, None, ALU.mult).then_inc(w_out_done, 1)
            nc.vector.tensor_scalar(w_out[:], w_out[:], 0.5, None, ALU.mult).then_inc(w_out_done, 1)
            for b in range(BATCH):
                statistics(H, 1, b, h_done)
            for b in range(BATCH):
                dve.wait_ge(p1_rstd, BATCH + b + 1)
                with dve.Fori(0, SEG) as s:
                    for tt in range(NT):
                        normalise(X, H, 1, s * NT + (b * span + tt))
            meet(dve, 1)

            def conv(c, D, q):
                S = q - 1
                drained(dve, S, "xp", c)
                src = xp[:, c % 2, :]
                dst = xc[:, D, c, :]
                for j in range(TAPS):
                    at = j if D == 0 else HALO - j
                    w = w_conv[:, D, c, j:j + 1]
                    if j == 0:
                        ins = nc.vector.tensor_scalar(dst, src[:, at:at + TB], w, None, ALU.mult)
                    else:
                        dve.wait_ge(conv_step, HALO * (NC * q + c) + j)
                        ins = nc.vector.scalar_tensor_tensor(dst, src[:, at:at + TB], w, dst, ALU.mult, ALU.add)
                    ins.then_inc(conv_step if j < HALO else conv_done, 1)

            def split_r1(q):
                dve.wait_ge(bc_hi, q + 1)
                bank = filled(dve, q - 1, "xdbl", 0)
                nc.vector.tensor_tensor(bc_r[:], psum[0:32, bank, :], bc3[0:32, :], ALU.subtract
                                        ).then_inc(bank_free[bank - PS_P], 1)

            def split_lo(q):
                dve.wait_ge(bc_mid_done, 2 * q + 2)
                nc.vector.tensor_tensor(bc3[64:96, :], bc_r[:], bc_mid[:], ALU.subtract).then_inc(bc_lo, 1)

            def add_skip(c, D, q):
                dve.wait_ge(unit_summed, UNITS * q + NG * (c + 1))
                nc.vector.scalar_tensor_tensor(xc[:, D, c, :], xc[:, D, c, :], d_skip[:, D, c:c + 1],
                                               psum[:, PS_Y, :], ALU.mult, ALU.add).then_inc(y_skip, 1)

            def gate_y(c, D, q):
                dve.wait_ge(y_skip, NC * q + c + 1)
                drained(dve, q, "z", c)
                nc.vector.tensor_tensor(xc[:, D, c, :], xc[:, D, c, :], sz[:, c, :], ALU.mult
                                        ).then_inc(yg_done, 1)

            def add_out(S):
                dve.wait_ge(t_loaded, 16 * S)
                for b in range(2):
                    bank = filled(dve, S, "out", b)
                    dst = t_blk[:, b * TB:(b + 1) * TB]
                    nc.vector.tensor_tensor(dst, dst, psum[:, bank, :], ALU.add
                                            ).then_inc(bank_free[bank - PS_P], 1)

            def multiply(u, D, q):
                c, g = divmod(u, NG)
                U = UNITS * q + u
                if g == 0:
                    dve.wait_ge(dt_done, NC * q + c + 1)
                    dve.wait_ge(xc_done, NC * q + c + 1)
                    if not (isinstance(U, int) and U == 0):
                        dve.wait_ge(mult_done, U)
                    nc.vector.tensor_tensor(psum[:, PS_U, :], dt[:, D, c, :], xc[:, D, c, :], ALU.mult
                                            ).then_inc(dtu_done, 1)
                    dve.wait_ge(dtu_done, NC * q + c + 1)
                rows_ready(dve, 0, g, q)
                if not (isinstance(U, int) and U < 2):
                    dve.wait_ge(scan_done, GN * (U - 1))
                nc.vector.tensor_tensor(dbu[:, u % 2, :, :],
                                        psum[:, PS_U:PS_U + 1, :].broadcast_to((P, GN, TB)),
                                        b_wide[:, 0, g * GN:(g + 1) * GN, :], ALU.mult).then_inc(mult_done, 1)

            def scans(u, D, q):
                U = UNITS * q + u
                dve.wait_ge(mult_done, U + 1)
                if not (isinstance(U, int) and U < 4):
                    dve.wait_ge(unit_summed, U - 3)
                for n in range(GN):
                    dve.wait_ge(exp_done, GN * U + n + 1)
                    nc.vector.tensor_tensor_scan(
                        time_order(hst[:, u % 4, n, :], D), time_order(psum[:, PS_A + n, :], D),
                        time_order(dbu[:, u % 2, n, :], D), state[:, D, u * GN + n:u * GN + n + 1],
                        ALU.mult, ALU.add).then_inc(scan_done, 1)

            dve.wait_ge(zeroed, 2)
            for c in range(NC):
                conv(c, 0, 0)
            split_r1(0)
            split_lo(0)
            multiply(0, 0, 0)

            def step(i, D, q):
                for t in range(UNITS):
                    if t == 2 and not is_first(q):
                        add_skip(3, 1 - D, q - 1)
                        gate_y(3, 1 - D, q - 1)
                    if t == 4 and not is_first(q):
                        add_out(q)
                    if t in (6, 10, 14):
                        add_skip((t - 6) // 4, D, q)
                    if t in (9, 11, 15):
                        gate_y({9: 0, 11: 1, 15: 2}[t], D, q)
                    if t + 1 < UNITS:
                        multiply(t + 1, D, q)
                    elif not is_last(q):
                        multiply(0, 1 - D, q + 1)
                    scans(t, D, q)
                    if is_last(q):
                        continue
                    if 4 <= t < 8:
                        conv(t - 4, 1 - D, q + 1)
                    if t == 10:
                        split_r1(q + 1)
                    if t == 11:
                        split_lo(q + 1)

            run_steps(dve, step)
            add_skip(3, 1, STEPS - 1)
            gate_y(3, 1, STEPS - 1)
            add_out(STEPS)
            meet(dve, 2)

            nc.vector.memset(wm3[:], 0.0).then_inc(wm3_zeroed, 1)
            dve.wait_ge(f_gate_loaded, 32)

            def mod_row(n, j):
                return fmod[:, bass.ds(n // SEG, 1), j:j + 1, :].rearrange(
                    "p a b d -> p (a b) d").broadcast_to((P, NT, DM))

            def norm_statistics(n, half):
                dve.wait_ge(f_in, 32 * (n + 1))
                if not (isinstance(n, int) and n < 2):
                    dve.wait_ge(f_o, n - 1)
                nc.vector.tensor_tensor(x1[:, half], tin[:], mod_row(n, 0), ALU.mult).then_inc(f_x1, 1)
                dve.wait_ge(f_x1, 2 * n + 1)
                nc.vector.tensor_tensor(x1[:, half], x1[:, half], xin[:], ALU.add).then_inc(f_x1, 1)
                dve.wait_ge(f_x1, 2 * n + 2)
                for tt in range(NT):
                    nc.vector.bn_stats(fstats[:, tt, :], x1[:, half, tt, :]).then_inc(f_stat, 1)
                dve.wait_ge(f_stat, NT * (n + 1))
                wait_apart(dve)
                for tt in range(NT):
                    nc.vector.bn_aggr(fmv[:, tt, :], fstats[:, tt, :]).then_inc(f_aggr, 1)
                dve.wait_ge(f_aggr, NT * (n + 1))
                nc.vector.tensor_scalar(fvar[:], fmv[:, :, 1], EPS, None, ALU.add).then_inc(f_var, 1)

            def norm_apply(n, half):
                dve.wait_ge(f_rstd, n + 1)
                if not (isinstance(n, int) and n == 0):
                    for kd in range(KD):
                        g_filled(dve, n - 2, "T", kd)
                for tt in range(NT):
                    nc.vector.tensor_scalar(h2[:, tt, :], x1[:, half, tt, :], fmv[:, tt, 0:1], frstd[:, tt:tt + 1],
                                            ALU.subtract, ALU.mult).then_inc(f_norm, 1)
                dve.wait_ge(f_norm, NT * (n + 1))
                nc.vector.tensor_tensor(h2[:], h2[:], mod_row(n, 2), ALU.mult).then_inc(f_scaled, 1)

            def shift_logits(n):
                g_filled(dve, n - 1, "gate", 0)
                logits = psum[:, 0, 0:NT * NE].rearrange("p (t e) -> p t e", t=NT)
                nc.vector.tensor_reduce(fmax[:], logits, axis=AX_X, op=ALU.max).then_inc(f_route, 1)
                dve.wait_ge(f_route, ROUTE * n + 1)
                nc.vector.tensor_tensor(score[:], logits,
                                        fmax[:].rearrange("p (t a) -> p t a", a=1).broadcast_to((P, NT, NE)),
                                        ALU.subtract).then_inc(g_free[0], 1)

            def top_two(n):
                count = [ROUTE * n + 1]

                def chain(ins):
                    ins.then_inc(f_route, 1)
                    count[0] = count[0] + 1
                    dve.wait_ge(f_route, count[0])

                dve.wait_ge(f_exp, n + 1)
                chain(nc.vector.tensor_reduce(fsum[:], score[:], axis=AX_X, op=ALU.add))
                chain(nc.vector.reciprocal(fsum[:], fsum[:]))
                chain(nc.vector.tensor_tensor(
                    score[:], score[:], fsum[:].rearrange("p (t a) -> p t a", a=1).broadcast_to((P, NT, NE)),
                    ALU.mult))
                other = score[:].rearrange("p t (a e) -> p t a e", a=1).broadcast_to((P, NT, NE, NE))
                own = score[:].rearrange("p t (e a) -> p t e a", a=1).broadcast_to((P, NT, NE, NE))
                chain(nc.vector.tensor_tensor(cmp_gt[:], other, own, ALU.is_gt))
                chain(nc.vector.tensor_tensor(cmp_eq[:], other, own, ALU.is_equal))
                chain(nc.vector.tensor_tensor(
                    cmp_eq[:], cmp_eq[:],
                    lower[:].rearrange("p (a e) f -> p a e f", a=1).broadcast_to((P, NT, NE, NE)), ALU.mult))
                chain(nc.vector.tensor_tensor(cmp_gt[:], cmp_gt[:], cmp_eq[:], ALU.add))
                chain(nc.vector.tensor_reduce(rank[:], cmp_gt[:], axis=AX_X, op=ALU.add))
                chain(nc.vector.tensor_scalar(wm[:, :, NE:2 * NE], rank[:], 1.5, None, ALU.is_lt))
                nc.vector.tensor_tensor(wm[:, :, 0:NE], score[:], wm[:, :, NE:2 * NE], ALU.mult).then_inc(f_wm, 1)

            def route_r1(n, half):
                dve.wait_ge(f_whi, n + 1)
                g_filled(dve, n - 1, "wmT", 1)
                nc.vector.tensor_tensor(wm_r[:], psum[0:16, 1, :], wm3[0:16, half, :], ALU.subtract
                                        ).then_inc(g_free[1], 1)

            def route_lo(n, half):
                dve.wait_ge(f_wmid, 2 * n + 2)
                nc.vector.tensor_tensor(wm3[64:80, half, :], wm_r[:], wm_mid[:], ALU.subtract).then_inc(f_wlo, 1)

            def scale_in(e, half, i):
                g_filled(dve, i, "weight", e)
                if not (isinstance(i, int) and i == 0 and e < 2):
                    dve.wait_ge(f_x3_full, H_USES * i + 2 * e - (2 if e > 1 else 2 + NC))
                nc.vector.tensor_tensor(xs[:, e % 2], h2T[:, half], psum[:, 0:1, :].broadcast_to((P, KD, TB)),
                                        ALU.mult).then_inc(g_free[0], 1)

            def gate_x3(e, half, i):
                g_drained(dve, i, "mask", e)
                for c in range(KD):
                    dve.wait_ge(f_x3_full, H_USES * i + 2 * e + c + 1)
                    nc.vector.scalar_tensor_tensor(m3[:, e % 2, c, :], psum[:, 4 + c, :], b3[:, e, c:c + 1],
                                                   mask_wide[:, e % 2, :], ALU.add, ALU.mult).then_inc(f_m3, 1)

            def combine(e, half, i):
                dve.wait_ge(f_m3, 2 * NE * i + 2 * e + 2)
                if e > 2:
                    dve.wait_ge(f_y, (NE - 1) * i + e - 2)
                elif e > 0 and not (isinstance(i, int) and i == 0):
                    dve.wait_ge(f_y, (NE - 1) * i - (e - 1))
                if e == 0 and not (isinstance(i, int) and i < 2):
                    dve.wait_ge(f_o_full, 2 * (i - 1))
                for c in range(KD):
                    dve.wait_ge(f_x2_full, Y_USES * i + 2 * e + c + 1)
                    dst = y[:, half, c, :] if e == 0 else prod[:, e % 2, c, :]
                    nc.vector.scalar_tensor_tensor(dst, psum[:, 6 + c, :], b2[:, e, c:c + 1],
                                                   m3[:, e % 2, c, :], ALU.add, ALU.mult).then_inc(f_prod, 1)

            def shared(c, i):
                dve.wait_ge(f_h1, H_USES * i + 2 * NE + c + 1)
                dve.wait_ge(f_x3_full, H_USES * i + 2 * NE + c + 1)
                if not (isinstance(i, int) and i == 0):
                    dve.wait_ge(f_o_full, 2 * i)
                nc.vector.tensor_tensor(u_sh[:, c, :], g_silu[:, c % 2, :], psum[:, 4 + c % 2, :], ALU.mult
                                        ).then_inc(f_sh_u, 1)

            def scale_out(half, i, k):
                for b in range(2):
                    dve.wait_ge(f_o_full, 2 * i + b + 1)
                    if k is not None:
                        dve.wait_ge(f_out[half], 16 * k)
                    row = fmod[:, bass.ds(i // SEG, 1), 3:4, :].rearrange(
                        "p a b d -> p (a b) d").broadcast_to((P, 2, DM))
                    nc.vector.tensor_tensor(o_blk[:, half, 2 * b:2 * b + 2, :],
                                            psum[:, 6 + b, :].rearrange("p (t d) -> p t d", t=2), row,
                                            ALU.mult).then_inc(f_o_mul, 1)

            def body(half, i):
                ahead = not (isinstance(i, int) and i == NBLK - 1)
                scale_in(0, half, i)
                for e in range(NE):
                    if e + 1 < NE:
                        scale_in(e + 1, half, i)
                    gate_x3(e, half, i)
                    combine(e, half, i)
                    if ahead and e == 0:
                        norm_statistics(i + 1, 1 - half)
                    if ahead and e == 1:
                        norm_apply(i + 1, 1 - half)
                    if ahead and e == 4:
                        shift_logits(i + 1)
                    if ahead and e == 5:
                        top_two(i + 1)
                    if ahead and e == 6:
                        route_r1(i + 1, 1 - half)
                    if ahead and e == 7:
                        route_lo(i + 1, 1 - half)
                for c in range(NC):
                    shared(c, i)
                scale_out(half, i, None if isinstance(i, int) and i < 2 else (i - half) // 2)

            dve.wait_ge(f_const, 3)
            norm_statistics(0, 0)
            norm_apply(0, 0)
            shift_logits(0)
            top_two(0)
            route_r1(0, 0)
            route_lo(0, 0)
            dve.wait_ge(f_w_loaded, 16 * 9)
            run_blocks(dve, body)

        @block.tensor
        def _(pe):
            pe.wait_ge(c_ready, 4)
            for b in range(BATCH):
                for j in range(3):
                    for k in range(KD):
                        ins = nc.tensor.matmul(psum[:, 3 * b + j, :], c_wide[:, k, b, :],
                                               w_mod[:, k, j * TB:(j + 1) * TB], start=(k == 0), stop=(k == KD - 1))
                    ins.then_inc(mod_full, 1)
            pe.wait_ge(mod_copied, 6)
            pe.wait_ge(consts, 4)

            def transpose_xn(k):
                for half in range(2):
                    pe.wait_ge(p1_norm, NBLK * NT + k * 2 * NT + half * NT + NT)
                    if k > 0:
                        pe.wait_ge(xnT_copied, k * 4 + 2 * half - 2)
                    for kd in range(KD):
                        for tt in range(NT):
                            ins = nc.tensor.transpose(
                                psum[:, 2 * half + kd, tt * P:(tt + 1) * P],
                                X[:, (2 * k + half) * NT + tt, kd * P:(kd + 1) * P], ident[:])
                        ins.then_inc(xnT_full, 1)

            for k in range(NBLK // 2):
                transpose_xn(k)
            meet(pe, 1)

            def project_x(c, D, q):
                if c == 0:
                    n = q // 2 + 1 if isinstance(q, int) else (q - D) // 2 + 1
                    pe.wait_ge(xnT_loaded[D], 16 * n)
                bank = take_bank(pe, q - 1, "xp", c)
                for k in range(KD):
                    ins = nc.tensor.matmul(psum[:, PS_P + bank, :], w_in[:, D, k, c * P:(c + 1) * P],
                                           xnT[:, D, k, :], start=(k == 0), stop=(k == KD - 1))
                ins.then_inc(bank_full[bank], 1)

            def project_z(c, D, q):
                bank = take_bank(pe, q, "z", c)
                for k in range(KD):
                    ins = nc.tensor.matmul(psum[:, PS_P + bank, :], w_in[:, D, k, DI + c * P:DI + (c + 1) * P],
                                           xnT[:, D, k, :], start=(k == 0), stop=(k == KD - 1))
                ins.then_inc(bank_full[bank], 1)

            def project_out(D, S):
                pe.wait_ge(yg_done, NC * S)
                for b in range(2):
                    bank = take_bank(pe, S, "out", b)
                    for half in range(2):
                        tok = slice((2 * b + half) * P, (2 * b + half + 1) * P)
                        for c in range(NC):
                            ins = nc.tensor.matmul(psum[:, PS_P + bank, half * DM:(half + 1) * DM],
                                                   xc[:, D, c, tok], w_out[:, D, c, :],
                                                   start=(c == 0), stop=(c == NC - 1))
                    ins.then_inc(bank_full[bank], 1)

            def project_xdbl(D, q):
                pe.wait_ge(xc_done, NC * (q + 1))
                bank = take_bank(pe, q - 1, "xdbl", 0)
                for c in range(NC):
                    ins = nc.tensor.matmul(psum[0:48, PS_P + bank, :], w_x[:, D, c, :], xc[:, D, c, :],
                                           start=(c == 0), stop=(c == NC - 1))
                ins.then_inc(bank_full[bank], 1)

            def project_dt(c, D, q):
                pe.wait_ge(dtx_done, q + 1)
                bank = take_bank(pe, q - 1, "dt", c)
                nc.tensor.matmul(psum[:, PS_P + bank, :], w_dt[32:48, D, c * P:(c + 1) * P], dtx[32:48, :],
                                 start=True, stop=True).then_inc(bank_full[bank], 1)

            def spread_row(r, S, q):
                is_c, n = row_of(r)
                if r == 0:
                    pe.wait_ge(bc_lo, q + 1)
                bank = take_bank(pe, S, "row", r)
                m = DS * is_c + n
                nc.tensor.matmul(psum[:, PS_P + bank, :], row_pick[:, m:m + 1].broadcast_to((96, P)), bc3[:],
                                 start=True, stop=True).then_inc(bank_full[bank], 1)

            def sum_state(u, n, D, q):
                c, g = divmod(u, NG)
                U = UNITS * q + u
                if n == 0:
                    pe.wait_ge(prod_done, U + 1)
                    if g == 0 and not (isinstance(U, int) and U == 0):
                        pe.wait_ge(y_skip, NC * q + c)
                ins = nc.tensor.matmul(psum[:, PS_Y, :], ident[:], hst[:, u % 4, n, :],
                                       start=(g == 0 and n == 0), stop=(g == NG - 1 and n == GN - 1))
                if n == GN - 1:
                    ins.then_inc(unit_summed, 1)

            pe.wait_ge(w_out_done, 2)
            for c in range(NC):
                project_x(c, 0, 0)
            project_xdbl(0, 0)
            for c in range(NC):
                project_dt(c, 0, 0)
            for r in range(HEAD_ROWS):
                spread_row(r, -1, 0)

            def step(i, D, q):
                for t in range(UNITS):
                    for n in range(GN):
                        if t == 0:
                            spread_row(HEAD_ROWS + 2 * n, q, q)
                            spread_row(HEAD_ROWS + 2 * n + 1, q, q)
                        if t == 1:
                            spread_row(HEAD_ROWS + 8 + n, q, q)
                        if t == 3 and n == 0 and not is_first(q):
                            project_out(1 - D, q)
                        if t == 7 and n == 0:
                            project_z(0, D, q)
                            project_z(1, D, q)
                        if not is_last(q):
                            if t == 2 and n < 2:
                                project_x(n, 1 - D, q + 1)
                            if t in (4, 5) and n == 0:
                                project_x(t - 2, 1 - D, q + 1)
                            if (t, n) == (9, 0):
                                project_xdbl(1 - D, q + 1)
                            if (t, n) == (12, 0):
                                project_dt(2, 1 - D, q + 1)
                            if t == 13:
                                spread_row(n, q, q + 1)
                            if t in (14, 15):
                                spread_row(GN + 8 * (t - 14) + 2 * n, q, q + 1)
                                spread_row(GN + 8 * (t - 14) + 2 * n + 1, q, q + 1)
                        if t >= 2:
                            sum_state(t - 2, n, D, q)
                        elif not is_first(q):
                            sum_state(UNITS + t - 2, n, 1 - D, q - 1)
                    if t == 8:
                        project_z(2, D, q)
                        project_z(3, D, q)
                    if not is_last(q) and t in (10, 11, 12):
                        project_dt({10: 0, 11: 1, 12: 3}[t], 1 - D, q + 1)

            run_steps(pe, step)
            for u in (UNITS - 2, UNITS - 1):
                for n in range(GN):
                    sum_state(u, n, 1, STEPS - 1)
            project_out(1, STEPS)
            meet(pe, 2)

            def transpose_h2(n):
                pe.wait_ge(f_h2, n + 1)
                for kd in range(KD):
                    g_take(pe, n - 1, "T", kd)
                    for tt in range(NT):
                        ins = nc.tensor.transpose(psum[:, kd, tt * P:(tt + 1) * P],
                                                  h2[:, tt, kd * P:(kd + 1) * P], ident[:])
                    ins.then_inc(g_full[kd], 1)

            def router(n, half):
                for kd in range(KD):
                    g_drained(pe, n - 1, "T", kd)
                g_take(pe, n - 1, "gate", 0)
                for tt in range(NT):
                    for kd in range(KD):
                        ins = nc.tensor.matmul(psum[:, 0, tt * NE:(tt + 1) * NE],
                                               h2T[:, half, kd, tt * P:(tt + 1) * P], gate[:, kd, :],
                                               start=(kd == 0), stop=(kd == KD - 1))
                ins.then_inc(g_full[0], 1)

            def transpose_wm(n):
                pe.wait_ge(f_wm, n + 1)
                g_take(pe, n - 1, "wmT", 1)
                for tt in range(NT):
                    ins = nc.tensor.transpose(psum[0:16, 1, tt * P:(tt + 1) * P], wm[:, tt, :], ident[:])
                ins.then_inc(g_full[1], 1)

            def spread_weight(e, half, i):
                if e == 0:
                    pe.wait_ge(f_wlo, i + 1)
                for bank, kind in ((0, "weight"), (1, "mask")):
                    g_take(pe, i, kind, e)
                    m = NE * bank + e
                    nc.tensor.matmul(psum[:, bank, :], row_pick[:, m:m + 1].broadcast_to((96, P)),
                                     wm3[:, half, :], start=True, stop=True).then_inc(g_full[bank], 1)

            def matrix(dst, w, c, src):
                for k in range(KD):
                    ins = nc.tensor.matmul(dst, w[:, k, c * P:(c + 1) * P], src[:, k, :],
                                           start=(k == 0), stop=(k == KD - 1))
                return ins

            def body(half, i):
                ahead = not (isinstance(i, int) and i == NBLK - 1)
                spread_weight(0, half, i)
                for e in range(NE):
                    if e + 1 < NE:
                        spread_weight(e + 1, half, i)
                    g_drained(pe, i, "weight", e)
                    for c in range(KD):
                        if not (isinstance(i, int) and i == 0 and e == 0):
                            pe.wait_ge(f_h1, H_USES * i + 2 * e + c - 1)
                        matrix(psum[:, 2 + c, :], w1[:, e], c, xs[:, e % 2]).then_inc(f_h1_full, 1)
                    for c in range(KD):
                        if not (isinstance(i, int) and i == 0 and e == 0):
                            if e > 0:
                                pe.wait_ge(f_m3, 2 * NE * i + 2 * e + c - 1)
                            else:
                                pe.wait_ge(f_sh_u, NC * i + c - 1)
                        matrix(psum[:, 4 + c, :], w3[:, e], c, xs[:, e % 2]).then_inc(f_x3_full, 1)
                    pe.wait_ge(f_h1, H_USES * i + 2 * e + 2)
                    for c in range(KD):
                        if not (isinstance(i, int) and i == 0 and e == 0):
                            if e > 0:
                                pe.wait_ge(f_prod, 2 * NE * i + 2 * e + c - 1)
                            else:
                                pe.wait_ge(f_o_mul, 2 * i + c - 1)
                        matrix(psum[:, 6 + c, :], w2[:, e], c, h1[:, e % 2]).then_inc(f_x2_full, 1)
                    if ahead and e == 2:
                        transpose_h2(i + 1)
                    if ahead and e == 4:
                        router(i + 1, 1 - half)
                    if ahead and e == 6:
                        transpose_wm(i + 1)
                for c in range(NC):
                    pe.wait_ge(f_h1, H_USES * i + 2 * NE + c - 1)
                    matrix(psum[:, 2 + c % 2, :], sw1[:], c, h2T[:, half]).then_inc(f_h1_full, 1)
                    if c < 2:
                        pe.wait_ge(f_m3, 2 * NE * (i + 1) + c - 1)
                    else:
                        pe.wait_ge(f_sh_u, NC * i + c - 1)
                    matrix(psum[:, 4 + c % 2, :], sw2[:], c, h2T[:, half]).then_inc(f_x3_full, 1)
                pe.wait_ge(f_sh_u, NC * (i + 1))
                pe.wait_ge(f_y, (NE - 1) * (i + 1))
                for b in range(2):
                    pe.wait_ge(f_prod, 2 * NE * (i + 1) + b - 1)
                    for tt in (2 * b, 2 * b + 1):
                        tok = slice(tt * P, (tt + 1) * P)
                        cols = psum[:, 6 + b, (tt % 2) * DM:(tt % 2 + 1) * DM]
                        for c in range(NC):
                            nc.tensor.matmul(cols, u_sh[:, c, tok], sw3[:, c, :], start=(c == 0), stop=False)
                        for k in range(KD):
                            ins = nc.tensor.matmul(cols[:, k * P:(k + 1) * P], y[:, half, k, tok], ident[:],
                                                   start=False, stop=(k == KD - 1))
                    ins.then_inc(f_o_full, 1)

            pe.wait_ge(f_gate_loaded, 32)
            transpose_h2(0)
            router(0, 0)
            transpose_wm(0)
            pe.wait_ge(f_w_loaded, 16 * 9)
            run_blocks(pe, body)


def on_partitions(w):
    return w.reshape(w.shape[0] // P, P, *w.shape[1:]).swapaxes(0, 1)


def lay_out(inputs):
    import numpy as np
    a = {k.replace("L0_", ""): np.asarray(v) for k, v in inputs.items()}
    both = lambda name: (a["attn_f_" + name], a["attn_b_" + name])
    stack = lambda parts: np.stack(parts, axis=1)
    out = {
        "x": a["attn_x"].reshape(NBLK, NT, P, DM).transpose(0, 2, 1, 3).reshape(NBLK, P, NT * DM),
        "cT": on_partitions(a["c"].T),
        "w_mod": on_partitions(a["wmod"]),
        "ln_w": on_partitions(a["attn_ln_w"]),
        "ln_b": on_partitions(a["attn_ln_b"]),
        "w_in": stack([on_partitions(w.T) for w in both("W_in")]),
        "w_x": stack([on_partitions(np.concatenate([w[DR:], w[:DR]]).T) for w in both("W_x")]),
        "w_dt": stack([w.T for w in both("W_dt")]),
        "w_out": stack([on_partitions(w.T) for w in both("W_out")]),
        "a_log": stack([on_partitions(w) for w in both("A_log")]),
        "w_conv": stack([on_partitions(w) for w in both("W_conv")]),
        "b_conv": stack([on_partitions(w) for w in both("b_conv")]),
        "b_dt": stack([on_partitions(w) for w in both("b_dt")]),
        "d_skip": stack([on_partitions(w) for w in both("D")]),
        "gate": on_partitions(a["ffn_gate_w"].T),
        "sw1": on_partitions(a["ffn_sw1"].T),
        "sw2": on_partitions(a["ffn_sw2"].T),
        "sw3": on_partitions(a["ffn_sw3"].T),
    }
    for n in "123":
        out["w" + n] = stack([on_partitions(w.T) for w in a["ffn_w" + n]])
        out["b" + n] = stack([on_partitions(b) for b in a["ffn_b" + n]])
    return {k: np.ascontiguousarray(v) for k, v in out.items()}


def kernel(**inputs):
    import numpy as np
    import concourse.bacc as bacc
    from concourse.bass_utils import run_bass_kernel_spmd

    nc = bacc.Bacc("TRN2", target_bir_lowering=False, num_devices=1)
    arrays = lay_out(inputs)
    aps = {name: nc.dram_tensor(f"in_{name}", v.shape, mybir.dt.from_np(v.dtype), kind="ExternalInput").ap()
           for name, v in arrays.items()}
    out = nc.dram_tensor("out_x", (NBLK, P, NT * DM), F32, kind="ExternalOutput").ap()
    mixer_and_experts(nc, aps, out)
    r = run_bass_kernel_spmd(nc, [{f"in_{k}": v for k, v in arrays.items()}], core_ids=[0])
    y = np.asarray(r.results[0]["out_x"])
    return y.reshape(NBLK, P, NT, DM).transpose(0, 2, 1, 3).reshape(BATCH, SEQ, DM)
```

```python
from contextlib import ExitStack

import concourse.bass as bass
from concourse import mybir

ALU = mybir.AluOpType
ACT = mybir.ActivationFunctionType
AX_X = mybir.AxisListType.X
F32 = mybir.dt.float32
BF16 = mybir.dt.bfloat16

P = 128
BATCH, SEQ, DM = 2, 2048, 256
DI = 2 * DM
DS = 16
DR = DM // 16
TAPS = 4
HALO = TAPS - 1
TB = 512
NBLK = BATCH * SEQ // TB
SEG = SEQ // TB
NT = TB // P
KD = DM // P
NC = DI // P
GN = 4
NG = DS // GN
UNITS = NC * NG
STEPS = 2 * NBLK
NE = 8
BIG = 3.4e38
EPS = 1e-5
ROWS = 2 * DS


G_USES = (
    [("weight", e) for e in range(4)] + [("T", 0), ("weight", 4), ("weight", 5), ("gate", 0), ("weight", 6), ("weight", 7)],
    [("mask", e) for e in range(4)] + [("T", 1)] + [("mask", e) for e in (4, 5, 6, 7)] + [("wmT", 1)])
G_FIRST = ([("T", 0), ("gate", 0)], [("T", 1), ("wmT", 1)])
H_USES = 2 * NE + NC
Y_USES = 2 * NE
ROUTE = 10

STEP_USES = (
    [("out", 0, 0), ("out", 1, 1), ("xp", 0, 0), ("xp", 1, 1), ("xp", 2, 0), ("xp", 3, 1)]
    + [("z", 0, 0), ("z", 1, 1)]
    + [("xdbl", 0, 0), ("dt", 0, 1), ("dt", 1, 0), ("dt", 2, 1), ("dt", 3, 0), ("z", 2, 1), ("z", 3, 0)])
XP_AT = [(5, 0), (5, 2), (7, 1), (8, 0)]
DT_AT = [(12, 0), (12, 2), (13, 0), (13, 2)]
FIRST_USES = [u for u in STEP_USES if u[0] in ("xp", "xdbl", "dt")]


def uses_of_step(step):
    if step == -1:
        return FIRST_USES
    if step == STEPS:
        return [u for u in STEP_USES if u[0] == "out"]
    own = [u for u in STEP_USES if u[0] in ("out", "z")]
    uses = own if step == STEPS - 1 else STEP_USES
    return [u for u in uses if u[0] != "out"] if step == 0 else uses


def bank_use(step, kind, index):
    bank = [u[2] for u in STEP_USES if u[:2] == (kind, index)][0]
    of_bank = lambda uses: [u[:2] for u in uses if u[2] == bank]
    if isinstance(step, int):
        return bank, (sum(len(of_bank(uses_of_step(k))) for k in range(-1, step))
                      + of_bank(uses_of_step(step)).index((kind, index)))
    mine = of_bank(STEP_USES)
    return bank, len(of_bank(FIRST_USES)) - 1 + len(mine) * step + mine.index((kind, index))


def mixer_and_experts(nc, A, out):
    with ExitStack() as top:
        sem = lambda name: top.enter_context(nc.semaphore(name))
        dram = lambda name, shape: nc.dram_tensor(name, shape, F32, kind="Internal").ap()

        xnT_dram = dram("xnT_scratch", (NBLK, P, KD * TB))
        t_dram = dram("t_scratch", (NBLK, P, NT * DM))
        bc_dram = dram("bc_scratch", (2, 1, ROWS * TB))
        mod_dram = dram("mod_scratch", (P, BATCH * 4 * DM))

        psum = top.enter_context(nc.psum_tensor("psum", [P, 8, TB], F32))
        keep = lambda name, shape, dt=F32: top.enter_context(nc.sbuf_tensor(name, shape, dt))
        ident = keep("ident", [P, P])
        row_pick = keep("row_pick", [96, 32], BF16)
        row_pick32 = keep("row_pick32", [96, 32])

        mix = ExitStack()
        sb2 = lambda name, shape, dt=F32: mix.enter_context(nc.sbuf_tensor(name, shape, dt))
        w_in = sb2("w_in", [P, 2, KD, 2 * DI])
        w_x = sb2("w_x", [P, 2, NC, 48])
        w_dt = sb2("w_dt", [48, 2, DI])
        w_out = sb2("w_out", [P, 2, NC, DM])
        neg_a = sb2("neg_a", [P, 2, NC, DS])
        w_conv = sb2("w_conv", [P, 2, NC, TAPS])
        b_conv = sb2("b_conv", [P, 2, NC])
        b_dt = sb2("b_dt", [P, 2, NC])
        d_skip = sb2("d_skip", [P, 2, NC])
        limits = sb2("limits", [P, NBLK, 2])

        pre = ExitStack()
        sb1 = lambda name, shape, dt=F32: pre.enter_context(nc.sbuf_tensor(name, shape, dt))
        cT = sb1("cT", [P, KD, BATCH])
        c_wide = sb1("c_wide", [P, KD, BATCH, P])
        w_mod = sb1("w_mod", [P, KD, 6 * DM])
        mod = sb1("mod", [P, BATCH, 6, DM])
        mod_abs = sb1("mod_abs", [P, BATCH, DM])
        mod_sign = sb1("mod_sign", [P, BATCH, DM])
        ln_w = sb1("ln_w", [P, KD])
        ln_b = sb1("ln_b", [P, KD])
        X = sb1("X", [P, NBLK * NT, DM])
        H = sb1("H", [P, NBLK * NT, DM])
        stats = sb1("stats", [P, NBLK * NT, 6])
        mv = sb1("mv", [P, 2, NBLK * NT, 2])
        var_eps = sb1("var_eps", [P, 2, NBLK * NT])
        rstd = sb1("rstd", [P, 2, NBLK * NT])
        minus_half = sb1("minus_half", [P, SEG * NT])
        xnT_out = sb1("xnT_out", [P, 2, KD, TB])
        pre.close()

        xnT = sb2("xnT", [P, 2, KD, TB])
        xc = sb2("xc", [P, 2, NC, TB])
        dt = sb2("dt", [P, 2, NC, TB])
        sp_tmp = sb2("sp_tmp", [P, NC, TB])
        t_blk = sp_tmp[:, 0:2, :].rearrange("p a b -> p (a b)")
        xp = sb2("xp", [P, 2, TB + HALO])
        halo = sb2("halo", [P, 2, NC, HALO])
        limit_now = sb2("limit_now", [P, 2, 2])
        sz = sb2("sz", [P, NC, TB])
        b_wide = sb2("b_wide", [P, 2, DS, TB])
        dbu = sb2("dbu", [P, 2, GN, TB])
        hst = sb2("hst", [P, 4, GN, TB])
        state = sb2("state", [P, 2, UNITS * GN])
        x_dbl = sb2("x_dbl", [48, TB])
        mix.close()
        PS_A, PS_U, PS_Y, PS_P = 0, 4, 5, 6

        ffn = ExitStack()
        sb3 = lambda name, shape, dt_=F32: ffn.enter_context(nc.sbuf_tensor(name, shape, dt_))
        w1 = sb3("w1", [P, NE, KD, DM])
        w2 = sb3("w2", [P, NE, KD, DM])
        w3 = sb3("w3", [P, NE, KD, DM])
        b1 = sb3("b1", [P, NE, KD])
        b2 = sb3("b2", [P, NE, KD])
        b3 = sb3("b3", [P, NE, KD])
        sw1 = sb3("sw1", [P, KD, 2 * DM])
        sw2 = sb3("sw2", [P, KD, 2 * DM])
        sw3 = sb3("sw3", [P, NC, DM])
        gate = sb3("gate", [P, KD, NE])
        fmod = sb3("fmod", [P, BATCH, 4, DM])
        lower = sb3("lower", [P, NE, NE])
        minus_half3 = sb3("minus_half3", [P, NT])
        xin = sb3("xin", [P, NT, DM])
        tin = sb3("tin", [P, NT, DM])
        x1 = sb3("x1", [P, 2, NT, DM])
        h2 = sb3("h2", [P, NT, DM])
        h2T = sb3("h2T", [P, 2, KD, TB])
        fstats = sb3("fstats", [P, NT, 6])
        fmv = sb3("fmv", [P, NT, 2])
        fvar = sb3("fvar", [P, NT])
        frstd = sb3("frstd", [P, NT])
        fmax = sb3("fmax", [P, NT])
        fsum = sb3("fsum", [P, NT])
        score = sb3("score", [P, NT, NE])
        cmp_gt = sb3("cmp_gt", [P, NT, NE, NE])
        cmp_eq = sb3("cmp_eq", [P, NT, NE, NE])
        rank = sb3("rank", [P, NT, NE])
        wm = sb3("wm", [P, NT, 2 * NE])
        wm_r = sb3("wm_r", [16, TB])
        wm_mid = sb3("wm_mid", [16, TB], BF16)
        wm3 = sb3("wm3", [96, 2, TB], BF16)
        mask_wide = sb3("mask_wide", [P, 2, TB])
        xs = sb3("xs", [P, 2, KD, TB])
        h1 = sb3("h1", [P, 2, KD, TB])
        m3 = sb3("m3", [P, 2, KD, TB])
        prod = sb3("prod", [P, 2, KD, TB])
        y = sb3("y", [P, 2, KD, TB])
        g_silu = sb3("g_silu", [P, 2, TB])
        u_sh = sb3("u_sh", [P, NC, TB])
        o_blk = sb3("o_blk", [P, 2, NT, DM])
        ffn.close()

        phase = sem("phase")
        waited = sem("waited")
        w_loaded = sem("w_loaded")
        x_loaded = [sem("x_loaded0"), sem("x_loaded1")]
        w_mod_loaded = sem("w_mod_loaded")
        consts = sem("consts")
        neg_a_done = sem("neg_a_done")
        w_out_done = sem("w_out_done")
        c_ready = sem("c_ready")
        mod_full = sem("mod_full")
        mod_copied = sem("mod_copied")
        mod_step = sem("mod_step")
        mod_stored = sem("mod_stored")
        p1_stat = sem("p1_stat")
        p1_aggr = sem("p1_aggr")
        p1_var = sem("p1_var")
        p1_rstd = sem("p1_rstd")
        p1_norm = sem("p1_norm")
        p1_scaled = sem("p1_scaled")
        h_done = sem("h_done")
        h_stored = sem("h_stored")
        xn_done = sem("xn_done")
        xnT_full = sem("xnT_full")
        xnT_copied = sem("xnT_copied")
        xnT_stored = [sem("xnT_stored0"), sem("xnT_stored1")]
        xnT_loaded = [sem("xnT_loaded0"), sem("xnT_loaded1")]
        bank_full = [sem("bank_full0"), sem("bank_full1")]
        bank_free = [sem("bank_free0"), sem("bank_free1")]
        xp_head = sem("xp_head")
        xp_body = sem("xp_body")
        halo_saved = sem("halo_saved")
        conv_step = sem("conv_step")
        conv_done = sem("conv_done")
        xc_done = sem("xc_done")
        bc_stored = sem("bc_stored")
        rows_loaded = [[sem(f"rows_loaded{k}{g}") for g in range(NG)] for k in range(2)]
        sp_relu = sem("sp_relu")
        sp_exp = sem("sp_exp")
        sp_done = sem("sp_done")
        dt_done = sem("dt_done")
        dtu_done = sem("dtu_done")
        exp_done = sem("exp_done")
        mult_done = sem("mult_done")
        scan_done = sem("scan_done")
        limit_set = sem("limit_set")
        prod_done = sem("prod_done")
        state_saved = sem("state_saved")
        unit_summed = sem("unit_summed")
        y_skip = sem("y_skip")
        yg_done = sem("yg_done")
        t_loaded = sem("t_loaded")
        t_stored = sem("t_stored")
        zeroed = sem("zeroed")
        f_gate_loaded = sem("f_gate_loaded")
        f_w_loaded = sem("f_w_loaded")
        f_const = sem("f_const")
        wm3_zeroed = sem("wm3_zeroed")
        f_in = sem("f_in")
        f_x1 = sem("f_x1")
        f_stat = sem("f_stat")
        f_aggr = sem("f_aggr")
        f_var = sem("f_var")
        f_rstd = sem("f_rstd")
        f_norm = sem("f_norm")
        f_scaled = sem("f_scaled")
        f_h2 = sem("f_h2")
        f_route = sem("f_route")
        f_exp = sem("f_exp")
        f_wm = sem("f_wm")
        f_whi = sem("f_whi")
        f_wmid = sem("f_wmid")
        f_wlo = sem("f_wlo")
        f_h2T = sem("f_h2T")
        g_full = [sem("g_full0"), sem("g_full1")]
        g_free = [sem("g_free0"), sem("g_free1")]
        f_mask = sem("f_mask")
        f_xs = sem("f_xs")
        f_h1_full = sem("f_h1_full")
        f_h1 = sem("f_h1")
        f_x3_full = sem("f_x3_full")
        f_m3 = sem("f_m3")
        f_x2_full = sem("f_x2_full")
        f_prod = sem("f_prod")
        f_y = sem("f_y")
        f_sh_u = sem("f_sh_u")
        f_o_full = sem("f_o_full")
        f_o_mul = sem("f_o_mul")
        f_o = sem("f_o")
        f_out = [sem("f_out0"), sem("f_out1")]

        block = top.enter_context(nc.Block())

        def meet(eng, n):
            eng.drain().then_inc(phase, 1)
            eng.wait_ge(phase, 5 * n)

        def time_order(ap, backward):
            return ap[:, ::-1] if backward else ap

        def wait_apart(eng):
            eng.sem_inc(waited, 1)

        def filled(eng, S, kind, index):
            bank, before = bank_use(S, kind, index)
            eng.wait_ge(bank_full[bank], before + 1)
            return PS_P + bank

        def drained(eng, S, kind, index):
            bank, before = bank_use(S, kind, index)
            eng.wait_ge(bank_free[bank], before + 1)

        def rows_ready(eng, is_c, g, q):
            eng.wait_ge(rows_loaded[is_c][g], 16 * (q + 1))

        def take_bank(pe, S, kind, index):
            bank, before = bank_use(S, kind, index)
            if not (isinstance(before, int) and before == 0):
                pe.wait_ge(bank_free[bank], before)
            return bank

        def run_steps(eng, step):
            step(0, 0, 0)
            step(0, 1, 1)
            with eng.Fori(1, NBLK - 1) as i:
                step(i, 0, 2 * i)
                step(i, 1, 2 * i + 1)
            step(NBLK - 1, 0, STEPS - 2)
            step(NBLK - 1, 1, STEPS - 1)

        def is_first(q):
            return isinstance(q, int) and q == 0

        def is_last(q):
            return isinstance(q, int) and q == STEPS - 1

        def run_blocks(eng, body):
            body(0, 0)
            body(1, 1)
            with eng.Fori(1, NBLK // 2 - 1) as k:
                for half in range(2):
                    body(half, 2 * k + half)
            body(0, NBLK - 2)
            body(1, NBLK - 1)

        def g_count(i, kind, index, bank):
            if isinstance(i, int) and i == -1:
                return G_FIRST[bank].index((kind, index))
            uses = G_USES[bank]
            if isinstance(i, int) and i == NBLK - 1:
                uses = [u for u in uses if u not in G_FIRST[bank]]
            return len(G_FIRST[bank]) + len(G_USES[bank]) * i + uses.index((kind, index))

        def g_bank(kind, index):
            return {"T": index, "gate": 0, "weight": 0, "mask": 1, "wmT": 1}[kind]

        def g_filled(eng, i, kind, index):
            bank = g_bank(kind, index)
            eng.wait_ge(g_full[bank], g_count(i, kind, index, bank) + 1)

        def g_drained(eng, i, kind, index):
            bank = g_bank(kind, index)
            eng.wait_ge(g_free[bank], g_count(i, kind, index, bank) + 1)

        def g_take(pe, i, kind, index):
            bank = g_bank(kind, index)
            before = g_count(i, kind, index, bank)
            if not (isinstance(before, int) and before == 0):
                pe.wait_ge(g_free[bank], before)

        @block.sync
        def _(sp):
            for b in range(BATCH):
                sp.dma_start(X[:, b * SEG * NT:(b + 1) * SEG * NT, :].rearrange("p (k t) d -> p k (t d)", t=NT),
                             A["x"][b * SEG:(b + 1) * SEG].rearrange("k p n -> p k n")).then_inc(x_loaded[b], 16)
                if b == 0:
                    sp.dma_start(w_mod[:], A["w_mod"]).then_inc(w_mod_loaded, 16)
                    sp.dma_start(cT[:], A["cT"]).then_inc(w_mod_loaded, 16)
                    sp.dma_start(ln_w[:], A["ln_w"]).then_inc(w_mod_loaded, 16)
                    sp.dma_start(ln_b[:], A["ln_b"]).then_inc(w_mod_loaded, 16)
            for dst, name in ((neg_a, "a_log"), (w_in, "w_in"), (w_x, "w_x"), (w_out, "w_out"),
                              (w_conv, "w_conv"), (b_conv, "b_conv"), (b_dt, "b_dt"), (d_skip, "d_skip")):
                sp.dma_start(dst[:], A[name]).then_inc(w_loaded, 16)
            sp.dma_start(w_dt[32:48], A["w_dt"]).then_inc(w_loaded, 16)
            sp.wait_ge(mod_step, 10)
            sp.dma_start(mod_dram, mod[:, :, 2:6, :]).then_inc(mod_stored, 16)
            with sp.Fori(0, NBLK) as k:
                sp.wait_ge(h_done, k + 1)
                sp.dma_start(t_dram[bass.ds(k, 1)].rearrange("k p n -> (k p) n"),
                             H[:, bass.ds(k * NT, NT), :].rearrange("p t d -> p (t d)")).then_inc(h_stored, 16)
            with sp.Fori(0, NBLK // 2) as k:
                for half in range(2):
                    sp.wait_ge(xnT_copied, k * 4 + 2 * half + 2)
                    sp.dma_start(xnT_dram[bass.ds(2 * k + half, 1)].rearrange("k p n -> (k p) n"),
                                 xnT_out[:, half].rearrange("p k t -> p (k t)")).then_inc(xnT_stored[half], 16)
            sp.wait_ge(h_stored, 16 * NBLK)
            sp.wait_ge(mod_stored, 16)
            sp.wait_ge(w_loaded, 16 * 9)
            for half in range(2):
                sp.wait_ge(xnT_stored[half], 16 * NBLK // 2)
            meet(sp, 1)

            def block_of(i, D):
                if D == 0:
                    return i
                return (i // SEG) * SEG + (SEG - 1 - i % SEG)

            def load_xnT(i, D):
                wait_apart(sp)
                sp.dma_start(xnT[:, D].rearrange("p k t -> p (k t)"),
                             xnT_dram[bass.ds(block_of(i, D), 1)].rearrange("k p n -> (k p) n")
                             ).then_inc(xnT_loaded[D], 16)

            def store_rows(q, D):
                drained(sp, q - 1, "xdbl", 0)
                sp.dma_start(bc_dram[D].rearrange("a (r t) -> (a r) t", r=ROWS), x_dbl[0:ROWS, :]
                             ).then_inc(bc_stored, 16)

            def spread_rows(is_c, g, q, D):
                if g == 0 and not is_c:
                    sp.wait_ge(bc_stored, 16 * (q + 1))
                    wait_apart(sp)
                if not is_first(q):
                    sp.wait_ge(prod_done if is_c else mult_done, UNITS * (q - 1) + UNITS - NG + g + 1)
                at = (DS * is_c + GN * g) * TB
                sp.dma_start(b_wide[:, is_c, g * GN:(g + 1) * GN, :].rearrange("p n t -> p (n t)"),
                             bc_dram[D, :, at:at + GN * TB].broadcast_to((P, GN * TB))
                             ).then_inc(rows_loaded[is_c][g], 16)

            def spread_first_rows(q, D):
                store_rows(q, D)
                for is_c, g in ((0, 0), (0, 1), (0, 2), (1, 0), (0, 3), (1, 1)):
                    spread_rows(is_c, g, q, D)

            def load_sum(i, D, q):
                if not is_first(q):
                    sp.wait_ge(t_stored, 16 * q)
                    wait_apart(sp)
                sp.wait_ge(dt_done, NC * (q + 1) + (0 if is_last(q) else 2))
                wait_apart(sp)
                sp.dma_start(t_blk, t_dram[bass.ds(block_of(i, D), 1)].rearrange("k p n -> (k p) n")
                             ).then_inc(t_loaded, 16)

            def store_sum(i, D, q):
                drained(sp, q + 1, "out", 1)
                wait_apart(sp)
                sp.dma_start(t_dram[bass.ds(block_of(i, D), 1)].rearrange("k p n -> (k p) n"), t_blk
                             ).then_inc(t_stored, 16)

            load_xnT(0, 0)
            load_xnT(0, 1)
            spread_first_rows(0, 0)

            def step(i, D, q):
                before = (i if D else i - 1, 1 - D, q - 1)
                if not is_first(q):
                    load_sum(*before)
                for g in (2, 3):
                    spread_rows(1, g, q, D)
                if not is_first(q):
                    store_sum(*before)
                if not is_last(q):
                    spread_first_rows(q + 1, 1 - D)
                if not (isinstance(q, int) and q + 2 >= STEPS):
                    filled(sp, q, "z", 3)
                    load_xnT(i + 1, D)

            run_steps(sp, step)
            load_sum(NBLK - 1, 1, STEPS - 1)
            store_sum(NBLK - 1, 1, STEPS - 1)
            sp.wait_ge(t_stored, 16 * STEPS)
            meet(sp, 2)

            for dst, name in ((gate, "gate"), (fmod, None)):
                sp.dma_start(dst[:], mod_dram if name is None else A[name]).then_inc(f_gate_loaded, 16)

            def load_block(i):
                wait_apart(sp)
                sp.dma_start(xin[:].rearrange("p t d -> p (t d)"),
                             A["x"][bass.ds(i, 1)].rearrange("k p n -> (k p) n")).then_inc(f_in, 16)
                sp.dma_start(tin[:].rearrange("p t d -> p (t d)"),
                             t_dram[bass.ds(i, 1)].rearrange("k p n -> (k p) n")).then_inc(f_in, 16)

            load_block(0)
            for dst, name in ((w1, "w1"), (w3, "w3"), (w2, "w2"), (b1, "b1"), (b2, "b2"), (b3, "b3"),
                              (sw1, "sw1"), (sw2, "sw2"), (sw3, "sw3")):
                sp.dma_start(dst[:], A[name]).then_inc(f_w_loaded, 16)

            def store_block(i, half):
                sp.wait_ge(f_o, i + 1)
                wait_apart(sp)
                sp.dma_start(out[bass.ds(i, 1)].rearrange("k p n -> (k p) n"),
                             o_blk[:, half].rearrange("p t d -> p (t d)")).then_inc(f_out[half], 16)

            sp.wait_ge(f_x1, 2)
            load_block(1)
            with sp.Fori(0, NBLK // 2 - 1) as k:
                for half in range(2):
                    sp.wait_ge(f_x1, k * 4 + 2 * half + 4)
                    load_block(2 * k + half + 2)
                    store_block(2 * k + half, half)
            store_block(NBLK - 2, 0)
            store_block(NBLK - 1, 1)
            for half in range(2):
                sp.wait_ge(f_out[half], 16 * NBLK // 2)

        @block.gpsimd
        def _(pool):
            nc.gpsimd.memset(ident[:], 0.0).then_inc(consts, 1)
            nc.gpsimd.memset(row_pick32[:], 0.0).then_inc(consts, 1)
            nc.gpsimd.memset(minus_half[:], -0.5).then_inc(consts, 1)
            pool.wait_ge(consts, 3)
            nc.gpsimd.affine_select(out=ident[:], in_=ident[:], compare_op=ALU.not_equal, fill=1.0,
                                    base=0, pattern=[[-1, P]], channel_multiplier=1).then_inc(consts, 1)
            for part in range(3):
                nc.gpsimd.affine_select(out=row_pick32[:], in_=row_pick32[:], compare_op=ALU.not_equal,
                                        fill=1.0, base=-32 * part, pattern=[[-1, 32]],
                                        channel_multiplier=1).then_inc(consts, 1)
                pool.wait_ge(consts, 5 + part)
            nc.gpsimd.tensor_copy(row_pick[:], row_pick32[:]).then_inc(consts, 1)
            for k in range(NBLK):
                bound = 0.0 if k % SEG == SEG - 1 else BIG
                nc.gpsimd.memset(limits[:, k, 0:1], bound).then_inc(consts, 1)
                nc.gpsimd.memset(limits[:, k, 1:2], -bound).then_inc(consts, 1)
            pool.wait_ge(consts, 8 + 2 * NBLK)

            span = SEG * NT
            for ln in range(2):
                for b in range(BATCH):
                    n = ln * BATCH + b
                    pool.wait_ge(p1_var, n + 1)
                    nc.gpsimd.tensor_tensor(rstd[:, ln, b * span:(b + 1) * span],
                                            var_eps[:, ln, b * span:(b + 1) * span], minus_half[:],
                                            ALU.pow).then_inc(p1_rstd, 1)
                if ln == 0:
                    for b in range(BATCH):
                        with pool.Fori(0, SEG) as s:
                            pool.wait_ge(p1_scaled, s + (b * SEG + 1))
                            Hb = H[:, bass.ds(s * NT + b * span, NT), :]
                            nc.gpsimd.tensor_tensor(Hb, Hb, mod[:, b, 0:1, :].broadcast_to((P, NT, DM)),
                                                    ALU.add).then_inc(h_done, 1)
            meet(pool, 1)

            nc.gpsimd.memset(state[:], 0.0).then_inc(zeroed, 1)
            nc.gpsimd.memset(halo[:], 0.0).then_inc(zeroed, 1)

            def set_limit(i, D):
                nc.gpsimd.tensor_copy(limit_now[:, D:D + 1, :], limits[:, bass.ds(i, 1), :]).then_inc(limit_set, 1)

            def clamp(dst, src, D, signal):
                nc.gpsimd.tensor_scalar(dst, src, limit_now[:, D, 0:1], limit_now[:, D, 1:2],
                                        ALU.min, ALU.max).then_inc(signal, 1)

            def save_halo(c, D, q):
                pool.wait_ge(limit_set, q + 1)
                drained(pool, q - 1, "xp", c)
                wait_apart(pool)
                edge = slice(TB, TB + HALO) if D == 0 else slice(0, HALO)
                clamp(halo[:, D, c, :], xp[:, c % 2, edge], D, halo_saved)

            def add_dt(c, D, q):
                pool.wait_ge(sp_done, q + 1)
                nc.gpsimd.tensor_tensor(dt[:, D, c, :], dt[:, D, c, :], sp_tmp[:, c, :],
                                        ALU.add).then_inc(dt_done, 1)

            def unit(u, D, q):
                g = u % NG
                U = UNITS * q + u
                last = TB - 1 if D == 0 else 0
                h = hst[:, u % 4, :, :]
                pool.wait_ge(scan_done, GN * U + GN)
                wait_apart(pool)
                clamp(state[:, D, u * GN:(u + 1) * GN].rearrange("p (a b) -> p a b", b=1),
                      h[:, :, last:last + 1], D, state_saved)
                rows_ready(pool, 1, g, q)
                pool.wait_ge(state_saved, U + 1)
                nc.gpsimd.tensor_tensor(h, h, b_wide[:, 1, g * GN:(g + 1) * GN, :],
                                        ALU.mult).then_inc(prod_done, 1)

            set_limit(0, 0)
            pool.wait_ge(zeroed, 2)
            for c in range(NC):
                save_halo(c, 0, 0)
            for c in range(NC):
                add_dt(c, 0, 0)

            def step(i, D, q):
                for t in range(UNITS):
                    ahead = not is_last(q)
                    if ahead and t == 2:
                        set_limit(i + D, 1 - D)
                    if ahead and t in (6, 7, 8, 9):
                        save_halo(t - 6, 1 - D, q + 1)
                    if t in (0, 1) and not is_first(q):
                        add_dt(2 + t, D, q)
                    if t > 0:
                        unit(t - 1, D, q)
                    elif not is_first(q):
                        unit(UNITS - 1, 1 - D, q - 1)
                    if ahead and t in (14, 15):
                        add_dt(t - 14, 1 - D, q + 1)

            run_steps(pool, step)
            unit(UNITS - 1, 1, STEPS - 1)
            meet(pool, 2)

            nc.gpsimd.memset(minus_half3[:], -0.5).then_inc(f_const, 1)
            nc.gpsimd.memset(lower[:], 1.0).then_inc(f_const, 1)
            pool.wait_ge(f_const, 2)
            nc.gpsimd.affine_select(out=lower[:], in_=lower[:], compare_op=ALU.is_gt, fill=0.0, base=0,
                                    pattern=[[1, NE], [-1, NE]], channel_multiplier=0).then_inc(f_const, 1)
            pool.wait_ge(f_gate_loaded, 32)

            def mod_row(n, j):
                return fmod[:, bass.ds(n // SEG, 1), j:j + 1, :].rearrange(
                    "p a b d -> p (a b) d").broadcast_to((P, NT, DM))

            def norm_power(n):
                pool.wait_ge(f_var, n + 1)
                nc.gpsimd.tensor_tensor(frstd[:], fvar[:], minus_half3[:], ALU.pow).then_inc(f_rstd, 1)

            def norm_shift(n):
                pool.wait_ge(f_scaled, n + 1)
                nc.gpsimd.tensor_tensor(h2[:], h2[:], mod_row(n, 1), ALU.add).then_inc(f_h2, 1)

            def add_expert(e, half, i):
                pool.wait_ge(f_prod, 2 * NE * i + 2 * e + 2)
                if e > 1:
                    pool.wait_ge(f_y, (NE - 1) * i + e - 1)
                nc.gpsimd.tensor_tensor(y[:, half], y[:, half], prod[:, e % 2], ALU.add).then_inc(f_y, 1)

            def add_residual(half, i):
                pool.wait_ge(f_o_mul, 2 * i + 2)
                nc.gpsimd.tensor_tensor(o_blk[:, half], o_blk[:, half], x1[:, half], ALU.add).then_inc(f_o, 1)

            def body(half, i):
                ahead = not (isinstance(i, int) and i == NBLK - 1)
                for e in range(1, NE):
                    if ahead and e == 1:
                        norm_power(i + 1)
                    add_expert(e, half, i)
                    if ahead and e == 2:
                        norm_shift(i + 1)
                add_residual(half, i)

            norm_power(0)
            norm_shift(0)
            run_blocks(pool, body)

        @block.scalar
        def _(act):
            act.wait_ge(w_mod_loaded, 16 * 4)
            for k in range(KD):
                for b in range(BATCH):
                    nc.scalar.activation(c_wide[:, k, b, :], cT[:, k, b:b + 1].broadcast_to((P, P)),
                                         ACT.Silu).then_inc(c_ready, 1)
            for b in range(BATCH):
                for j in range(3):
                    act.wait_ge(mod_full, 3 * b + j + 1)
                    nc.scalar.activation(mod[:, b, 2 * j:2 * j + 2, :].rearrange("p a d -> p (a d)"),
                                         psum[:, 3 * b + j, :], ACT.Copy).then_inc(mod_copied, 1)
            act.wait_ge(w_loaded, 16 * 9)
            nc.scalar.activation(neg_a[:], neg_a[:], ACT.Exp).then_inc(neg_a_done, 1)

            def copy_xnT(k):
                for half in range(2):
                    for kd in range(KD):
                        act.wait_ge(xnT_full, k * 4 + 2 * half + kd + 1)
                        if not isinstance(k, int):
                            act.wait_ge(xnT_stored[half], 16 * k)
                        nc.scalar.activation(xnT_out[:, half, kd, :], psum[:, 2 * half + kd, :], ACT.Identity,
                                             scale=ln_w[:, kd:kd + 1], bias=ln_b[:, kd:kd + 1]
                                             ).then_inc(xnT_copied, 1)

            copy_xnT(0)
            with act.Fori(1, NBLK // 2) as k:
                copy_xnT(k)
            meet(act, 1)

            def copy_xp(c, D, q):
                if not (isinstance(q, int) and q == 0 and c < 2):
                    act.wait_ge(conv_done, NC * q + c - 1)
                    act.wait_ge(halo_saved, NC * q + c - 1)
                if c == 0 and not (isinstance(q, int) and q < 2):
                    filled(act, q - 1, "out", 1)
                edge = slice(0, HALO) if D == 0 else slice(TB, TB + HALO)
                body_ = slice(HALO, HALO + TB) if D == 0 else slice(0, TB)
                nc.scalar.activation(xp[:, c % 2, edge], halo[:, D, c, :], ACT.Copy).then_inc(xp_head, 1)
                bank = filled(act, q - 1, "xp", c)
                nc.scalar.activation(xp[:, c % 2, body_], psum[:, bank, :], ACT.Copy).then_inc(xp_body, 1)
                nc.scalar.activation(xc[:, D, c, :], psum[:, bank, :], ACT.Copy,
                                     scale=w_conv[:, D, c, HALO:TAPS]).then_inc(bank_free[bank - PS_P], 1)

            def silu_z(c, q):
                if not is_first(q):
                    act.wait_ge(yg_done, NC * q)
                bank = filled(act, q, "z", c)
                nc.scalar.activation(sz[:, c, :], psum[:, bank, :], ACT.Silu).then_inc(bank_free[bank - PS_P], 1)

            def silu_xc(c, D, q):
                act.wait_ge(conv_done, NC * q + c + 1)
                nc.scalar.activation(xc[:, D, c, :], xc[:, D, c, :], ACT.Silu,
                                     bias=b_conv[:, D, c:c + 1]).then_inc(xc_done, 1)

            def copy_x_dbl(q):
                if not is_first(q):
                    act.wait_ge(bc_stored, 16 * q)
                bank = filled(act, q - 1, "xdbl", 0)
                nc.scalar.activation(x_dbl[:], psum[0:48, bank, :], ACT.Copy).then_inc(bank_free[bank - PS_P], 1)

            def softplus(c, D, q):
                if c == 0 and not is_first(q):
                    act.wait_ge(dt_done, NC * q)
                if c == 0 and not (isinstance(q, int) and q < 2):
                    act.wait_ge(t_stored, 16 * (q - 1))
                bank = filled(act, q - 1, "dt", c)
                nc.scalar.activation(dt[:, D, c, :], psum[:, bank, :], ACT.Relu,
                                     bias=b_dt[:, D, c:c + 1]).then_inc(sp_relu, 1)
                nc.scalar.activation(sp_tmp[:, c, :], psum[:, bank, :], ACT.Abs,
                                     bias=b_dt[:, D, c:c + 1]).then_inc(bank_free[bank - PS_P], 1)
                drained(act, q - 1, "dt", c)
                nc.scalar.activation(sp_tmp[:, c, :], sp_tmp[:, c, :], ACT.Exp, scale=-1.0).then_inc(sp_exp, 1)

            def softplus_log(q):
                act.wait_ge(sp_exp, NC * (q + 1))
                nc.scalar.activation(sp_tmp[:], sp_tmp[:], ACT.Ln, bias=1.0).then_inc(sp_done, 1)

            def decay(u, n, D, q):
                c, g = divmod(u, NG)
                K = GN * (UNITS * q + u) + n
                if g == 0 and n == 0:
                    act.wait_ge(dt_done, NC * q + c + 1)
                if not (isinstance(K, int) and K < GN):
                    act.wait_ge(scan_done, K - GN + 1)
                nc.scalar.activation(psum[:, PS_A + n, :], dt[:, D, c, :], ACT.Exp,
                                     scale=neg_a[:, D, c, g * GN + n:g * GN + n + 1]).then_inc(exp_done, 1)

            act.wait_ge(zeroed, 2)
            for c in range(NC):
                copy_xp(c, 0, 0)
            for c in range(NC):
                silu_xc(c, 0, 0)
            copy_x_dbl(0)
            for c in range(NC):
                softplus(c, 0, 0)
            softplus_log(0)

            def step(i, D, q):
                for t in range(UNITS):
                    for n in range(GN):
                        if (t, n) == (10, 1):
                            silu_z(0, q)
                            silu_z(1, q)
                            if not is_last(q):
                                for c in range(NC):
                                    silu_xc(c, 1 - D, q + 1)
                        if (t, n) == (14, 3):
                            silu_z(2, q)
                            silu_z(3, q)
                        decay(t, n, D, q)
                        if is_last(q):
                            continue
                        if (t, n) in XP_AT:
                            copy_xp(XP_AT.index((t, n)), 1 - D, q + 1)
                        if (t, n) == (11, 1):
                            copy_x_dbl(q + 1)
                        if (t, n) in DT_AT:
                            softplus(DT_AT.index((t, n)), 1 - D, q + 1)
                        if (t, n) == (13, 3):
                            softplus_log(q + 1)

            run_steps(act, step)
            meet(act, 2)

            def h2_transposed(n, half):
                for kd in range(KD):
                    g_filled(act, n - 1, "T", kd)
                    nc.scalar.activation(h2T[:, half, kd, :], psum[:, kd, :], ACT.Copy).then_inc(g_free[kd], 1)

            def exp_scores(n):
                g_drained(act, n - 1, "gate", 0)
                nc.scalar.activation(score[:], score[:], ACT.Exp).then_inc(f_exp, 1)

            def route_hi(n, half):
                g_filled(act, n - 1, "wmT", 1)
                nc.scalar.activation(wm3[0:16, half, :], psum[0:16, 1, :], ACT.Copy).then_inc(f_whi, 1)

            def route_mid(n, half):
                g_drained(act, n - 1, "wmT", 1)
                nc.scalar.activation(wm_mid[:], wm_r[:], ACT.Copy).then_inc(f_wmid, 1)
                nc.scalar.activation(wm3[32:48, half, :], wm_r[:], ACT.Copy).then_inc(f_wmid, 1)

            def mask_row(e, i):
                if not (isinstance(i, int) and i == 0 and e < 2):
                    act.wait_ge(f_m3, 2 * (NE * i + e - 2) + 2)
                g_filled(act, i, "mask", e)
                nc.scalar.activation(mask_wide[:, e % 2, :], psum[:, 1, :], ACT.Copy).then_inc(g_free[1], 1)

            def silu_h1(e, i):
                for hc in range(2):
                    act.wait_ge(f_h1_full, H_USES * i + 2 * e + hc + 1)
                    if not (isinstance(i, int) and i == 0 and e < 2):
                        act.wait_ge(f_x2_full, Y_USES * i + 2 * e - 2)
                    nc.scalar.activation(h1[:, e % 2, hc, :], psum[:, 2 + hc, :], ACT.Silu,
                                         bias=b1[:, e, hc:hc + 1]).then_inc(f_h1, 1)

            def silu_shared(c, i):
                act.wait_ge(f_h1_full, H_USES * i + 2 * NE + c + 1)
                if not (isinstance(i, int) and i == 0 and c < 2):
                    act.wait_ge(f_sh_u, NC * i + c - 1)
                nc.scalar.activation(g_silu[:, c % 2, :], psum[:, 2 + c % 2, :], ACT.Silu).then_inc(f_h1, 1)

            def body(half, i):
                ahead = not (isinstance(i, int) and i == NBLK - 1)
                mask_row(0, i)
                for e in range(NE):
                    if e + 1 < NE:
                        mask_row(e + 1, i)
                    silu_h1(e, i)
                    if ahead and e == 2:
                        h2_transposed(i + 1, 1 - half)
                    if ahead and e == 5:
                        exp_scores(i + 1)
                    if ahead and e == 6:
                        route_hi(i + 1, 1 - half)
                    if ahead and e == 7:
                        route_mid(i + 1, 1 - half)
                for c in range(NC):
                    silu_shared(c, i)

            act.wait_ge(wm3_zeroed, 1)
            h2_transposed(0, 0)
            exp_scores(0)
            route_hi(0, 0)
            route_mid(0, 0)
            act.wait_ge(f_w_loaded, 16 * 9)
            run_blocks(act, body)

        @block.vector
        def _(dve):
            span = SEG * NT

            def statistics(src, ln, b, ready):
                with dve.Fori(0, SEG) as s:
                    for tt in range(NT):
                        tile = s * NT + (b * span + tt)
                        if ready is not None and tt == 0:
                            dve.wait_ge(ready, s + (b * SEG + 1))
                        nc.vector.bn_stats(stats[:, bass.ds(tile, 1), :].rearrange("p a n -> p (a n)"),
                                           src[:, bass.ds(tile, 1), :].rearrange("p a n -> p (a n)")
                                           ).then_inc(p1_stat, 1)
                dve.wait_ge(p1_stat, span * (ln * BATCH + b + 1))
                for tile in range(b * span, (b + 1) * span):
                    nc.vector.bn_aggr(mv[:, ln, tile, :], stats[:, tile, :]).then_inc(p1_aggr, 1)
                dve.wait_ge(p1_aggr, span * (ln * BATCH + b + 1))
                nc.vector.tensor_scalar(var_eps[:, ln, b * span:(b + 1) * span],
                                        mv[:, ln, b * span:(b + 1) * span, 1], EPS, None, ALU.add
                                        ).then_inc(p1_var, 1)

            def normalise(dst, src, ln, tile):
                nc.vector.tensor_scalar(dst[:, bass.ds(tile, 1), :].rearrange("p a n -> p (a n)"),
                                        src[:, bass.ds(tile, 1), :].rearrange("p a n -> p (a n)"),
                                        mv[:, ln, bass.ds(tile, 1), 0:1].rearrange("p a n -> p (a n)"),
                                        rstd[:, ln, bass.ds(tile, 1)],
                                        ALU.subtract, ALU.mult).then_inc(p1_norm, 1)

            dve.wait_ge(x_loaded[0], 16)
            statistics(X, 0, 0, None)
            dve.wait_ge(mod_copied, 6)
            for j in (1, 4):
                nc.vector.tensor_scalar(mod[:, :, j, :], mod[:, :, j, :], 1.0, None, ALU.add).then_inc(mod_step, 1)
            for n, j in enumerate((2, 5)):
                nc.vector.tensor_scalar(mod_abs[:], mod[:, :, j, :], -1.0, 0.25, ALU.mult, ALU.max
                                        ).then_inc(mod_step, 1)
                nc.vector.tensor_scalar(mod_sign[:], mod[:, :, j, :], 0.0, 2.0, ALU.is_ge, ALU.mult
                                        ).then_inc(mod_step, 1)
                dve.wait_ge(mod_step, 2 + 4 * n + 2)
                nc.vector.tensor_tensor(mod_abs[:], mod_abs[:], mod[:, :, j, :], ALU.max).then_inc(mod_step, 1)
                dve.wait_ge(mod_step, 2 + 4 * n + 3)
                nc.vector.scalar_tensor_tensor(mod[:, :, j, :], mod_sign[:], -1.0, mod_abs[:], ALU.add, ALU.mult
                                               ).then_inc(mod_step, 1)
                dve.wait_ge(mod_step, 2 + 4 * n + 4)
            dve.wait_ge(x_loaded[1], 16)
            statistics(X, 0, 1, None)
            for b in range(BATCH):
                dve.wait_ge(p1_rstd, b + 1)
                with dve.Fori(0, SEG) as s:
                    for tt in range(NT):
                        normalise(H, X, 0, s * NT + (b * span + tt))
                    dve.wait_ge(p1_norm, s * NT + (b * span + NT))
                    Hb = H[:, bass.ds(s * NT + b * span, NT), :]
                    nc.vector.tensor_tensor(Hb, Hb, mod[:, b, 1:2, :].broadcast_to((P, NT, DM)),
                                            ALU.mult).then_inc(p1_scaled, 1)
            dve.wait_ge(w_loaded, 16 * 9)
            dve.wait_ge(neg_a_done, 1)
            nc.vector.tensor_scalar(neg_a[:], neg_a[:], -1.0, None, ALU.mult).then_inc(w_out_done, 1)
            nc.vector.tensor_scalar(w_out[:], w_out[:], 0.5, None, ALU.mult).then_inc(w_out_done, 1)
            for b in range(BATCH):
                statistics(H, 1, b, h_done)
            for b in range(BATCH):
                dve.wait_ge(p1_rstd, BATCH + b + 1)
                with dve.Fori(0, SEG) as s:
                    for tt in range(NT):
                        normalise(X, H, 1, s * NT + (b * span + tt))
            meet(dve, 1)

            def conv(c, D, q):
                S = q - 1
                drained(dve, S, "xp", c)
                src = xp[:, c % 2, :]
                dst = xc[:, D, c, :]
                for j in range(HALO):
                    at = j if D == 0 else HALO - j
                    if j > 0:
                        dve.wait_ge(conv_step, (HALO - 1) * (NC * q + c) + j)
                    nc.vector.scalar_tensor_tensor(dst, src[:, at:at + TB], w_conv[:, D, c, j:j + 1], dst,
                                                   ALU.mult, ALU.add
                                                   ).then_inc(conv_step if j < HALO - 1 else conv_done, 1)

            def add_skip(c, D, q):
                dve.wait_ge(unit_summed, UNITS * q + NG * (c + 1))
                nc.vector.scalar_tensor_tensor(xc[:, D, c, :], xc[:, D, c, :], d_skip[:, D, c:c + 1],
                                               psum[:, PS_Y, :], ALU.mult, ALU.add).then_inc(y_skip, 1)

            def gate_y(c, D, q):
                dve.wait_ge(y_skip, NC * q + c + 1)
                drained(dve, q, "z", c)
                nc.vector.tensor_tensor(xc[:, D, c, :], xc[:, D, c, :], sz[:, c, :], ALU.mult
                                        ).then_inc(yg_done, 1)

            def add_out(S):
                dve.wait_ge(t_loaded, 16 * S)
                for b in range(2):
                    bank = filled(dve, S, "out", b)
                    dst = t_blk[:, b * TB:(b + 1) * TB]
                    nc.vector.tensor_tensor(dst, dst, psum[:, bank, :], ALU.add
                                            ).then_inc(bank_free[bank - PS_P], 1)

            def multiply(u, D, q):
                c, g = divmod(u, NG)
                U = UNITS * q + u
                if g == 0:
                    dve.wait_ge(dt_done, NC * q + c + 1)
                    dve.wait_ge(xc_done, NC * q + c + 1)
                    if not (isinstance(U, int) and U == 0):
                        dve.wait_ge(mult_done, U)
                    nc.vector.tensor_tensor(psum[:, PS_U, :], dt[:, D, c, :], xc[:, D, c, :], ALU.mult
                                            ).then_inc(dtu_done, 1)
                    dve.wait_ge(dtu_done, NC * q + c + 1)
                rows_ready(dve, 0, g, q)
                if not (isinstance(U, int) and U < 2):
                    dve.wait_ge(scan_done, GN * (U - 1))
                nc.vector.tensor_tensor(dbu[:, u % 2, :, :],
                                        psum[:, PS_U:PS_U + 1, :].broadcast_to((P, GN, TB)),
                                        b_wide[:, 0, g * GN:(g + 1) * GN, :], ALU.mult).then_inc(mult_done, 1)

            def scans(u, D, q):
                U = UNITS * q + u
                dve.wait_ge(mult_done, U + 1)
                if not (isinstance(U, int) and U < 4):
                    dve.wait_ge(unit_summed, U - 3)
                for n in range(GN):
                    dve.wait_ge(exp_done, GN * U + n + 1)
                    nc.vector.tensor_tensor_scan(
                        time_order(hst[:, u % 4, n, :], D), time_order(psum[:, PS_A + n, :], D),
                        time_order(dbu[:, u % 2, n, :], D), state[:, D, u * GN + n:u * GN + n + 1],
                        ALU.mult, ALU.add).then_inc(scan_done, 1)

            dve.wait_ge(zeroed, 2)
            for c in range(NC):
                conv(c, 0, 0)
            multiply(0, 0, 0)

            def step(i, D, q):
                for t in range(UNITS):
                    if t == 2 and not is_first(q):
                        add_skip(3, 1 - D, q - 1)
                        gate_y(3, 1 - D, q - 1)
                    if t == 4 and not is_first(q):
                        add_out(q)
                    if t in (6, 10, 14):
                        add_skip((t - 6) // 4, D, q)
                    if t in (11, 12):
                        gate_y(t - 11, D, q)
                    if t + 1 < UNITS:
                        multiply(t + 1, D, q)
                    elif not is_last(q):
                        multiply(0, 1 - D, q + 1)
                    scans(t, D, q)
                    if t == 15:
                        gate_y(2, D, q)
                    if is_last(q):
                        continue
                    if 5 <= t < 9:
                        conv(t - 5, 1 - D, q + 1)

            run_steps(dve, step)
            add_skip(3, 1, STEPS - 1)
            gate_y(3, 1, STEPS - 1)
            add_out(STEPS)
            meet(dve, 2)

            nc.vector.memset(wm3[:], 0.0).then_inc(wm3_zeroed, 1)
            dve.wait_ge(f_gate_loaded, 32)

            def mod_row(n, j):
                return fmod[:, bass.ds(n // SEG, 1), j:j + 1, :].rearrange(
                    "p a b d -> p (a b) d").broadcast_to((P, NT, DM))

            def norm_statistics(n, half):
                dve.wait_ge(f_in, 32 * (n + 1))
                if not (isinstance(n, int) and n < 2):
                    dve.wait_ge(f_o, n - 1)
                nc.vector.tensor_tensor(x1[:, half], tin[:], mod_row(n, 0), ALU.mult).then_inc(f_x1, 1)
                dve.wait_ge(f_x1, 2 * n + 1)
                nc.vector.tensor_tensor(x1[:, half], x1[:, half], xin[:], ALU.add).then_inc(f_x1, 1)
                dve.wait_ge(f_x1, 2 * n + 2)
                for tt in range(NT):
                    nc.vector.bn_stats(fstats[:, tt, :], x1[:, half, tt, :]).then_inc(f_stat, 1)
                dve.wait_ge(f_stat, NT * (n + 1))
                wait_apart(dve)
                for tt in range(NT):
                    nc.vector.bn_aggr(fmv[:, tt, :], fstats[:, tt, :]).then_inc(f_aggr, 1)
                dve.wait_ge(f_aggr, NT * (n + 1))
                nc.vector.tensor_scalar(fvar[:], fmv[:, :, 1], EPS, None, ALU.add).then_inc(f_var, 1)

            def norm_apply(n, half):
                dve.wait_ge(f_rstd, n + 1)
                if not (isinstance(n, int) and n == 0):
                    for kd in range(KD):
                        g_filled(dve, n - 2, "T", kd)
                for tt in range(NT):
                    nc.vector.tensor_scalar(h2[:, tt, :], x1[:, half, tt, :], fmv[:, tt, 0:1], frstd[:, tt:tt + 1],
                                            ALU.subtract, ALU.mult).then_inc(f_norm, 1)
                dve.wait_ge(f_norm, NT * (n + 1))
                nc.vector.tensor_tensor(h2[:], h2[:], mod_row(n, 2), ALU.mult).then_inc(f_scaled, 1)

            def shift_logits(n):
                g_filled(dve, n - 1, "gate", 0)
                logits = psum[:, 0, 0:NT * NE].rearrange("p (t e) -> p t e", t=NT)
                nc.vector.tensor_reduce(fmax[:], logits, axis=AX_X, op=ALU.max).then_inc(f_route, 1)
                dve.wait_ge(f_route, ROUTE * n + 1)
                nc.vector.tensor_tensor(score[:], logits,
                                        fmax[:].rearrange("p (t a) -> p t a", a=1).broadcast_to((P, NT, NE)),
                                        ALU.subtract).then_inc(g_free[0], 1)

            def top_two(n):
                count = [ROUTE * n + 1]

                def chain(ins):
                    ins.then_inc(f_route, 1)
                    count[0] = count[0] + 1
                    dve.wait_ge(f_route, count[0])

                dve.wait_ge(f_exp, n + 1)
                chain(nc.vector.tensor_reduce(fsum[:], score[:], axis=AX_X, op=ALU.add))
                chain(nc.vector.reciprocal(fsum[:], fsum[:]))
                chain(nc.vector.tensor_tensor(
                    score[:], score[:], fsum[:].rearrange("p (t a) -> p t a", a=1).broadcast_to((P, NT, NE)),
                    ALU.mult))
                other = score[:].rearrange("p t (a e) -> p t a e", a=1).broadcast_to((P, NT, NE, NE))
                own = score[:].rearrange("p t (e a) -> p t e a", a=1).broadcast_to((P, NT, NE, NE))
                chain(nc.vector.tensor_tensor(cmp_gt[:], other, own, ALU.is_gt))
                chain(nc.vector.tensor_tensor(cmp_eq[:], other, own, ALU.is_equal))
                chain(nc.vector.tensor_tensor(
                    cmp_eq[:], cmp_eq[:],
                    lower[:].rearrange("p (a e) f -> p a e f", a=1).broadcast_to((P, NT, NE, NE)), ALU.mult))
                chain(nc.vector.tensor_tensor(cmp_gt[:], cmp_gt[:], cmp_eq[:], ALU.add))
                chain(nc.vector.tensor_reduce(rank[:], cmp_gt[:], axis=AX_X, op=ALU.add))
                chain(nc.vector.tensor_scalar(wm[:, :, NE:2 * NE], rank[:], 1.5, None, ALU.is_lt))
                nc.vector.tensor_tensor(wm[:, :, 0:NE], score[:], wm[:, :, NE:2 * NE], ALU.mult).then_inc(f_wm, 1)

            def route_r1(n, half):
                dve.wait_ge(f_whi, n + 1)
                g_filled(dve, n - 1, "wmT", 1)
                nc.vector.tensor_tensor(wm_r[:], psum[0:16, 1, :], wm3[0:16, half, :], ALU.subtract
                                        ).then_inc(g_free[1], 1)

            def route_lo(n, half):
                dve.wait_ge(f_wmid, 2 * n + 2)
                nc.vector.tensor_tensor(wm3[64:80, half, :], wm_r[:], wm_mid[:], ALU.subtract).then_inc(f_wlo, 1)

            def scale_in(e, half, i):
                g_filled(dve, i, "weight", e)
                if not (isinstance(i, int) and i == 0 and e < 2):
                    dve.wait_ge(f_x3_full, H_USES * i + 2 * e - (2 if e > 1 else 2 + NC))
                nc.vector.tensor_tensor(xs[:, e % 2], h2T[:, half], psum[:, 0:1, :].broadcast_to((P, KD, TB)),
                                        ALU.mult).then_inc(g_free[0], 1)

            def gate_x3(e, half, i):
                g_drained(dve, i, "mask", e)
                for c in range(KD):
                    dve.wait_ge(f_x3_full, H_USES * i + 2 * e + c + 1)
                    nc.vector.scalar_tensor_tensor(m3[:, e % 2, c, :], psum[:, 4 + c, :], b3[:, e, c:c + 1],
                                                   mask_wide[:, e % 2, :], ALU.add, ALU.mult).then_inc(f_m3, 1)

            def combine(e, half, i):
                dve.wait_ge(f_m3, 2 * NE * i + 2 * e + 2)
                if e > 2:
                    dve.wait_ge(f_y, (NE - 1) * i + e - 2)
                elif e > 0 and not (isinstance(i, int) and i == 0):
                    dve.wait_ge(f_y, (NE - 1) * i - (e - 1))
                if e == 0 and not (isinstance(i, int) and i < 2):
                    dve.wait_ge(f_o_full, 2 * (i - 1))
                for c in range(KD):
                    dve.wait_ge(f_x2_full, Y_USES * i + 2 * e + c + 1)
                    dst = y[:, half, c, :] if e == 0 else prod[:, e % 2, c, :]
                    nc.vector.scalar_tensor_tensor(dst, psum[:, 6 + c, :], b2[:, e, c:c + 1],
                                                   m3[:, e % 2, c, :], ALU.add, ALU.mult).then_inc(f_prod, 1)

            def shared(c, i):
                dve.wait_ge(f_h1, H_USES * i + 2 * NE + c + 1)
                dve.wait_ge(f_x3_full, H_USES * i + 2 * NE + c + 1)
                if not (isinstance(i, int) and i == 0):
                    dve.wait_ge(f_o_full, 2 * i)
                nc.vector.tensor_tensor(u_sh[:, c, :], g_silu[:, c % 2, :], psum[:, 4 + c % 2, :], ALU.mult
                                        ).then_inc(f_sh_u, 1)

            def scale_out(half, i, k):
                for b in range(2):
                    dve.wait_ge(f_o_full, 2 * i + b + 1)
                    if k is not None:
                        dve.wait_ge(f_out[half], 16 * k)
                    row = fmod[:, bass.ds(i // SEG, 1), 3:4, :].rearrange(
                        "p a b d -> p (a b) d").broadcast_to((P, 2, DM))
                    nc.vector.tensor_tensor(o_blk[:, half, 2 * b:2 * b + 2, :],
                                            psum[:, 6 + b, :].rearrange("p (t d) -> p t d", t=2), row,
                                            ALU.mult).then_inc(f_o_mul, 1)

            def body(half, i):
                ahead = not (isinstance(i, int) and i == NBLK - 1)
                scale_in(0, half, i)
                for e in range(NE):
                    if e + 1 < NE:
                        scale_in(e + 1, half, i)
                    gate_x3(e, half, i)
                    combine(e, half, i)
                    if ahead and e == 0:
                        norm_statistics(i + 1, 1 - half)
                    if ahead and e == 1:
                        norm_apply(i + 1, 1 - half)
                    if ahead and e == 4:
                        shift_logits(i + 1)
                    if ahead and e == 5:
                        top_two(i + 1)
                    if ahead and e == 6:
                        route_r1(i + 1, 1 - half)
                    if ahead and e == 7:
                        route_lo(i + 1, 1 - half)
                for c in range(NC):
                    shared(c, i)
                scale_out(half, i, None if isinstance(i, int) and i < 2 else (i - half) // 2)

            dve.wait_ge(f_const, 3)
            norm_statistics(0, 0)
            norm_apply(0, 0)
            shift_logits(0)
            top_two(0)
            route_r1(0, 0)
            route_lo(0, 0)
            dve.wait_ge(f_w_loaded, 16 * 9)
            run_blocks(dve, body)

        @block.tensor
        def _(pe):
            pe.wait_ge(c_ready, 4)
            for b in range(BATCH):
                for j in range(3):
                    for k in range(KD):
                        ins = nc.tensor.matmul(psum[:, 3 * b + j, :], c_wide[:, k, b, :],
                                               w_mod[:, k, j * TB:(j + 1) * TB], start=(k == 0), stop=(k == KD - 1))
                    ins.then_inc(mod_full, 1)
            pe.wait_ge(mod_copied, 6)
            pe.wait_ge(consts, 4)

            def transpose_xn(k):
                for half in range(2):
                    pe.wait_ge(p1_norm, NBLK * NT + k * 2 * NT + half * NT + NT)
                    if k > 0:
                        pe.wait_ge(xnT_copied, k * 4 + 2 * half - 2)
                    for kd in range(KD):
                        for tt in range(NT):
                            ins = nc.tensor.transpose(
                                psum[:, 2 * half + kd, tt * P:(tt + 1) * P],
                                X[:, (2 * k + half) * NT + tt, kd * P:(kd + 1) * P], ident[:])
                        ins.then_inc(xnT_full, 1)

            for k in range(NBLK // 2):
                transpose_xn(k)
            meet(pe, 1)

            def project_x(c, D, q):
                if c == 0:
                    n = q // 2 + 1 if isinstance(q, int) else (q - D) // 2 + 1
                    pe.wait_ge(xnT_loaded[D], 16 * n)
                bank = take_bank(pe, q - 1, "xp", c)
                for k in range(KD):
                    ins = nc.tensor.matmul(psum[:, PS_P + bank, :], w_in[:, D, k, c * P:(c + 1) * P],
                                           xnT[:, D, k, :], start=(k == 0), stop=(k == KD - 1))
                ins.then_inc(bank_full[bank], 1)

            def project_z(c, D, q):
                bank = take_bank(pe, q, "z", c)
                for k in range(KD):
                    ins = nc.tensor.matmul(psum[:, PS_P + bank, :], w_in[:, D, k, DI + c * P:DI + (c + 1) * P],
                                           xnT[:, D, k, :], start=(k == 0), stop=(k == KD - 1))
                ins.then_inc(bank_full[bank], 1)

            def project_out(D, S):
                pe.wait_ge(yg_done, NC * S)
                for b in range(2):
                    bank = take_bank(pe, S, "out", b)
                    for half in range(2):
                        tok = slice((2 * b + half) * P, (2 * b + half + 1) * P)
                        for c in range(NC):
                            ins = nc.tensor.matmul(psum[:, PS_P + bank, half * DM:(half + 1) * DM],
                                                   xc[:, D, c, tok], w_out[:, D, c, :],
                                                   start=(c == 0), stop=(c == NC - 1))
                    ins.then_inc(bank_full[bank], 1)

            def project_xdbl(D, q):
                pe.wait_ge(xc_done, NC * (q + 1))
                bank = take_bank(pe, q - 1, "xdbl", 0)
                for c in range(NC):
                    ins = nc.tensor.matmul(psum[0:48, PS_P + bank, :], w_x[:, D, c, :], xc[:, D, c, :],
                                           start=(c == 0), stop=(c == NC - 1))
                ins.then_inc(bank_full[bank], 1)

            def project_dt(c, D, q):
                drained(pe, q - 1, "xdbl", 0)
                bank = take_bank(pe, q - 1, "dt", c)
                nc.tensor.matmul(psum[:, PS_P + bank, :], w_dt[32:48, D, c * P:(c + 1) * P], x_dbl[32:48, :],
                                 start=True, stop=True).then_inc(bank_full[bank], 1)

            def sum_state(u, n, D, q):
                c, g = divmod(u, NG)
                U = UNITS * q + u
                if n == 0:
                    pe.wait_ge(prod_done, U + 1)
                    if g == 0 and not (isinstance(U, int) and U == 0):
                        pe.wait_ge(y_skip, NC * q + c)
                ins = nc.tensor.matmul(psum[:, PS_Y, :], ident[:], hst[:, u % 4, n, :],
                                       start=(g == 0 and n == 0), stop=(g == NG - 1 and n == GN - 1))
                if n == GN - 1:
                    ins.then_inc(unit_summed, 1)

            pe.wait_ge(w_out_done, 2)
            for c in range(NC):
                project_x(c, 0, 0)
            project_xdbl(0, 0)
            for c in range(NC):
                project_dt(c, 0, 0)

            def step(i, D, q):
                for t in range(UNITS):
                    for n in range(GN):
                        if t == 3 and n == 0 and not is_first(q):
                            project_out(1 - D, q)
                        if t in (8, 13) and n in (1, 3):
                            project_z(2 * (t == 13) + n // 2, D, q)
                        if not is_last(q):
                            if t in (4, 6) and n in (1, 3):
                                project_x(t - 4 + n // 2, 1 - D, q + 1)
                            if (t, n) == (10, 2):
                                project_xdbl(1 - D, q + 1)
                            if t in (11, 12) and n in (1, 3):
                                project_dt(2 * (t - 11) + n // 2, 1 - D, q + 1)
                        if t >= 2:
                            sum_state(t - 2, n, D, q)
                        elif not is_first(q):
                            sum_state(UNITS + t - 2, n, 1 - D, q - 1)

            run_steps(pe, step)
            for u in (UNITS - 2, UNITS - 1):
                for n in range(GN):
                    sum_state(u, n, 1, STEPS - 1)
            project_out(1, STEPS)
            meet(pe, 2)

            def transpose_h2(n):
                pe.wait_ge(f_h2, n + 1)
                for kd in range(KD):
                    g_take(pe, n - 1, "T", kd)
                    for tt in range(NT):
                        ins = nc.tensor.transpose(psum[:, kd, tt * P:(tt + 1) * P],
                                                  h2[:, tt, kd * P:(kd + 1) * P], ident[:])
                    ins.then_inc(g_full[kd], 1)

            def router(n, half):
                for kd in range(KD):
                    g_drained(pe, n - 1, "T", kd)
                g_take(pe, n - 1, "gate", 0)
                for tt in range(NT):
                    for kd in range(KD):
                        ins = nc.tensor.matmul(psum[:, 0, tt * NE:(tt + 1) * NE],
                                               h2T[:, half, kd, tt * P:(tt + 1) * P], gate[:, kd, :],
                                               start=(kd == 0), stop=(kd == KD - 1))
                ins.then_inc(g_full[0], 1)

            def transpose_wm(n):
                pe.wait_ge(f_wm, n + 1)
                g_take(pe, n - 1, "wmT", 1)
                for tt in range(NT):
                    ins = nc.tensor.transpose(psum[0:16, 1, tt * P:(tt + 1) * P], wm[:, tt, :], ident[:])
                ins.then_inc(g_full[1], 1)

            def spread_weight(e, half, i):
                if e == 0:
                    pe.wait_ge(f_wlo, i + 1)
                for bank, kind in ((0, "weight"), (1, "mask")):
                    g_take(pe, i, kind, e)
                    m = NE * bank + e
                    nc.tensor.matmul(psum[:, bank, :], row_pick[:, m:m + 1].broadcast_to((96, P)),
                                     wm3[:, half, :], start=True, stop=True).then_inc(g_full[bank], 1)

            def matrix(dst, w, c, src):
                for k in range(KD):
                    ins = nc.tensor.matmul(dst, w[:, k, c * P:(c + 1) * P], src[:, k, :],
                                           start=(k == 0), stop=(k == KD - 1))
                return ins

            def body(half, i):
                ahead = not (isinstance(i, int) and i == NBLK - 1)
                spread_weight(0, half, i)
                for e in range(NE):
                    if e + 1 < NE:
                        spread_weight(e + 1, half, i)
                    g_drained(pe, i, "weight", e)
                    for c in range(KD):
                        if not (isinstance(i, int) and i == 0 and e == 0):
                            pe.wait_ge(f_h1, H_USES * i + 2 * e + c - 1)
                        matrix(psum[:, 2 + c, :], w1[:, e], c, xs[:, e % 2]).then_inc(f_h1_full, 1)
                    for c in range(KD):
                        if not (isinstance(i, int) and i == 0 and e == 0):
                            if e > 0:
                                pe.wait_ge(f_m3, 2 * NE * i + 2 * e + c - 1)
                            else:
                                pe.wait_ge(f_sh_u, NC * i + c - 1)
                        matrix(psum[:, 4 + c, :], w3[:, e], c, xs[:, e % 2]).then_inc(f_x3_full, 1)
                    pe.wait_ge(f_h1, H_USES * i + 2 * e + 2)
                    for c in range(KD):
                        if not (isinstance(i, int) and i == 0 and e == 0):
                            if e > 0:
                                pe.wait_ge(f_prod, 2 * NE * i + 2 * e + c - 1)
                            else:
                                pe.wait_ge(f_o_mul, 2 * i + c - 1)
                        matrix(psum[:, 6 + c, :], w2[:, e], c, h1[:, e % 2]).then_inc(f_x2_full, 1)
                    if ahead and e == 2:
                        transpose_h2(i + 1)
                    if ahead and e == 4:
                        router(i + 1, 1 - half)
                    if ahead and e == 6:
                        transpose_wm(i + 1)
                for c in range(NC):
                    pe.wait_ge(f_h1, H_USES * i + 2 * NE + c - 1)
                    matrix(psum[:, 2 + c % 2, :], sw1[:], c, h2T[:, half]).then_inc(f_h1_full, 1)
                    if c < 2:
                        pe.wait_ge(f_m3, 2 * NE * (i + 1) + c - 1)
                    else:
                        pe.wait_ge(f_sh_u, NC * i + c - 1)
                    matrix(psum[:, 4 + c % 2, :], sw2[:], c, h2T[:, half]).then_inc(f_x3_full, 1)
                pe.wait_ge(f_sh_u, NC * (i + 1))
                pe.wait_ge(f_y, (NE - 1) * (i + 1))
                for b in range(2):
                    pe.wait_ge(f_prod, 2 * NE * (i + 1) + b - 1)
                    for tt in (2 * b, 2 * b + 1):
                        tok = slice(tt * P, (tt + 1) * P)
                        cols = psum[:, 6 + b, (tt % 2) * DM:(tt % 2 + 1) * DM]
                        for c in range(NC):
                            nc.tensor.matmul(cols, u_sh[:, c, tok], sw3[:, c, :], start=(c == 0), stop=False)
                        for k in range(KD):
                            ins = nc.tensor.matmul(cols[:, k * P:(k + 1) * P], y[:, half, k, tok], ident[:],
                                                   start=False, stop=(k == KD - 1))
                    ins.then_inc(f_o_full, 1)

            pe.wait_ge(f_gate_loaded, 32)
            transpose_h2(0)
            router(0, 0)
            transpose_wm(0)
            pe.wait_ge(f_w_loaded, 16 * 9)
            run_blocks(pe, body)


def on_partitions(w):
    return w.reshape(w.shape[0] // P, P, *w.shape[1:]).swapaxes(0, 1)


def lay_out(inputs):
    import numpy as np
    a = {k.replace("L0_", ""): np.asarray(v) for k, v in inputs.items()}
    both = lambda name: (a["attn_f_" + name], a["attn_b_" + name])
    stack = lambda parts: np.stack(parts, axis=1)
    out = {
        "x": a["attn_x"].reshape(NBLK, NT, P, DM).transpose(0, 2, 1, 3).reshape(NBLK, P, NT * DM),
        "cT": on_partitions(a["c"].T),
        "w_mod": on_partitions(a["wmod"]),
        "ln_w": on_partitions(a["attn_ln_w"]),
        "ln_b": on_partitions(a["attn_ln_b"]),
        "w_in": stack([on_partitions(w.T) for w in both("W_in")]),
        "w_x": stack([on_partitions(np.concatenate([w[DR:], w[:DR]]).T) for w in both("W_x")]),
        "w_dt": stack([w.T for w in both("W_dt")]),
        "w_out": stack([on_partitions(w.T) for w in both("W_out")]),
        "a_log": stack([on_partitions(w) for w in both("A_log")]),
        "w_conv": stack([on_partitions(w) for w in both("W_conv")]),
        "b_conv": stack([on_partitions(w) for w in both("b_conv")]),
        "b_dt": stack([on_partitions(w) for w in both("b_dt")]),
        "d_skip": stack([on_partitions(w) for w in both("D")]),
        "gate": on_partitions(a["ffn_gate_w"].T),
        "sw1": on_partitions(a["ffn_sw1"].T),
        "sw2": on_partitions(a["ffn_sw2"].T),
        "sw3": on_partitions(a["ffn_sw3"].T),
    }
    for n in "123":
        out["w" + n] = stack([on_partitions(w.T) for w in a["ffn_w" + n]])
        out["b" + n] = stack([on_partitions(b) for b in a["ffn_b" + n]])
    return {k: np.ascontiguousarray(v) for k, v in out.items()}


def kernel(**inputs):
    import numpy as np
    import concourse.bacc as bacc
    from concourse.bass_utils import run_bass_kernel_spmd

    nc = bacc.Bacc("TRN2", target_bir_lowering=False, num_devices=1)
    arrays = lay_out(inputs)
    aps = {name: nc.dram_tensor(f"in_{name}", v.shape, mybir.dt.from_np(v.dtype), kind="ExternalInput").ap()
           for name, v in arrays.items()}
    out = nc.dram_tensor("out_x", (NBLK, P, NT * DM), F32, kind="ExternalOutput").ap()
    mixer_and_experts(nc, aps, out)
    r = run_bass_kernel_spmd(nc, [{f"in_{k}": v for k, v in arrays.items()}], core_ids=[0])
    y = np.asarray(r.results[0]["out_x"])
    return y.reshape(NBLK, P, NT, DM).transpose(0, 2, 1, 3).reshape(BATCH, SEQ, DM)
```

```python
from contextlib import ExitStack

import concourse.bass as bass
from concourse import mybir

ALU = mybir.AluOpType
ACT = mybir.ActivationFunctionType
AX_X = mybir.AxisListType.X
F32 = mybir.dt.float32
U32 = mybir.dt.uint32
I32 = mybir.dt.int32

P = 128
BATCH, SEQ, DM = 2, 2048, 256
DI = 2 * DM
DS = 16
DR = DM // 16
TAPS = 4
HALO = TAPS - 1
TB = 512
NBLK = BATCH * SEQ // TB
SEG = SEQ // TB
NT = TB // P
KD = DM // P
NC = DI // P
GN = 4
NG = DS // GN
UNITS = NC * NG
STEPS = 2 * NBLK
NE = 8
BIG = 3.4e38
EPS = 1e-5
ROWS = 2 * DS


PAIRS = 2 * BATCH * SEQ
TILES = PAIRS // P + NE
T3 = NBLK * NT
UNROLL = 4
FILLS = 9
ROUTE = 8
EARLY = NBLK // 2 - 1
MIDDLE = 2 * EARLY

STEP_USES = (
    [("z", 0, 0), ("z", 1, 1), ("out", 0, 0), ("out", 1, 1)]
    + [("xp", 0, 0), ("xp", 1, 1), ("xp", 2, 0), ("xp", 3, 1), ("z", 2, 0), ("z", 3, 1)]
    + [("xdbl", 0, 0), ("dt", 0, 1), ("dt", 1, 0), ("dt", 2, 1), ("dt", 3, 0)])
XP_AT = [(5, 2), (6, 0), (7, 2), (8, 1)]
OUT_AT = [(3, 0), (3, 2)]
X_AT = [(4, 1), (5, 0), (6, 1), (6, 3)]
STEP_SIZE_AT = [(10, 2), (11, 0), (11, 2), (12, 0)]
Z_AT = [(0, 0), (0, 2), (7, 2), (8, 0)]
ADD_DT_AT = [1, 5, 6]
DT_AT = [(11, 3), (12, 1), (12, 3), (13, 0)]
FIRST_USES = [u for u in STEP_USES if u[0] in ("xp", "xdbl", "dt")]


def uses_of_step(step):
    if step == -1:
        return FIRST_USES
    if step == STEPS:
        return [u for u in STEP_USES if u[0] == "out"]
    own = [u for u in STEP_USES if u[0] in ("out", "z")]
    uses = own if step == STEPS - 1 else STEP_USES
    return [u for u in uses if u[0] != "out"] if step == 0 else uses


def bank_use(step, kind, index):
    bank = [u[2] for u in STEP_USES if u[:2] == (kind, index)][0]
    of_bank = lambda uses: [u[:2] for u in uses if u[2] == bank]
    if isinstance(step, int):
        return bank, (sum(len(of_bank(uses_of_step(k))) for k in range(-1, step))
                      + of_bank(uses_of_step(step)).index((kind, index)))
    mine = of_bank(STEP_USES)
    return bank, len(of_bank(FIRST_USES)) - 1 + len(mine) * step + mine.index((kind, index))


def mixer_and_experts(nc, A, out):
    with ExitStack() as top:
        sem = lambda name: top.enter_context(nc.semaphore(name))
        dram = lambda name, shape: nc.dram_tensor(name, shape, F32, kind="Internal").ap()

        xnT_dram = dram("xnT_scratch", (NBLK, P, KD * TB))
        t_dram = dram("t_scratch", (NBLK, P, NT * DM))
        bc_dram = dram("bc_scratch", (2, 1, ROWS * TB))
        slot_dram = dram("slot_scratch", (TILES * P, DM))
        yslot_dram = dram("yslot_scratch", (TILES * P, DM))
        mod_dram = dram("mod_scratch", (P, BATCH * 4 * DM))

        psum = top.enter_context(nc.psum_tensor("psum", [P, 8, TB], F32))
        keep = lambda name, shape, dt=F32: top.enter_context(nc.sbuf_tensor(name, shape, dt))
        ident = keep("ident", [P, P])

        mix = ExitStack()
        sb2 = lambda name, shape, dt=F32: mix.enter_context(nc.sbuf_tensor(name, shape, dt))
        w_in = sb2("w_in", [P, 2, KD, 2 * DI])
        w_x = sb2("w_x", [P, 2, NC, 48])
        w_dt = sb2("w_dt", [48, 2, DI])
        w_out = sb2("w_out", [P, 2, NC, DM])
        neg_a = sb2("neg_a", [P, 2, NC, DS])
        w_conv = sb2("w_conv", [P, 2, NC, TAPS])
        b_conv = sb2("b_conv", [P, 2, NC])
        b_dt = sb2("b_dt", [P, 2, NC])
        d_skip = sb2("d_skip", [P, 2, NC])
        diag_d = sb2("diag_d", [P, 2, NC, P])
        limits = sb2("limits", [P, NBLK, 2])

        pre = ExitStack()
        sb1 = lambda name, shape, dt=F32: pre.enter_context(nc.sbuf_tensor(name, shape, dt))
        cT = sb1("cT", [P, KD, BATCH])
        c_wide = sb1("c_wide", [P, KD, BATCH, P])
        w_mod = sb1("w_mod", [P, KD, 6 * DM])
        mod = sb1("mod", [P, BATCH, 6, DM])
        mod_abs = sb1("mod_abs", [P, BATCH, DM])
        mod_sign = sb1("mod_sign", [P, BATCH, DM])
        ln_w = sb1("ln_w", [P, KD])
        ln_b = sb1("ln_b", [P, KD])
        X = sb1("X", [P, NBLK * NT, DM])
        H = sb1("H", [P, NBLK * NT, DM])
        stats = sb1("stats", [P, NBLK * NT, 6])
        mv = sb1("mv", [P, 2, NBLK * NT, 2])
        var_eps = sb1("var_eps", [P, 2, NBLK * NT])
        rstd = sb1("rstd", [P, 2, NBLK * NT])
        shift = sb1("shift", [P, NBLK * NT])
        minus_half = sb1("minus_half", [P, SEG * NT])
        xnT_out = sb1("xnT_out", [P, 2, KD, TB])
        zeros = sb1("zeros", [P, TILES // FILLS * DM])
        pre.close()

        xnT = sb2("xnT", [P, 2, KD, TB])
        xc = sb2("xc", [P, 2, NC, TB])
        dt = sb2("dt", [P, 2, NC, TB])
        sp_tmp = sb2("sp_tmp", [P, NC, TB])
        t_blk = sp_tmp[:, 0:2, :].rearrange("p a b -> p (a b)")
        x_dbl = sp_tmp[0:48, NC - 1, :]
        xp = sb2("xp", [P, 2, TB + HALO])
        halo = sb2("halo", [P, 2, NC, HALO])
        limit_now = sb2("limit_now", [P, 2, 2])
        sz = sb2("sz", [P, NC, TB])
        b_wide = sb2("b_wide", [P, 2, DS, TB])
        dbu = sb2("dbu", [P, 2, GN, TB])
        hst = sb2("hst", [P, 4, GN, TB])
        state = sb2("state", [P, 2, UNITS * GN])
        mix.close()
        PS_A, PS_U, PS_Y, PS_P = 0, 4, 5, 6

        ffn = ExitStack()
        sb3 = lambda name, shape, dt_=F32: ffn.enter_context(nc.sbuf_tensor(name, shape, dt_))
        w13 = sb3("w13", [P, NE * KD, 2 * DM])
        w2 = sb3("w2", [P, NE * KD, DM])
        b13 = sb3("b13", [P, NE, 2 * DM])
        b2 = sb3("b2", [P, NE, DM])
        sw1 = sb3("sw1", [P, KD, 2 * DM])
        sw2 = sb3("sw2", [P, KD, 2 * DM])
        sw3 = sb3("sw3", [P, NC, DM])
        gate = sb3("gate", [P, KD, NE])
        fmod = sb3("fmod", [P, BATCH, 4, DM])
        x1 = sb3("x1", [P, T3, DM])
        h2 = sb3("h2", [P, T3, DM])
        flat = h2[:].rearrange("p t d -> p (t d)")
        part = lambda at, n, m: flat[:, at * DM:(at + n * m) * DM].rearrange("p (n d) -> p n d", n=n)
        xt = part(0, 4, 1)
        hx = part(4, 4, 2)
        yt = part(12, 4, 1)
        xtT = part(16, 2, 1)
        hs = part(18, 2, 1)
        hsT = part(20, 2, 1)
        tin = sb3("tin", [P, 2, NT, DM])
        h2T_r = sb3("h2T_r", [P, KD, TB])
        h2T_s = sb3("h2T_s", [P, KD, TB])
        g_silu = sb3("g_silu", [P, 2, TB])
        big = sb3("big", [P, 4, NT * DM])
        send = [big[:, 0, :], big[:, 1, :]] + [tin[:, b].rearrange("p t d -> p (t d)") for b in range(2)]
        yg = w13[:].rearrange("p (r a) n -> p r (a n)", a=2)
        u_sh = big[:, 2:4, :].rearrange("p a (c t) -> p (a c) t", c=2)
        o_tmp = sb3("o_tmp", [P, 2, DM])
        lower = sb3("lower", [P, NE, NE])
        minus_half3 = sb3("minus_half3", [P, NT])
        before = sb3("before", [P, P])
        ones = sb3("ones", [P, P])
        count_i = sb3("count_i", [P, TILES], I32)
        tile_no = sb3("tile_no", [P, TILES])
        fstats = sb3("fstats", [P, NT, 6])
        fmv = sb3("fmv", [P, 2, NT, 2])
        fvar = sb3("fvar", [P, 2, NT])
        frstd = sb3("frstd", [P, 2, NT])
        fmax = sb3("fmax", [P, NT])
        fsum = sb3("fsum", [P, NT])
        score = sb3("score", [P, T3, NE])
        rank = sb3("rank", [P, T3, NE])
        cmp_gt = sb3("cmp_gt", [P, NT, NE, NE])
        cmp_eq = sb3("cmp_eq", [P, NT, NE, NE])
        mask = sb3("mask", [P, T3, NE])
        running = sb3("running", [P, NE, T3])
        place = sb3("place", [P, T3, NE])
        chosen = sb3("chosen", [P, T3, NE])
        picked = sb3("picked", [P, T3, NE])
        weight = sb3("weight", [P, 2, T3])
        slot = sb3("slot", [P, 2, T3])
        slot_u = sb3("slot_u", [P, 2, T3], U32)
        cmp_n = cmp_gt[:].rearrange("p t e f -> p (t e f)").rearrange("p (e t) -> p e t", e=NE)
        n_tiles = sb3("n_tiles", [P, NE])
        n_before = sb3("n_before", [P, NE, NE])
        first_tile = sb3("first_tile", [P, NE])
        end_tile = sb3("end_tile", [P, NE])
        cmp_s = h2T_r[:].rearrange("p k t -> p (k t)")[:, 0:TILES * NE].rearrange("p (s e) -> p s e", e=NE)
        expert = sb3("expert", [P, TILES])
        expert_u = sb3("expert_u", [P, TILES], U32)
        ffn.close()

        phase = sem("phase")
        waited = sem("waited")
        w_loaded = sem("w_loaded")
        x_loaded = [sem("x_loaded0"), sem("x_loaded1")]
        w_mod_loaded = sem("w_mod_loaded")
        consts = sem("consts")
        neg_a_done = sem("neg_a_done")
        diag_done = sem("diag_done")
        w_out_done = sem("w_out_done")
        c_ready = sem("c_ready")
        mod_full = sem("mod_full")
        mod_copied = sem("mod_copied")
        mod_step = sem("mod_step")
        mod_stored = sem("mod_stored")
        p1_stat = sem("p1_stat")
        p1_aggr = sem("p1_aggr")
        p1_var = sem("p1_var")
        p1_rstd = sem("p1_rstd")
        p1_shift = sem("p1_shift")
        p1_first = sem("p1_first")
        p1_norm = sem("p1_norm")
        p1_scaled = sem("p1_scaled")
        h_done = sem("h_done")
        h_stored = sem("h_stored")
        xnT_full = sem("xnT_full")
        xnT_copied = sem("xnT_copied")
        xnT_stored = [sem("xnT_stored0"), sem("xnT_stored1")]
        xnT_loaded = [sem("xnT_loaded0"), sem("xnT_loaded1")]
        bank_full = [sem("bank_full0"), sem("bank_full1")]
        bank_free = [sem("bank_free0"), sem("bank_free1")]
        xp_head = sem("xp_head")
        xp_body = sem("xp_body")
        halo_saved = sem("halo_saved")
        conv_step = sem("conv_step")
        conv_done = sem("conv_done")
        xc_done = sem("xc_done")
        bc_stored = sem("bc_stored")
        rows_loaded = [[sem(f"rows_loaded{k}{g}") for g in range(NG)] for k in range(2)]
        sp_relu = sem("sp_relu")
        sp_exp = sem("sp_exp")
        sp_done = sem("sp_done")
        dt_done = sem("dt_done")
        dtu_done = sem("dtu_done")
        exp_done = sem("exp_done")
        mult_done = sem("mult_done")
        scan_done = sem("scan_done")
        limit_set = sem("limit_set")
        prod_done = sem("prod_done")
        state_saved = sem("state_saved")
        unit_summed = sem("unit_summed")
        yg_done = sem("yg_done")
        t_loaded = sem("t_loaded")
        t_stored = sem("t_stored")
        zeroed = sem("zeroed")
        fills = sem("fills")
        zeros_set = sem("zeros_set")
        f_gate_loaded = sem("f_gate_loaded")
        f_sw_loaded = sem("f_sw_loaded")
        f_w_loaded = sem("f_w_loaded")
        f_const = sem("f_const")
        f_count = sem("f_count")
        f_in = [sem("f_in0"), sem("f_in1")]
        f_x1 = sem("f_x1")
        f_stat = sem("f_stat")
        f_aggr = sem("f_aggr")
        f_var = sem("f_var")
        f_rstd = sem("f_rstd")
        f_norm = sem("f_norm")
        f_scaled = sem("f_scaled")
        f_h2 = sem("f_h2")
        t_full = [sem("t_full0"), sem("t_full1")]
        t_free = [sem("t_free0"), sem("t_free1")]
        f_logits = sem("f_logits")
        f_max = sem("f_max")
        f_shift = sem("f_shift")
        f_exp = sem("f_exp")
        f_route = sem("f_route")
        s_g_full = sem("s_g_full")
        s_u_full = sem("s_u_full")
        s_silu = sem("s_silu")
        s_u = sem("s_u")
        s_o_full = sem("s_o_full")
        s_o_mul = sem("s_o_mul")
        s_x1 = sem("s_x1")
        a_step = sem("a_step")
        a_mask = sem("a_mask")
        a_counted = sem("a_counted")
        a_slots = sem("a_slots")
        a_experts = sem("a_experts")
        scaled = sem("scaled")
        scattered = [sem(f"scattered{r}") for r in range(4)]
        xt_loaded = [sem(f"xt_loaded{r}") for r in range(4)]
        xt_turned = sem("xt_turned")
        xtT_copied = sem("xtT_copied")
        hx_full = sem("hx_full")
        hx_done = sem("hx_done")
        hs_done = sem("hs_done")
        hs_turned = sem("hs_turned")
        hsT_copied = sem("hsT_copied")
        y_full = sem("y_full")
        y_biased = sem("y_biased")
        y_done = sem("y_done")
        y_stored = [sem(f"y_stored{r}") for r in range(4)]
        gathered = [sem(f"gathered{r}") for r in range(8)]
        f_fin = sem("f_fin")
        f_out = sem("f_out")

        block = top.enter_context(nc.Block())

        def meet(eng, n):
            eng.drain().then_inc(phase, 1)
            eng.wait_ge(phase, 5 * n)

        def time_order(ap, backward):
            return ap[:, ::-1] if backward else ap

        def wait_apart(eng):
            eng.sem_inc(waited, 1)

        def filled(eng, S, kind, index):
            bank, before = bank_use(S, kind, index)
            eng.wait_ge(bank_full[bank], before + 1)
            return PS_P + bank

        def drained(eng, S, kind, index):
            bank, before = bank_use(S, kind, index)
            eng.wait_ge(bank_free[bank], before + 1)

        def rows_ready(eng, is_c, g, q):
            eng.wait_ge(rows_loaded[is_c][g], 16 * (q + 1))

        def take_bank(pe, S, kind, index):
            bank, before = bank_use(S, kind, index)
            if not (isinstance(before, int) and before == 0):
                pe.wait_ge(bank_free[bank], before)
            return bank

        def run_steps(eng, step):
            step(0, 0, 0)
            step(0, 1, 1)
            with eng.Fori(1, NBLK - 1) as i:
                step(i, 0, 2 * i)
                step(i, 1, 2 * i + 1)
            step(NBLK - 1, 0, STEPS - 2)
            step(NBLK - 1, 1, STEPS - 1)

        def is_first(q):
            return isinstance(q, int) and q == 0

        def is_last(q):
            return isinstance(q, int) and q == STEPS - 1

        def turn_shared(j):
            return 3 * j + 2 if j < EARLY else 2 * EARLY + 2 + j

        def turn_router(n):
            return 3 * (n // 2) + n % 2

        def router_loop(body):
            for k in range(NBLK // 2):
                body(k)

        def tile_loop(eng, body):
            for s in range(UNROLL):
                body(s, s)
            with eng.Fori(1, TILES // UNROLL - 1) as m:
                for r in range(UNROLL):
                    body(m * UNROLL + r, r)
            for r in range(UNROLL):
                body(TILES - UNROLL + r, r)

        def rows_of(i):
            return bass.ds(i * NT, NT)

        @block.sync
        def _(sp):
            for b in range(BATCH):
                sp.dma_start(X[:, b * SEG * NT:(b + 1) * SEG * NT, :].rearrange("p (k t) d -> p k (t d)", t=NT),
                             A["x"][b * SEG:(b + 1) * SEG].rearrange("k p n -> p k n")).then_inc(x_loaded[b], 16)
                if b == 0:
                    sp.dma_start(w_mod[:], A["w_mod"]).then_inc(w_mod_loaded, 16)
                    sp.dma_start(cT[:], A["cT"]).then_inc(w_mod_loaded, 16)
                    sp.dma_start(ln_w[:], A["ln_w"]).then_inc(w_mod_loaded, 16)
                    sp.dma_start(ln_b[:], A["ln_b"]).then_inc(w_mod_loaded, 16)
            for dst, name in ((neg_a, "a_log"), (w_in, "w_in"), (w_x, "w_x"), (w_out, "w_out"),
                              (w_conv, "w_conv"), (b_conv, "b_conv"), (b_dt, "b_dt"), (d_skip, "d_skip")):
                sp.dma_start(dst[:], A[name]).then_inc(w_loaded, 16)
            sp.dma_start(w_dt[32:48], A["w_dt"]).then_inc(w_loaded, 16)
            sp.wait_ge(zeros_set, 1)
            for f in range(FILLS):
                rows = TILES * P // FILLS
                sp.dma_start(slot_dram[f * rows:(f + 1) * rows, :].rearrange("(p a) d -> p (a d)", p=P), zeros[:]
                             ).then_inc(fills, 16)
            sp.wait_ge(mod_step, 10)
            sp.dma_start(mod_dram, mod[:, :, 2:6, :]).then_inc(mod_stored, 16)
            with sp.Fori(0, NBLK) as k:
                sp.wait_ge(h_done, k + 1)
                sp.dma_start(t_dram[bass.ds(k, 1)].rearrange("k p n -> (k p) n"),
                             H[:, bass.ds(k * NT, NT), :].rearrange("p t d -> p (t d)")).then_inc(h_stored, 16)
            with sp.Fori(0, NBLK // 2) as k:
                for half in range(2):
                    sp.wait_ge(xnT_copied, k * 4 + 2 * half + 2)
                    sp.dma_start(xnT_dram[bass.ds(2 * k + half, 1)].rearrange("k p n -> (k p) n"),
                                 xnT_out[:, half].rearrange("p k t -> p (k t)")).then_inc(xnT_stored[half], 16)
            sp.wait_ge(h_stored, 16 * NBLK)
            sp.wait_ge(mod_stored, 16)
            sp.wait_ge(w_loaded, 16 * 9)
            sp.wait_ge(fills, 16 * FILLS)
            for half in range(2):
                sp.wait_ge(xnT_stored[half], 16 * NBLK // 2)
            meet(sp, 1)

            def block_of(i, D):
                if D == 0:
                    return i
                return (i // SEG) * SEG + (SEG - 1 - i % SEG)

            def load_xnT(i, D):
                wait_apart(sp)
                sp.dma_start(xnT[:, D].rearrange("p k t -> p (k t)"),
                             xnT_dram[bass.ds(block_of(i, D), 1)].rearrange("k p n -> (k p) n")
                             ).then_inc(xnT_loaded[D], 16)

            def store_rows(q, D):
                drained(sp, q - 1, "xdbl", 0)
                sp.dma_start(bc_dram[D].rearrange("a (r t) -> (a r) t", r=ROWS), x_dbl[0:ROWS, :]
                             ).then_inc(bc_stored, 16)

            def spread_rows(is_c, g, q, D):
                if g == 0 and not is_c:
                    sp.wait_ge(bc_stored, 16 * (q + 1))
                    wait_apart(sp)
                if not is_first(q):
                    sp.wait_ge(prod_done if is_c else mult_done, UNITS * (q - 1) + UNITS - NG + g + 1)
                at = (DS * is_c + GN * g) * TB
                sp.dma_start(b_wide[:, is_c, g * GN:(g + 1) * GN, :].rearrange("p n t -> p (n t)"),
                             bc_dram[D, :, at:at + GN * TB].broadcast_to((P, GN * TB))
                             ).then_inc(rows_loaded[is_c][g], 16)

            def spread_first_rows(q, D):
                store_rows(q, D)
                for is_c, g in ((0, 0), (0, 1), (0, 2), (1, 0), (0, 3), (1, 1)):
                    spread_rows(is_c, g, q, D)

            def load_sum(i, D, q):
                if not is_first(q):
                    sp.wait_ge(t_stored, 16 * q)
                    wait_apart(sp)
                sp.wait_ge(dt_done, NC * (q + 1) + (0 if is_last(q) else 2))
                wait_apart(sp)
                sp.dma_start(t_blk, t_dram[bass.ds(block_of(i, D), 1)].rearrange("k p n -> (k p) n")
                             ).then_inc(t_loaded, 16)

            def store_sum(i, D, q):
                drained(sp, q + 1, "out", 1)
                wait_apart(sp)
                sp.dma_start(t_dram[bass.ds(block_of(i, D), 1)].rearrange("k p n -> (k p) n"), t_blk
                             ).then_inc(t_stored, 16)

            load_xnT(0, 0)
            load_xnT(0, 1)
            spread_first_rows(0, 0)

            def step(i, D, q):
                before = (i if D else i - 1, 1 - D, q - 1)
                for g in (2, 3):
                    spread_rows(1, g, q, D)
                if not is_first(q):
                    load_sum(*before)
                    store_sum(*before)
                if not is_last(q):
                    spread_first_rows(q + 1, 1 - D)
                if not (isinstance(q, int) and q + 2 >= STEPS):
                    filled(sp, q, "z", 3)
                    load_xnT(i + 1, D)

            run_steps(sp, step)
            load_sum(NBLK - 1, 1, STEPS - 1)
            store_sum(NBLK - 1, 1, STEPS - 1)
            sp.wait_ge(t_stored, 16 * STEPS)
            meet(sp, 2)

            for dst, name in ((gate, "gate"), (fmod, None)):
                sp.dma_start(dst[:], mod_dram if name is None else A[name]).then_inc(f_gate_loaded, 16)

            def load_block(n, half):
                sp.dma_start(x1[:, rows_of(n), :].rearrange("p t d -> p (t d)"),
                             A["x"][bass.ds(n, 1)].rearrange("k p n -> (k p) n")).then_inc(f_in[half], 16)
                sp.dma_start(tin[:, half].rearrange("p t d -> p (t d)"),
                             t_dram[bass.ds(n, 1)].rearrange("k p n -> (k p) n")).then_inc(f_in[half], 16)

            load_block(0, 0)
            load_block(1, 1)
            for dst, name in ((sw1, "sw1"), (sw2, "sw2"), (sw3, "sw3")):
                sp.dma_start(dst[:], A[name]).then_inc(f_sw_loaded, 16)
            with sp.Fori(1, NBLK // 2) as k:
                for half in range(2):
                    sp.wait_ge(f_x1, 4 * k + 2 * half - 2)
                    wait_apart(sp)
                    load_block(2 * k + half, half)
            for dst, name in ((w13, "w13"), (b13, "b13"), (w2, "w2"), (b2, "b2")):
                src = A[name].broadcast_to((P, A[name].shape[1])) if name in ("b13", "b2") else A[name]
                flat_dst = dst[:].rearrange("p a b -> p (a b)")
                sp.dma_start(flat_dst, src).then_inc(f_w_loaded, 16)

            def load_tile(s, r):
                sp.dma_start(xt[:, r, :], slot_dram[bass.ds(s * P, P)]).then_inc(xt_loaded[r], 16)

            def store_tile(s, r):
                sp.wait_ge(y_done, s + 1)
                wait_apart(sp)
                sp.dma_start(yslot_dram[bass.ds(s * P, P)], yt[:, r, :]).then_inc(y_stored[r], 16)

            for r in range(4):
                sp.wait_ge(scattered[r], 16 * NT * 2 * NBLK // 4)
            for kd in range(KD):
                sp.wait_ge(t_full[kd], turn_shared(MIDDLE - 1) + 1)
            for s in range(4):
                load_tile(s, s)

            def tiles(s, r):
                if not (isinstance(s, int) and s + 4 >= TILES):
                    sp.wait_ge(xt_turned, s + 1)
                    wait_apart(sp)
                    load_tile(s + 4, r)
                if not (isinstance(s, int) and s < 2):
                    store_tile(s - 2, (r + 2) % 4)

            tile_loop(sp, tiles)
            store_tile(TILES - 2, 2)
            store_tile(TILES - 1, 3)
            with sp.Fori(0, NBLK) as i:
                sp.wait_ge(f_fin, 3 * i + 3)
                wait_apart(sp)
                sp.dma_start(out[bass.ds(i, 1)].rearrange("k p n -> (k p) n"),
                             x1[:, rows_of(i), :].rearrange("p t d -> p (t d)")).then_inc(f_out, 16)
            sp.wait_ge(f_out, 16 * NBLK)

        @block.gpsimd
        def _(pool):
            nc.gpsimd.memset(ident[:], 0.0).then_inc(consts, 1)
            nc.gpsimd.memset(minus_half[:], -0.5).then_inc(consts, 1)
            pool.wait_ge(consts, 2)
            nc.gpsimd.affine_select(out=ident[:], in_=ident[:], compare_op=ALU.not_equal, fill=1.0,
                                    base=0, pattern=[[-1, P]], channel_multiplier=1).then_inc(consts, 1)
            nc.gpsimd.memset(zeros[:], 0.0).then_inc(zeros_set, 1)
            for k in range(NBLK):
                bound = 0.0 if k % SEG == SEG - 1 else BIG
                nc.gpsimd.memset(limits[:, k, 0:1], bound).then_inc(consts, 1)
                nc.gpsimd.memset(limits[:, k, 1:2], -bound).then_inc(consts, 1)
            pool.wait_ge(consts, 3 + 2 * NBLK)

            span = SEG * NT

            def power(ln, b):
                pool.wait_ge(p1_var, ln * BATCH + b + 1)
                nc.gpsimd.tensor_tensor(rstd[:, ln, b * span:(b + 1) * span],
                                        var_eps[:, ln, b * span:(b + 1) * span], minus_half[:],
                                        ALU.pow).then_inc(p1_rstd, 1)

            for b in range(BATCH):
                power(0, b)
            for b in range(BATCH):
                with pool.Fori(0, SEG) as s:
                    pool.wait_ge(p1_scaled, s + (b * SEG + 1))
                    Hb = H[:, bass.ds(s * NT + b * span, NT), :]
                    nc.gpsimd.tensor_tensor(Hb, Hb, mod[:, b, 0:1, :].broadcast_to((P, NT, DM)),
                                            ALU.add).then_inc(h_done, 1)
            for b in range(BATCH):
                power(1, b)
            meet(pool, 1)

            nc.gpsimd.memset(state[:], 0.0).then_inc(zeroed, 1)
            nc.gpsimd.memset(halo[:], 0.0).then_inc(zeroed, 1)

            def set_limit(i, D):
                nc.gpsimd.tensor_copy(limit_now[:, D:D + 1, :], limits[:, bass.ds(i, 1), :]).then_inc(limit_set, 1)

            def clamp(dst, src, D, signal):
                nc.gpsimd.tensor_scalar(dst, src, limit_now[:, D, 0:1], limit_now[:, D, 1:2],
                                        ALU.min, ALU.max).then_inc(signal, 1)

            def save_halo(c, D, q):
                pool.wait_ge(limit_set, q + 1)
                drained(pool, q - 1, "xp", c)
                wait_apart(pool)
                edge = slice(TB, TB + HALO) if D == 0 else slice(0, HALO)
                clamp(halo[:, D, c, :], xp[:, c % 2, edge], D, halo_saved)

            def add_dt(c, D, q):
                pool.wait_ge(sp_done, q + 1)
                nc.gpsimd.tensor_tensor(dt[:, D, c, :], dt[:, D, c, :], sp_tmp[:, c, :],
                                        ALU.add).then_inc(dt_done, 1)

            def unit(u, D, q):
                g = u % NG
                U = UNITS * q + u
                last = TB - 1 if D == 0 else 0
                h = hst[:, u % 4, :, :]
                pool.wait_ge(scan_done, GN * U + GN)
                wait_apart(pool)
                clamp(state[:, D, u * GN:(u + 1) * GN].rearrange("p (a b) -> p a b", b=1),
                      h[:, :, last:last + 1], D, state_saved)
                rows_ready(pool, 1, g, q)
                pool.wait_ge(state_saved, U + 1)
                nc.gpsimd.tensor_tensor(h, h, b_wide[:, 1, g * GN:(g + 1) * GN, :],
                                        ALU.mult).then_inc(prod_done, 1)

            set_limit(0, 0)
            pool.wait_ge(zeroed, 2)
            for c in range(NC):
                save_halo(c, 0, 0)
            for c in range(NC):
                add_dt(c, 0, 0)

            def step(i, D, q):
                for t in range(UNITS):
                    ahead = not is_last(q)
                    if ahead and t == 2:
                        set_limit(i + D, 1 - D)
                    if ahead and t in (6, 7, 8, 9):
                        save_halo(t - 6, 1 - D, q + 1)
                    if t in ADD_DT_AT and not is_first(q):
                        add_dt(1 + ADD_DT_AT.index(t), D, q)
                    if t > 0:
                        unit(t - 1, D, q)
                    elif not is_first(q):
                        unit(UNITS - 1, 1 - D, q - 1)
                    if ahead and t == 14:
                        add_dt(0, 1 - D, q + 1)

            run_steps(pool, step)
            unit(UNITS - 1, 1, STEPS - 1)
            meet(pool, 2)

            nc.gpsimd.memset(minus_half3[:], -0.5).then_inc(f_const, 1)
            nc.gpsimd.memset(lower[:], 1.0).then_inc(f_const, 1)
            nc.gpsimd.memset(before[:], 1.0).then_inc(f_const, 1)
            nc.gpsimd.memset(ones[:], 1.0).then_inc(f_const, 1)
            pool.wait_ge(f_const, 4)
            nc.gpsimd.affine_select(out=lower[:], in_=lower[:], compare_op=ALU.is_gt, fill=0.0, base=0,
                                    pattern=[[1, NE], [-1, NE]], channel_multiplier=0).then_inc(f_const, 1)
            nc.gpsimd.affine_select(out=before[:], in_=before[:], compare_op=ALU.is_gt, fill=0.0, base=0,
                                    pattern=[[1, P]], channel_multiplier=-1).then_inc(f_const, 1)
            nc.gpsimd.iota(count_i[:], pattern=[[1, TILES]], base=0, channel_multiplier=0).then_inc(f_count, 1)
            pool.wait_ge(f_count, 1)
            nc.gpsimd.tensor_copy(tile_no[:], count_i[:]).then_inc(f_const, 1)
            pool.wait_ge(f_gate_loaded, 32)

            def norm_power(n, half):
                pool.wait_ge(f_var, n + 1)
                nc.gpsimd.tensor_tensor(frstd[:, half], fvar[:, half], minus_half3[:], ALU.pow).then_inc(f_rstd, 1)

            def norm_shift(n):
                pool.wait_ge(f_scaled, n + 1)
                wait_apart(pool)
                nc.gpsimd.tensor_tensor(h2[:, rows_of(n), :], h2[:, rows_of(n), :],
                                        fmod[:, bass.ds(n // SEG, 1), 1:2, :].rearrange(
                                            "p a b d -> p (a b) d").broadcast_to((P, NT, DM)),
                                        ALU.add).then_inc(f_h2, 1)

            def route(k):
                norm_shift(2 * k)
                norm_power(2 * k + 1, 1)
                norm_shift(2 * k + 1)
                if not (isinstance(k, int) and k == NBLK // 2 - 1):
                    norm_power(2 * k + 2, 0)

            norm_power(0, 0)
            router_loop(route)

            for k in range(2):
                pool.wait_ge(a_slots, k + 1)
                for i in range(NBLK):
                    r = i % 4
                    pool.wait_ge(scaled, NBLK * k + i + 1)
                    for tt in range(NT):
                        nc.gpsimd.indirect_dma_start(
                            slot_dram, bass.IndirectOffsetOnAxis(ap=slot_u[:, k, i * NT + tt:i * NT + tt + 1], axis=0),
                            send[r][:, tt * DM:(tt + 1) * DM], None).then_inc(scattered[r], 16)

            def tiles(s, r):
                pool.wait_ge(y_biased, s + 1)
                nc.gpsimd.tensor_tensor(yt[:, r, :], yt[:, r, :], hx[:, r, DM:2 * DM], ALU.mult).then_inc(y_done, 1)

            tile_loop(pool, tiles)

            for r in range(4):
                pool.wait_ge(y_stored[r], 16 * TILES // 4)
            for i in range(NBLK):
                for k in range(2):
                    r = 2 * (i % 4) + k
                    if i > 3:
                        pool.wait_ge(f_fin, 3 * (i - 3))
                    for tt in range(NT):
                        nc.gpsimd.indirect_dma_start(
                            yg[:, r, tt * DM:(tt + 1) * DM], None, yslot_dram,
                            bass.IndirectOffsetOnAxis(ap=slot_u[:, k, i * NT + tt:i * NT + tt + 1], axis=0)
                        ).then_inc(gathered[r], 16)

        @block.scalar
        def _(act):
            act.wait_ge(w_mod_loaded, 16 * 4)
            for k in range(KD):
                for b in range(BATCH):
                    nc.scalar.activation(c_wide[:, k, b, :], cT[:, k, b:b + 1].broadcast_to((P, P)),
                                         ACT.Silu).then_inc(c_ready, 1)
            for b in range(BATCH):
                for j in range(3):
                    act.wait_ge(mod_full, 3 * b + j + 1)
                    nc.scalar.activation(mod[:, b, 2 * j:2 * j + 2, :].rearrange("p a d -> p (a d)"),
                                         psum[:, 3 * b + j, :], ACT.Copy).then_inc(mod_copied, 1)
            for b in range(BATCH):
                act.wait_ge(p1_shift, b + 1)
                with act.Fori(0, SEG * NT) as t:
                    tile = bass.ds(t + b * SEG * NT, 1)
                    nc.scalar.activation(H[:, tile, :].rearrange("p a n -> p (a n)"),
                                         X[:, tile, :].rearrange("p a n -> p (a n)"), ACT.Identity,
                                         scale=rstd[:, 0, tile], bias=shift[:, tile]).then_inc(p1_first, 1)
            act.wait_ge(w_loaded, 16 * 9)
            nc.scalar.activation(neg_a[:], neg_a[:], ACT.Exp).then_inc(neg_a_done, 1)
            act.wait_ge(consts, 3)
            for D in range(2):
                for c in range(NC):
                    nc.scalar.activation(diag_d[:, D, c, :], ident[:], ACT.Copy, scale=d_skip[:, D, c:c + 1]
                                         ).then_inc(diag_done, 1)

            def copy_xnT(k):
                for half in range(2):
                    for kd in range(KD):
                        act.wait_ge(xnT_full, k * 4 + 2 * half + kd + 1)
                        if not isinstance(k, int):
                            act.wait_ge(xnT_stored[half], 16 * k)
                        nc.scalar.activation(xnT_out[:, half, kd, :], psum[:, 2 * half + kd, :], ACT.Identity,
                                             scale=ln_w[:, kd:kd + 1], bias=ln_b[:, kd:kd + 1]
                                             ).then_inc(xnT_copied, 1)

            copy_xnT(0)
            with act.Fori(1, NBLK // 2) as k:
                copy_xnT(k)
            meet(act, 1)

            def copy_xp(c, D, q):
                if not (isinstance(q, int) and q == 0 and c < 2):
                    act.wait_ge(conv_done, NC * q + c - 1)
                    act.wait_ge(halo_saved, NC * q + c - 1)
                if c == 0 and not (isinstance(q, int) and q < 2):
                    filled(act, q - 1, "out", 1)
                edge = slice(0, HALO) if D == 0 else slice(TB, TB + HALO)
                body_ = slice(HALO, HALO + TB) if D == 0 else slice(0, TB)
                nc.scalar.activation(xp[:, c % 2, edge], halo[:, D, c, :], ACT.Copy).then_inc(xp_head, 1)
                bank = filled(act, q - 1, "xp", c)
                nc.scalar.activation(xp[:, c % 2, body_], psum[:, bank, :], ACT.Copy).then_inc(xp_body, 1)
                nc.scalar.activation(xc[:, D, c, :], psum[:, bank, :], ACT.Copy,
                                     scale=w_conv[:, D, c, HALO:TAPS]).then_inc(bank_free[bank - PS_P], 1)

            def silu_z(c, q):
                if not is_first(q):
                    act.wait_ge(yg_done, NC * (q - 1) + c + 1)
                bank = filled(act, q, "z", c)
                nc.scalar.activation(sz[:, c, :], psum[:, bank, :], ACT.Silu).then_inc(bank_free[bank - PS_P], 1)

            def silu_xc(c, D, q):
                act.wait_ge(conv_done, NC * q + c + 1)
                nc.scalar.activation(xc[:, D, c, :], xc[:, D, c, :], ACT.Silu,
                                     bias=b_conv[:, D, c:c + 1]).then_inc(xc_done, 1)

            def copy_x_dbl(q):
                if not is_first(q):
                    act.wait_ge(dt_done, NC * q)
                bank = filled(act, q - 1, "xdbl", 0)
                nc.scalar.activation(x_dbl, psum[0:48, bank, :], ACT.Copy).then_inc(bank_free[bank - PS_P], 1)

            def softplus(c, D, q):
                if c == 0 and not is_first(q):
                    act.wait_ge(dt_done, NC * q)
                if c == 0 and not (isinstance(q, int) and q < 2):
                    act.wait_ge(t_stored, 16 * (q - 1))
                if c == NC - 1:
                    act.wait_ge(bc_stored, 16 * (q + 1))
                bank = filled(act, q - 1, "dt", c)
                nc.scalar.activation(dt[:, D, c, :], psum[:, bank, :], ACT.Relu,
                                     bias=b_dt[:, D, c:c + 1]).then_inc(sp_relu, 1)
                nc.scalar.activation(sp_tmp[:, c, :], psum[:, bank, :], ACT.Abs,
                                     bias=b_dt[:, D, c:c + 1]).then_inc(bank_free[bank - PS_P], 1)
                drained(act, q - 1, "dt", c)
                nc.scalar.activation(sp_tmp[:, c, :], sp_tmp[:, c, :], ACT.Exp, scale=-1.0).then_inc(sp_exp, 1)

            def softplus_log(q):
                act.wait_ge(sp_exp, NC * (q + 1))
                nc.scalar.activation(sp_tmp[:], sp_tmp[:], ACT.Ln, bias=1.0).then_inc(sp_done, 1)

            def decay(u, n, D, q):
                c, g = divmod(u, NG)
                K = GN * (UNITS * q + u) + n
                if g == 0 and n == 0:
                    act.wait_ge(dt_done, NC * q + c + 1)
                if not (isinstance(K, int) and K < GN):
                    act.wait_ge(scan_done, K - GN + 1)
                nc.scalar.activation(psum[:, PS_A + n, :], dt[:, D, c, :], ACT.Exp,
                                     scale=neg_a[:, D, c, g * GN + n:g * GN + n + 1]).then_inc(exp_done, 1)

            act.wait_ge(zeroed, 2)
            for c in range(NC):
                copy_xp(c, 0, 0)
            for c in range(NC):
                silu_xc(c, 0, 0)
            copy_x_dbl(0)
            for c in range(NC):
                softplus(c, 0, 0)
            softplus_log(0)

            def step(i, D, q):
                for t in range(UNITS):
                    for n in range(GN):
                        decay(t, n, D, q)
                        if (t, n) in ((2, 3), (9, 3)):
                            for c in range(2):
                                silu_z(2 * (t == 9) + c, q)
                        if is_last(q):
                            continue
                        if (t, n) in ((7, 3), (9, 3)):
                            for c in range(2):
                                silu_xc(t - 7 + c, 1 - D, q + 1)
                        if (t, n) in XP_AT:
                            copy_xp(XP_AT.index((t, n)), 1 - D, q + 1)
                        if (t, n) == (11, 1):
                            copy_x_dbl(q + 1)
                        if (t, n) in DT_AT:
                            softplus(DT_AT.index((t, n)), 1 - D, q + 1)
                        if (t, n) == (13, 3):
                            softplus_log(q + 1)

            run_steps(act, step)
            meet(act, 2)

            def copy_turned(dst, use):
                for kd in range(KD):
                    act.wait_ge(t_full[kd], use + 1)
                    nc.scalar.activation(dst[:, kd, :], psum[:, kd, :], ACT.Copy).then_inc(t_free[kd], 1)

            def turned_router(n):
                if not (isinstance(n, int) and n == 0):
                    act.wait_ge(f_logits, n)
                copy_turned(h2T_r, turn_router(n))

            def turned_shared(j):
                if not (isinstance(j, int) and j == 0):
                    act.wait_ge(s_u_full, NC * j)
                copy_turned(h2T_s, turn_shared(j))

            def exp_scores(n):
                act.wait_ge(f_shift, n + 1)
                nc.scalar.activation(score[:, rows_of(n), :], score[:, rows_of(n), :], ACT.Exp).then_inc(f_exp, 1)

            def silu_shared(c, j):
                act.wait_ge(s_g_full, NC * j + c + 1)
                if not (isinstance(j, int) and j == 0 and c < 2):
                    act.wait_ge(s_u, NC * j + c - 1)
                nc.scalar.activation(g_silu[:, c % 2, :], psum[:, 3 + c % 2, :], ACT.Silu).then_inc(s_silu, 1)

            def route(k):
                shared = not (isinstance(k, int) and k == 0)
                for half in range(2):
                    if shared:
                        if half == 0:
                            turned_shared(k - 1)
                        silu_shared(2 * half, k - 1)
                        silu_shared(2 * half + 1, k - 1)
                    turned_router(2 * k + half)
                    exp_scores(2 * k + half)

            router_loop(route)
            for j in range(EARLY, MIDDLE):
                turned_shared(j)
                for c in range(NC):
                    silu_shared(c, j)

            def copy_tile(s, r):
                act.wait_ge(xt_turned, s + 1)
                if not (isinstance(s, int) and s < 2):
                    act.wait_ge(hx_full, s - 1)
                nc.scalar.activation(xtT[:, r % 2, :], psum[:, r % 2, 0:DM], ACT.Copy).then_inc(xtT_copied, 1)

            def silu_tile(s, r):
                act.wait_ge(hx_done, s + 1)
                if not (isinstance(s, int) and s < 2):
                    act.wait_ge(hs_turned, s - 1)
                nc.scalar.activation(hs[:, r % 2, :], hx[:, r, 0:DM], ACT.Silu).then_inc(hs_done, 1)

            def copy_hidden(s, r):
                act.wait_ge(hs_turned, s + 1)
                if not (isinstance(s, int) and s < 2):
                    act.wait_ge(y_full, s - 1)
                nc.scalar.activation(hsT[:, r % 2, :], psum[:, 4 + r % 2, 0:DM], ACT.Copy).then_inc(hsT_copied, 1)

            def tiles(s, r):
                if not (isinstance(s, int) and s == 0):
                    copy_hidden(s - 1, (r + 3) % 4)
                if not (isinstance(s, int) and s == TILES - 1):
                    copy_tile(s + 1, (r + 1) % 4)
                silu_tile(s, r)

            copy_tile(0, 0)
            tile_loop(act, tiles)
            copy_hidden(TILES - 1, 3)
            for j in range(MIDDLE, NBLK):
                turned_shared(j)
                for c in range(NC):
                    silu_shared(c, j)

        @block.vector
        def _(dve):
            span = SEG * NT

            def statistics(src, ln, b, ready):
                with dve.Fori(0, SEG) as s:
                    for tt in range(NT):
                        tile = s * NT + (b * span + tt)
                        if ready is not None and tt == 0:
                            dve.wait_ge(ready, s + (b * SEG + 1))
                        nc.vector.bn_stats(stats[:, bass.ds(tile, 1), :].rearrange("p a n -> p (a n)"),
                                           src[:, bass.ds(tile, 1), :].rearrange("p a n -> p (a n)")
                                           ).then_inc(p1_stat, 1)
                dve.wait_ge(p1_stat, span * (ln * BATCH + b + 1))
                for tile in range(b * span, (b + 1) * span):
                    nc.vector.bn_aggr(mv[:, ln, tile, :], stats[:, tile, :]).then_inc(p1_aggr, 1)
                dve.wait_ge(p1_aggr, span * (ln * BATCH + b + 1))
                nc.vector.tensor_scalar(var_eps[:, ln, b * span:(b + 1) * span],
                                        mv[:, ln, b * span:(b + 1) * span, 1], EPS, None, ALU.add
                                        ).then_inc(p1_var, 1)

            def normalise(dst, src, ln, tile):
                nc.vector.tensor_scalar(dst[:, bass.ds(tile, 1), :].rearrange("p a n -> p (a n)"),
                                        src[:, bass.ds(tile, 1), :].rearrange("p a n -> p (a n)"),
                                        mv[:, ln, bass.ds(tile, 1), 0:1].rearrange("p a n -> p (a n)"),
                                        rstd[:, ln, bass.ds(tile, 1)],
                                        ALU.subtract, ALU.mult).then_inc(p1_norm, 1)

            dve.wait_ge(x_loaded[0], 16)
            statistics(X, 0, 0, None)
            dve.wait_ge(mod_copied, 6)
            for j in (1, 4):
                nc.vector.tensor_scalar(mod[:, :, j, :], mod[:, :, j, :], 1.0, None, ALU.add).then_inc(mod_step, 1)
            for n, j in enumerate((2, 5)):
                nc.vector.tensor_scalar(mod_abs[:], mod[:, :, j, :], -1.0, 0.25, ALU.mult, ALU.max
                                        ).then_inc(mod_step, 1)
                nc.vector.tensor_scalar(mod_sign[:], mod[:, :, j, :], 0.0, 2.0, ALU.is_ge, ALU.mult
                                        ).then_inc(mod_step, 1)
                dve.wait_ge(mod_step, 2 + 4 * n + 2)
                nc.vector.tensor_tensor(mod_abs[:], mod_abs[:], mod[:, :, j, :], ALU.max).then_inc(mod_step, 1)
                dve.wait_ge(mod_step, 2 + 4 * n + 3)
                nc.vector.scalar_tensor_tensor(mod[:, :, j, :], mod_sign[:], -1.0, mod_abs[:], ALU.add, ALU.mult
                                               ).then_inc(mod_step, 1)
                dve.wait_ge(mod_step, 2 + 4 * n + 4)
            dve.wait_ge(x_loaded[1], 16)
            for b in range(BATCH):
                if b == 1:
                    statistics(X, 0, 1, None)
                dve.wait_ge(p1_rstd, b + 1)
                part = slice(b * span, (b + 1) * span)
                nc.vector.scalar_tensor_tensor(shift[:, part], mv[:, 0, part, 0], -1.0, rstd[:, 0, part],
                                               ALU.mult, ALU.mult).then_inc(p1_shift, 1)
            for b in range(BATCH):
                with dve.Fori(0, SEG) as s:
                    dve.wait_ge(p1_first, s * NT + (b * span + NT))
                    Hb = H[:, bass.ds(s * NT + b * span, NT), :]
                    nc.vector.tensor_tensor(Hb, Hb, mod[:, b, 1:2, :].broadcast_to((P, NT, DM)),
                                            ALU.mult).then_inc(p1_scaled, 1)
            dve.wait_ge(w_loaded, 16 * 9)
            dve.wait_ge(neg_a_done, 1)
            nc.vector.tensor_scalar(neg_a[:], neg_a[:], -1.0, None, ALU.mult).then_inc(w_out_done, 1)
            nc.vector.tensor_scalar(w_out[:], w_out[:], 0.5, None, ALU.mult).then_inc(w_out_done, 1)
            for b in range(BATCH):
                statistics(H, 1, b, h_done)
            for b in range(BATCH):
                dve.wait_ge(p1_rstd, BATCH + b + 1)
                with dve.Fori(0, SEG) as s:
                    for tt in range(NT):
                        normalise(X, H, 1, s * NT + (b * span + tt))
            meet(dve, 1)

            def conv(c, D, q):
                S = q - 1
                drained(dve, S, "xp", c)
                src = xp[:, c % 2, :]
                dst = xc[:, D, c, :]
                for j in range(HALO):
                    at = j if D == 0 else HALO - j
                    if j > 0:
                        dve.wait_ge(conv_step, (HALO - 1) * (NC * q + c) + j)
                    nc.vector.scalar_tensor_tensor(dst, src[:, at:at + TB], w_conv[:, D, c, j:j + 1], dst,
                                                   ALU.mult, ALU.add
                                                   ).then_inc(conv_step if j < HALO - 1 else conv_done, 1)

            def gate_y(c, D, q):
                dve.wait_ge(unit_summed, UNITS * q + NG * (c + 1))
                drained(dve, q, "z", c)
                nc.vector.tensor_tensor(xc[:, D, c, :], psum[:, PS_Y, :], sz[:, c, :], ALU.mult
                                        ).then_inc(yg_done, 1)

            def add_out(b, S):
                if b == 0:
                    dve.wait_ge(t_loaded, 16 * S)
                bank = filled(dve, S, "out", b)
                dst = t_blk[:, b * TB:(b + 1) * TB]
                nc.vector.tensor_tensor(dst, dst, psum[:, bank, :], ALU.add).then_inc(bank_free[bank - PS_P], 1)

            def multiply(u, D, q):
                c, g = divmod(u, NG)
                U = UNITS * q + u
                if g == 0:
                    dve.wait_ge(dt_done, NC * q + c + 1)
                    dve.wait_ge(xc_done, NC * q + c + 1)
                    if not (isinstance(U, int) and U == 0):
                        dve.wait_ge(mult_done, U)
                    nc.vector.tensor_tensor(psum[:, PS_U, :], dt[:, D, c, :], xc[:, D, c, :], ALU.mult
                                            ).then_inc(dtu_done, 1)
                    dve.wait_ge(dtu_done, NC * q + c + 1)
                rows_ready(dve, 0, g, q)
                if not (isinstance(U, int) and U < 2):
                    dve.wait_ge(scan_done, GN * (U - 1))
                nc.vector.tensor_tensor(dbu[:, u % 2, :, :],
                                        psum[:, PS_U:PS_U + 1, :].broadcast_to((P, GN, TB)),
                                        b_wide[:, 0, g * GN:(g + 1) * GN, :], ALU.mult).then_inc(mult_done, 1)

            def scans(u, D, q):
                U = UNITS * q + u
                dve.wait_ge(mult_done, U + 1)
                if not (isinstance(U, int) and U < 4):
                    dve.wait_ge(unit_summed, U - 3)
                for n in range(GN):
                    dve.wait_ge(exp_done, GN * U + n + 1)
                    nc.vector.tensor_tensor_scan(
                        time_order(hst[:, u % 4, n, :], D), time_order(psum[:, PS_A + n, :], D),
                        time_order(dbu[:, u % 2, n, :], D), state[:, D, u * GN + n:u * GN + n + 1],
                        ALU.mult, ALU.add).then_inc(scan_done, 1)

            dve.wait_ge(zeroed, 2)
            for c in range(NC):
                conv(c, 0, 0)
            multiply(0, 0, 0)

            def step(i, D, q):
                for t in range(UNITS):
                    if t == 2 and not is_first(q):
                        gate_y(3, 1 - D, q - 1)
                    if t == 10:
                        gate_y(1, D, q)
                    if t + 1 < UNITS:
                        multiply(t + 1, D, q)
                    elif not is_last(q):
                        multiply(0, 1 - D, q + 1)
                    if t == 4 and not is_first(q):
                        add_out(1, q)
                    if t in (6, 14):
                        gate_y(t // 4 - 1, D, q)
                    scans(t, D, q)
                    if t == 3 and not is_first(q):
                        add_out(0, q)
                    if is_last(q):
                        continue
                    if 5 <= t < 9:
                        conv(t - 5, 1 - D, q + 1)

            run_steps(dve, step)
            gate_y(3, 1, STEPS - 1)
            for b in range(2):
                add_out(b, STEPS)
            meet(dve, 2)

            def row(n, j, count):
                return fmod[:, bass.ds(n // SEG, 1), j:j + 1, :].rearrange(
                    "p a b d -> p (a b) d").broadcast_to((P, count, DM))

            def norm_statistics(n, k, half):
                dve.wait_ge(f_in[half], 32 * k + 32)
                block_x1 = x1[:, rows_of(n), :]
                nc.vector.tensor_tensor(tin[:, half], tin[:, half], row(n, 0, NT), ALU.mult).then_inc(f_x1, 1)
                dve.wait_ge(f_x1, 2 * n + 1)
                nc.vector.tensor_tensor(block_x1, block_x1, tin[:, half], ALU.add).then_inc(f_x1, 1)
                dve.wait_ge(f_x1, 2 * n + 2)
                for tt in range(NT):
                    nc.vector.bn_stats(fstats[:, tt, :], x1[:, bass.ds(n * NT + tt, 1), :].rearrange(
                        "p a d -> p (a d)")).then_inc(f_stat, 1)
                dve.wait_ge(f_stat, NT * n + NT)
                wait_apart(dve)
                for tt in range(NT):
                    nc.vector.bn_aggr(fmv[:, half, tt, :], fstats[:, tt, :]).then_inc(f_aggr, 1)
                dve.wait_ge(f_aggr, NT * n + NT)
                nc.vector.tensor_scalar(fvar[:, half], fmv[:, half, :, 1], EPS, None, ALU.add).then_inc(f_var, 1)

            def norm_apply(n, half):
                dve.wait_ge(f_rstd, n + 1)
                for tt in range(NT):
                    tile = bass.ds(n * NT + tt, 1)
                    nc.vector.tensor_scalar(h2[:, tile, :].rearrange("p a d -> p (a d)"),
                                            x1[:, tile, :].rearrange("p a d -> p (a d)"),
                                            fmv[:, half, tt, 0:1], frstd[:, half, tt:tt + 1],
                                            ALU.subtract, ALU.mult).then_inc(f_norm, 1)
                dve.wait_ge(f_norm, NT * n + NT)
                nc.vector.tensor_tensor(h2[:, rows_of(n), :], h2[:, rows_of(n), :], row(n, 2, NT), ALU.mult
                                        ).then_inc(f_scaled, 1)

            def shift_logits(n):
                dve.wait_ge(f_logits, n + 1)
                logits = psum[:, 2, 0:NT * NE].rearrange("p (t e) -> p t e", t=NT)
                nc.vector.tensor_reduce(fmax[:], logits, axis=AX_X, op=ALU.max).then_inc(f_max, 1)
                dve.wait_ge(f_max, n + 1)
                nc.vector.tensor_tensor(score[:, rows_of(n), :], logits,
                                        fmax[:].rearrange("p (t a) -> p t a", a=1).broadcast_to((P, NT, NE)),
                                        ALU.subtract).then_inc(f_shift, 1)

            def rank_experts(n):
                count = [ROUTE * n]
                sc = score[:, rows_of(n), :]

                def chain(ins):
                    ins.then_inc(f_route, 1)
                    count[0] = count[0] + 1
                    dve.wait_ge(f_route, count[0])

                dve.wait_ge(f_exp, n + 1)
                chain(nc.vector.tensor_reduce(fsum[:], sc, axis=AX_X, op=ALU.add))
                chain(nc.vector.reciprocal(fsum[:], fsum[:]))
                chain(nc.vector.tensor_tensor(
                    sc, sc, fsum[:].rearrange("p (t a) -> p t a", a=1).broadcast_to((P, NT, NE)), ALU.mult))
                other = sc.rearrange("p t (a e) -> p t a e", a=1).broadcast_to((P, NT, NE, NE))
                own = sc.rearrange("p t (e a) -> p t e a", a=1).broadcast_to((P, NT, NE, NE))
                chain(nc.vector.tensor_tensor(cmp_gt[:], other, own, ALU.is_gt))
                chain(nc.vector.tensor_tensor(cmp_eq[:], other, own, ALU.is_equal))
                chain(nc.vector.tensor_tensor(
                    cmp_eq[:], cmp_eq[:],
                    lower[:].rearrange("p (a e) f -> p a e f", a=1).broadcast_to((P, NT, NE, NE)), ALU.mult))
                chain(nc.vector.tensor_tensor(cmp_gt[:], cmp_gt[:], cmp_eq[:], ALU.add))
                chain(nc.vector.tensor_reduce(rank[:, rows_of(n), :], cmp_gt[:], axis=AX_X, op=ALU.add))

            def shared(c, j):
                dve.wait_ge(s_silu, NC * j + c + 1)
                dve.wait_ge(s_u_full, NC * j + c + 1)
                if not (isinstance(j, int) and j == 0):
                    dve.wait_ge(s_o_full, 2 * j)
                nc.vector.tensor_tensor(u_sh[:, c, :], g_silu[:, c % 2, :], psum[:, 5 + c % 2, :], ALU.mult
                                        ).then_inc(s_u, 1)

            def add_shared(j):
                for b in range(2):
                    dve.wait_ge(s_o_full, 2 * j + b + 1)
                    if not (isinstance(j, int) and j == 0 and b == 0):
                        dve.wait_ge(s_x1, 2 * j + b)
                    nc.vector.tensor_tensor(o_tmp[:], psum[:, 7, :].rearrange("p (t d) -> p t d", t=2), row(j, 3, 2),
                                            ALU.mult).then_inc(s_o_mul, 1)
                    dve.wait_ge(s_o_mul, 2 * j + b + 1)
                    half_x1 = x1[:, bass.ds(j * NT + 2 * b, 2), :]
                    nc.vector.tensor_tensor(half_x1, half_x1, o_tmp[:], ALU.add).then_inc(s_x1, 1)

            def route(k):
                n0, n1 = 2 * k, 2 * k + 1
                with_shared = not (isinstance(k, int) and k == 0)
                norm_apply(n0, 0)
                if with_shared:
                    shared(0, k - 1)
                    shared(1, k - 1)
                norm_statistics(n1, k, 1)
                shift_logits(n0)
                norm_apply(n1, 1)
                if with_shared:
                    shared(2, k - 1)
                    shared(3, k - 1)
                rank_experts(n0)
                if not (isinstance(k, int) and k == NBLK // 2 - 1):
                    norm_statistics(n0 + 2, k + 1, 0)
                shift_logits(n1)
                if with_shared:
                    add_shared(k - 1)
                rank_experts(n1)

            dve.wait_ge(f_gate_loaded, 32)
            dve.wait_ge(f_const, 7)
            norm_statistics(0, 0, 0)
            router_loop(route)

            steps = [0]

            def chain(ins):
                ins.then_inc(a_step, 1)
                steps[0] += 1
                dve.wait_ge(a_step, steps[0])

            nc.vector.tensor_scalar(mask[:], rank[:], 1.5, None, ALU.is_lt).then_inc(a_mask, 1)
            dve.wait_ge(a_counted, 2)
            earlier = psum[:, 2, 0:T3 * NE].rearrange("p (t e) -> p t e", e=NE)
            in_tile = psum[:, 2, T3 * NE:2 * T3 * NE].rearrange("p (t e) -> p t e", e=NE)
            for e in range(NE):
                ins = nc.vector.tensor_tensor_scan(running[:, e, :], ones[:, 0:T3], in_tile[:, :, e], 0.0,
                                                   ALU.mult, ALU.add)
                chain(ins)
            chain(nc.vector.tensor_scalar(n_tiles[:], running[:, :, T3 - 1], 1.0 / P, None, ALU.mult))
            widen = lambda v, n: v.rearrange("p (e a) -> p e a", a=1).broadcast_to((P, NE, n))
            chain(nc.vector.tensor_tensor(cmp_n, widen(n_tiles[:], T3),
                                          tile_no[:, 0:T3].rearrange("p (a s) -> p a s", a=1).broadcast_to((P, NE, T3)),
                                          ALU.is_gt))
            chain(nc.vector.tensor_reduce(n_tiles[:], cmp_n, axis=AX_X, op=ALU.add))
            chain(nc.vector.tensor_tensor(n_before[:], lower[:],
                                          n_tiles[:].rearrange("p (a f) -> p a f", a=1).broadcast_to((P, NE, NE)),
                                          ALU.mult))
            chain(nc.vector.tensor_reduce(first_tile[:], n_before[:], axis=AX_X, op=ALU.add))
            chain(nc.vector.tensor_tensor(end_tile[:], first_tile[:], n_tiles[:], ALU.add))
            chain(nc.vector.tensor_scalar(first_tile[:], first_tile[:], float(P), None, ALU.mult))
            chain(nc.vector.tensor_tensor(place[:], running[:].rearrange("p e t -> p t e"), in_tile, ALU.subtract))
            chain(nc.vector.tensor_tensor(place[:], place[:], earlier, ALU.add))
            chain(nc.vector.tensor_tensor(place[:], place[:],
                                          first_tile[:].rearrange("p (a e) -> p a e", a=1).broadcast_to((P, T3, NE)),
                                          ALU.add))
            def scale_tokens(m):
                k, i = divmod(m, NBLK)
                if m > 3:
                    dve.wait_ge(scattered[m % 4], 16 * NT * (m // 4))
                nc.vector.tensor_tensor(
                    send[m % 4].rearrange("p (t d) -> p t d", t=NT), h2[:, i * NT:(i + 1) * NT, :],
                    weight[:, k, i * NT:(i + 1) * NT].rearrange("p (t a) -> p t a", a=1).broadcast_to((P, NT, DM)),
                    ALU.mult).then_inc(scaled, 1)

            for k in range(2):
                chain(nc.vector.tensor_scalar(chosen[:], rank[:], float(k), None, ALU.is_equal))
                chain(nc.vector.tensor_tensor(picked[:], chosen[:], place[:], ALU.mult))
                chain(nc.vector.tensor_reduce(slot[:, k, :], picked[:], axis=AX_X, op=ALU.add))
                nc.vector.tensor_copy(slot_u[:, k, :], slot[:, k, :]).then_inc(a_slots, 1)
                chain(nc.vector.tensor_tensor(picked[:], chosen[:], score[:], ALU.mult))
                chain(nc.vector.tensor_reduce(weight[:, k, :], picked[:], axis=AX_X, op=ALU.add))
                if k == 0:
                    for m in range(3):
                        scale_tokens(m)
            m = 3
            for j in range(EARLY, MIDDLE):
                for c in range(NC):
                    shared(c, j)
                    for _ in range(2 if c == NC - 1 else 1):
                        if m < 2 * NBLK:
                            scale_tokens(m)
                            m += 1
                    if j == EARLY and c == 1:
                        chain(nc.vector.tensor_tensor(
                            cmp_s, tile_no[:].rearrange("p (s a) -> p s a", a=1).broadcast_to((P, TILES, NE)),
                            end_tile[:].rearrange("p (a e) -> p a e", a=1).broadcast_to((P, TILES, NE)), ALU.is_ge))
                        chain(nc.vector.tensor_reduce(expert[:], cmp_s, axis=AX_X, op=ALU.add))
                        nc.vector.tensor_scalar(expert_u[:], expert[:], float(NE - 1), None, ALU.min
                                                ).then_inc(a_experts, 1)
                add_shared(j)
                if m < 2 * NBLK:
                    scale_tokens(m)
                    m += 1

            dve.wait_ge(a_experts, 1)
            dve.wait_ge(f_w_loaded, 16 * 4)

            def bias_hidden(s, r):
                e = nc.vector.value_load(expert_u[0:1, bass.ds(s, 1)], min_val=0, max_val=NE - 1)
                dve.wait_ge(hx_full, s + 1)
                if not (isinstance(s, int) and s < 4):
                    dve.wait_ge(y_done, s - 3)
                nc.vector.tensor_tensor(hx[:, r:r + 1, :], psum[:, 2 + r % 2:3 + r % 2, :], b13[:, bass.ds(e, 1), :],
                                        ALU.add).then_inc(hx_done, 1)

            def bias_result(s, r):
                e = nc.vector.value_load(expert_u[0:1, bass.ds(s, 1)], min_val=0, max_val=NE - 1)
                dve.wait_ge(y_full, s + 1)
                if not (isinstance(s, int) and s < 4):
                    dve.wait_ge(y_stored[r], 16 * (s // 4) if isinstance(s, int) else (s - r) * 4)
                nc.vector.tensor_tensor(yt[:, r:r + 1, :], psum[:, 6 + r % 2:7 + r % 2, 0:DM], b2[:, bass.ds(e, 1), :],
                                        ALU.add).then_inc(y_biased, 1)

            def tiles(s, r):
                bias_hidden(s, r)
                if not (isinstance(s, int) and s < 2):
                    bias_result(s - 2, (r + 2) % 4)

            tile_loop(dve, tiles)
            bias_result(TILES - 2, 2)
            bias_result(TILES - 1, 3)

            def finish(i):
                r = 2 * (i % 4)
                for k in range(2):
                    dve.wait_ge(gathered[r + k], (i // 4 + 1) * 16 * NT)
                both = yg[:, r, :].rearrange("p (t d) -> p t d", t=NT)
                second = yg[:, r + 1, :].rearrange("p (t d) -> p t d", t=NT)
                nc.vector.tensor_tensor(both, both, second, ALU.add).then_inc(f_fin, 1)
                dve.wait_ge(f_fin, 3 * i + 1)
                nc.vector.tensor_tensor(both, both, row(i, 3, NT), ALU.mult).then_inc(f_fin, 1)
                dve.wait_ge(f_fin, 3 * i + 2)
                nc.vector.tensor_tensor(x1[:, rows_of(i), :], x1[:, rows_of(i), :], both, ALU.add
                                        ).then_inc(f_fin, 1)

            done = 0
            for j in range(MIDDLE, NBLK):
                for c in range(NC):
                    shared(c, j)
                finish(done)
                add_shared(j)
                finish(done + 1)
                done += 2
            for i in range(done, NBLK):
                finish(i)

        @block.tensor
        def _(pe):
            pe.wait_ge(c_ready, 4)
            for b in range(BATCH):
                for j in range(3):
                    for k in range(KD):
                        ins = nc.tensor.matmul(psum[:, 3 * b + j, :], c_wide[:, k, b, :],
                                               w_mod[:, k, j * TB:(j + 1) * TB], start=(k == 0), stop=(k == KD - 1))
                    ins.then_inc(mod_full, 1)
            pe.wait_ge(mod_copied, 6)
            pe.wait_ge(consts, 3)

            def transpose_xn(k):
                for half in range(2):
                    pe.wait_ge(p1_norm, k * 2 * NT + half * NT + NT)
                    if k > 0:
                        pe.wait_ge(xnT_copied, k * 4 + 2 * half - 2)
                    for kd in range(KD):
                        for tt in range(NT):
                            ins = nc.tensor.transpose(
                                psum[:, 2 * half + kd, tt * P:(tt + 1) * P],
                                X[:, (2 * k + half) * NT + tt, kd * P:(kd + 1) * P], ident[:])
                        ins.then_inc(xnT_full, 1)

            for k in range(NBLK // 2):
                transpose_xn(k)
            meet(pe, 1)

            def project_x(c, D, q):
                if c == 0:
                    n = q // 2 + 1 if isinstance(q, int) else (q - D) // 2 + 1
                    pe.wait_ge(xnT_loaded[D], 16 * n)
                bank = take_bank(pe, q - 1, "xp", c)
                for k in range(KD):
                    ins = nc.tensor.matmul(psum[:, PS_P + bank, :], w_in[:, D, k, c * P:(c + 1) * P],
                                           xnT[:, D, k, :], start=(k == 0), stop=(k == KD - 1))
                ins.then_inc(bank_full[bank], 1)

            def project_z(c, D, q):
                bank = take_bank(pe, q, "z", c)
                for k in range(KD):
                    ins = nc.tensor.matmul(psum[:, PS_P + bank, :], w_in[:, D, k, DI + c * P:DI + (c + 1) * P],
                                           xnT[:, D, k, :], start=(k == 0), stop=(k == KD - 1))
                ins.then_inc(bank_full[bank], 1)

            def project_out(b, D, S):
                if b == 0:
                    pe.wait_ge(yg_done, NC * S)
                bank = take_bank(pe, S, "out", b)
                for half in range(2):
                    tok = slice((2 * b + half) * P, (2 * b + half + 1) * P)
                    for c in range(NC):
                        ins = nc.tensor.matmul(psum[:, PS_P + bank, half * DM:(half + 1) * DM],
                                               xc[:, D, c, tok], w_out[:, D, c, :],
                                               start=(c == 0), stop=(c == NC - 1))
                ins.then_inc(bank_full[bank], 1)

            def project_xdbl(D, q):
                pe.wait_ge(xc_done, NC * (q + 1))
                bank = take_bank(pe, q - 1, "xdbl", 0)
                for c in range(NC):
                    ins = nc.tensor.matmul(psum[0:48, PS_P + bank, :], w_x[:, D, c, :], xc[:, D, c, :],
                                           start=(c == 0), stop=(c == NC - 1))
                ins.then_inc(bank_full[bank], 1)

            def project_dt(c, D, q):
                drained(pe, q - 1, "xdbl", 0)
                bank = take_bank(pe, q - 1, "dt", c)
                nc.tensor.matmul(psum[:, PS_P + bank, :], w_dt[32:48, D, c * P:(c + 1) * P], x_dbl[32:48, :],
                                 start=True, stop=True).then_inc(bank_full[bank], 1)

            def sum_state(u, n, D, q):
                c, g = divmod(u, NG)
                U = UNITS * q + u
                if n == 0:
                    pe.wait_ge(prod_done, U + 1)
                    if g == 0 and not (isinstance(U, int) and U == 0):
                        pe.wait_ge(yg_done, NC * q + c)
                    if g == 0:
                        nc.tensor.matmul(psum[:, PS_Y, :], diag_d[:, D, c, :], xc[:, D, c, :], start=True, stop=False)
                ins = nc.tensor.matmul(psum[:, PS_Y, :], ident[:], hst[:, u % 4, n, :], start=False, stop=(g == NG - 1 and n == GN - 1))
                if n == GN - 1:
                    ins.then_inc(unit_summed, 1)

            pe.wait_ge(w_out_done, 2)
            pe.wait_ge(diag_done, 2 * NC)
            for c in range(NC):
                project_x(c, 0, 0)
            project_xdbl(0, 0)
            for c in range(NC):
                project_dt(c, 0, 0)

            def step(i, D, q):
                for t in range(UNITS):
                    for n in range(GN):
                        if (t, n) in OUT_AT and not is_first(q):
                            project_out(OUT_AT.index((t, n)), 1 - D, q)
                        if (t, n) in Z_AT:
                            project_z(Z_AT.index((t, n)), D, q)
                        if not is_last(q):
                            if (t, n) in X_AT:
                                project_x(X_AT.index((t, n)), 1 - D, q + 1)
                            if (t, n) == (10, 0):
                                project_xdbl(1 - D, q + 1)
                            if (t, n) in STEP_SIZE_AT:
                                project_dt(STEP_SIZE_AT.index((t, n)), 1 - D, q + 1)
                        if t >= 2:
                            sum_state(t - 2, n, D, q)
                        elif not is_first(q):
                            sum_state(UNITS + t - 2, n, 1 - D, q - 1)

            run_steps(pe, step)
            for u in (UNITS - 2, UNITS - 1):
                for n in range(GN):
                    sum_state(u, n, 1, STEPS - 1)
            for b in range(2):
                project_out(b, 1, STEPS)
            meet(pe, 2)

            def turn(i, use):
                for kd in range(KD):
                    if use > 0:
                        pe.wait_ge(t_free[kd], use)
                    for tt in range(NT):
                        ins = nc.tensor.transpose(psum[:, kd, tt * P:(tt + 1) * P],
                                                  h2[:, i * NT + tt, kd * P:(kd + 1) * P], ident[:])
                    ins.then_inc(t_full[kd], 1)

            def router(n):
                use = turn_router(n)
                pe.wait_ge(f_h2, n + 1)
                turn(n, use)
                for kd in range(KD):
                    pe.wait_ge(t_free[kd], use + 1)
                if n > 0:
                    pe.wait_ge(f_shift, n)
                for tt in range(NT):
                    for kd in range(KD):
                        ins = nc.tensor.matmul(psum[:, 2, tt * NE:(tt + 1) * NE],
                                               h2T_r[:, kd, tt * P:(tt + 1) * P], gate[:, kd, :],
                                               start=(kd == 0), stop=(kd == KD - 1))
                ins.then_inc(f_logits, 1)

            def shared_hidden(c, j):
                for bank, w, free, full in ((3, sw1, s_silu, s_g_full), (5, sw2, s_u, s_u_full)):
                    if NC * j + c > 1:
                        pe.wait_ge(free, NC * j + c - 1)
                    for k in range(KD):
                        ins = nc.tensor.matmul(psum[:, bank + c % 2, :], w[:, k, c * P:(c + 1) * P], h2T_s[:, k, :],
                                               start=(k == 0), stop=(k == KD - 1))
                    ins.then_inc(full, 1)

            def shared_out(j):
                pe.wait_ge(s_u, NC * (j + 1))
                for b in range(2):
                    if 2 * j + b > 0:
                        pe.wait_ge(s_o_mul, 2 * j + b)
                    for half in range(2):
                        tok = slice((2 * b + half) * P, (2 * b + half + 1) * P)
                        for c in range(NC):
                            ins = nc.tensor.matmul(psum[:, 7, half * DM:(half + 1) * DM], u_sh[:, c, tok],
                                                   sw3[:, c, :], start=(c == 0), stop=(c == NC - 1))
                    ins.then_inc(s_o_full, 1)

            def turn_for_shared(j):
                use = turn_shared(j)
                turn(j, use)
                for kd in range(KD):
                    pe.wait_ge(t_free[kd], use + 1)

            pe.wait_ge(f_gate_loaded, 32)
            for k in range(NBLK // 2):
                if k == 1:
                    pe.wait_ge(f_sw_loaded, 16 * 3)
                for half in range(2):
                    if k > 0:
                        if half == 0:
                            turn_for_shared(k - 1)
                        shared_hidden(2 * half, k - 1)
                        shared_hidden(2 * half + 1, k - 1)
                    router(2 * k + half)
                if k > 0:
                    shared_out(k - 1)
            pe.wait_ge(a_mask, 1)
            pe.wait_ge(f_const, 7)
            nc.tensor.matmul(psum[:, 2, 0:T3 * NE], before[:], mask[:].rearrange("p t e -> p (t e)"),
                             start=True, stop=True).then_inc(a_counted, 1)
            nc.tensor.matmul(psum[:, 2, T3 * NE:2 * T3 * NE], ones[:], mask[:].rearrange("p t e -> p (t e)"),
                             start=True, stop=True).then_inc(a_counted, 1)
            for j in range(EARLY, MIDDLE):
                turn_for_shared(j)
                for c in range(NC):
                    shared_hidden(c, j)
                shared_out(j)

            pe.wait_ge(a_experts, 1)
            pe.wait_ge(f_w_loaded, 16 * 4)
            pe.wait_ge(s_o_mul, 2 * MIDDLE)
            pe.wait_ge(a_slots, 2)

            def turn_tile(s, r, m):
                pe.wait_ge(xt_loaded[r], m * 16 + 16)
                if not (isinstance(s, int) and s < 2):
                    pe.wait_ge(xtT_copied, s - 1)
                for k in range(KD):
                    ins = nc.tensor.transpose(psum[:, r % 2, k * P:(k + 1) * P], xt[:, r, k * P:(k + 1) * P], ident[:])
                ins.then_inc(xt_turned, 1)

            def hidden(s, r):
                e = nc.tensor.value_load(expert_u[0:1, bass.ds(s, 1)], min_val=0, max_val=NE - 1)
                pe.wait_ge(xtT_copied, s + 1)
                if not (isinstance(s, int) and s < 2):
                    pe.wait_ge(hx_done, s - 1)
                for k in range(KD):
                    ins = nc.tensor.matmul(psum[:, 2 + r % 2, :], xtT[:, r % 2, k * P:(k + 1) * P],
                                           w13[:, bass.ds(e * KD + k, 1), :].rearrange("p a n -> p (a n)"),
                                           start=(k == 0), stop=(k == KD - 1))
                ins.then_inc(hx_full, 1)

            def turn_hidden(s, r):
                pe.wait_ge(hs_done, s + 1)
                if not (isinstance(s, int) and s < 2):
                    pe.wait_ge(hsT_copied, s - 1)
                for k in range(KD):
                    ins = nc.tensor.transpose(psum[:, 4 + r % 2, k * P:(k + 1) * P],
                                              hs[:, r % 2, k * P:(k + 1) * P], ident[:])
                ins.then_inc(hs_turned, 1)

            def result(s, r):
                e = nc.tensor.value_load(expert_u[0:1, bass.ds(s, 1)], min_val=0, max_val=NE - 1)
                pe.wait_ge(hsT_copied, s + 1)
                if not (isinstance(s, int) and s < 2):
                    pe.wait_ge(y_biased, s - 1)
                for k in range(KD):
                    ins = nc.tensor.matmul(psum[:, 6 + r % 2, 0:DM], hsT[:, r % 2, k * P:(k + 1) * P],
                                           w2[:, bass.ds(e * KD + k, 1), :].rearrange("p a n -> p (a n)"),
                                           start=(k == 0), stop=(k == KD - 1))
                ins.then_inc(y_full, 1)

            def tiles(s, r):
                hidden(s, r)
                if not (isinstance(s, int) and s == 0):
                    turn_hidden(s - 1, (r + 3) % 4)
                if not (isinstance(s, int) and s == TILES - 1):
                    m = (s + 1) // 4 if isinstance(s, int) else (s - r) // 4 + (1 if r == 3 else 0)
                    turn_tile(s + 1, (r + 1) % 4, m)
                if not (isinstance(s, int) and s < 2):
                    result(s - 2, (r + 2) % 4)

            turn_tile(0, 0, 0)
            tile_loop(pe, tiles)
            turn_hidden(TILES - 1, 3)
            result(TILES - 2, 2)
            result(TILES - 1, 3)
            for done in (xtT_copied, hx_done, hsT_copied, y_biased):
                pe.wait_ge(done, TILES)
            for j in range(MIDDLE, NBLK):
                turn_for_shared(j)
                for c in range(NC):
                    shared_hidden(c, j)
                shared_out(j)


def on_partitions(w):
    return w.reshape(w.shape[0] // P, P, *w.shape[1:]).swapaxes(0, 1)


def lay_out(inputs):
    import numpy as np
    a = {k.replace("L0_", ""): np.asarray(v) for k, v in inputs.items()}
    both = lambda name: (a["attn_f_" + name], a["attn_b_" + name])
    stack = lambda parts: np.stack(parts, axis=1)
    out = {
        "x": a["attn_x"].reshape(NBLK, NT, P, DM).transpose(0, 2, 1, 3).reshape(NBLK, P, NT * DM),
        "cT": on_partitions(a["c"].T),
        "w_mod": on_partitions(a["wmod"]),
        "ln_w": on_partitions(a["attn_ln_w"]),
        "ln_b": on_partitions(a["attn_ln_b"]),
        "w_in": stack([on_partitions(w.T) for w in both("W_in")]),
        "w_x": stack([on_partitions(np.concatenate([w[DR:], w[:DR]]).T) for w in both("W_x")]),
        "w_dt": stack([w.T for w in both("W_dt")]),
        "w_out": stack([on_partitions(w.T) for w in both("W_out")]),
        "a_log": stack([on_partitions(w) for w in both("A_log")]),
        "w_conv": stack([on_partitions(w) for w in both("W_conv")]),
        "b_conv": stack([on_partitions(w) for w in both("b_conv")]),
        "b_dt": stack([on_partitions(w) for w in both("b_dt")]),
        "d_skip": stack([on_partitions(w) for w in both("D")]),
        "gate": on_partitions(a["ffn_gate_w"].T),
        "sw1": on_partitions(a["ffn_sw1"].T),
        "sw2": on_partitions(a["ffn_sw2"].T),
        "sw3": on_partitions(a["ffn_sw3"].T),
    }
    w = {n: stack([on_partitions(w.T) for w in a["ffn_w" + n]]) for n in "123"}
    out["w13"] = np.concatenate([w["1"], w["3"]], axis=-1).reshape(P, -1)
    out["w2"] = w["2"].reshape(P, -1)
    out["b13"] = np.concatenate([a["ffn_b1"], a["ffn_b3"]], axis=1).reshape(1, -1)
    out["b2"] = a["ffn_b2"].reshape(1, -1)
    return {k: np.ascontiguousarray(v) for k, v in out.items()}


def kernel(**inputs):
    import numpy as np
    import concourse.bacc as bacc
    from concourse.bass_utils import run_bass_kernel_spmd

    nc = bacc.Bacc("TRN2", target_bir_lowering=False, num_devices=1)
    arrays = lay_out(inputs)
    aps = {name: nc.dram_tensor(f"in_{name}", v.shape, mybir.dt.from_np(v.dtype), kind="ExternalInput").ap()
           for name, v in arrays.items()}
    out = nc.dram_tensor("out_x", (NBLK, P, NT * DM), F32, kind="ExternalOutput").ap()
    mixer_and_experts(nc, aps, out)
    r = run_bass_kernel_spmd(nc, [{f"in_{k}": v for k, v in arrays.items()}], core_ids=[0])
    y = np.asarray(r.results[0]["out_x"])
    return y.reshape(NBLK, P, NT, DM).transpose(0, 2, 1, 3).reshape(BATCH, SEQ, DM)
```
